# Optimizing a Trainium2 kernel written in Bass

```python
import numpy as np
import jax
import jax.numpy as jnp

def _softmax(x, axis=-1):
    return jax.nn.softmax(x, axis=axis)

def _gelu(x):
    return jax.nn.gelu(x, approximate=True)

def _silu(x):
    return jax.nn.silu(x)

def _sigmoid(x):
    return jax.nn.sigmoid(x)

def _layernorm(x, axis=-1, eps=1e-05):
    m = jnp.mean(x, axis=axis, keepdims=True)
    v = jnp.var(x, axis=axis, keepdims=True)
    return (x - m) / jnp.sqrt(v + eps)

def _scatter_add(tgt, idx, src, axis=0):
    return tgt.at[idx].add(src)

def _segment_sum(src, seg, n):
    return jax.ops.segment_sum(src, seg, n)
kernel_name = 'mk_decoder_postln_d4_seqx_r4_ddbfa6'

def setup_inputs(seed: int=0):
    np.random.seed(seed)
    _w = jnp.asarray

    def _rec_inputs():
        import jax
        import jax.numpy as jnp
        _rk = jax.random.key(seed)
        x = 7.22e-05 + 1 * jax.random.normal(jax.random.fold_in(_rk, 1), (8, 100, 512), jnp.float32)
        _lenS = 100 - jax.random.randint(jax.random.fold_in(_rk, 7), (8,), 0, max(1, 100 // 4) + 1, jnp.int32)
        _lenS2 = 361 - jax.random.randint(jax.random.fold_in(_rk, 8), (8,), 0, max(1, 361 // 4) + 1, jnp.int32)
        _ctx_512P = jax.random.normal(jax.random.fold_in(_rk, 11), (8, 16, 128), jnp.float32)
        _ctx_512c = jax.random.dirichlet(jax.random.fold_in(_rk, 511), 0.3 * jnp.ones((16,), jnp.float32), (8, 361))
        _ctx_512t = jnp.einsum('bsk,bkd->bsd', _ctx_512c, _ctx_512P)
        _ctx_512t = _ctx_512t * jax.lax.rsqrt(jnp.mean(jnp.square(_ctx_512t)) + 1e-12) * 0.953939
        ctx_512 = -0.000514642 + 1.00011 * (_ctx_512t + 0.3 * jax.random.normal(jax.random.fold_in(_rk, 611), (8, 361, 128), jnp.float32))
        return (x, ctx_512)
    x, ctx_512 = _rec_inputs()

    def _L0_attn_setup():
        import jax, jax.numpy as jnp
        import numpy as np
        EPS = 1.1920929e-07

        def _rms(x):
            return x * jax.lax.rsqrt(jnp.mean(x * x, axis=-1, keepdims=True) + EPS)
        key = jax.random.key(seed)
        k0, k1, k2, k3 = jax.random.split(key, 4)
        B, S, D, DFF = (4, 512, 512, 2048)
        x = jax.random.normal(k0, (B, S, D), dtype=jnp.float32)
        w_qkv = jax.random.normal(k1, (3 * D, D), dtype=jnp.float32) * 0.02
        w_swiglu = jax.random.normal(k2, (2 * DFF, D), dtype=jnp.float32) * 0.02
        w_out = jax.random.normal(k3, (D, DFF), dtype=jnp.float32) * 0.02
        return {'x': x, 'w_qkv': w_qkv, 'w_swiglu': w_swiglu, 'w_out': w_out}
    _L0_attn_all = _L0_attn_setup()
    _L0_attn_in = {k: v for k, v in _L0_attn_all.items() if k in ('w_qkv', 'w_swiglu', 'w_out')}
    del _L0_attn_all

    def _L0_xattn_setup():
        import jax, jax.numpy as jnp
        import numpy as np
        B, S, H, NH, L = (2, 512, 512, 16, 128)
        HD = H // NH
        key = jax.random.key(seed)
        k1, k2, k3, k4, k5 = jax.random.split(key, 5)
        scale = 0.02
        return {'q': jax.random.normal(k1, (B, S, H), dtype=jnp.float32), 'latent_kv': jax.random.normal(k2, (B, S, L), dtype=jnp.float32), 'Wq': jax.random.normal(k3, (H, H), dtype=jnp.float32) * scale, 'Wkv_expand': jax.random.normal(k4, (2 * H, L), dtype=jnp.float32) * scale, 'Wout': jax.random.normal(k5, (H, H), dtype=jnp.float32) * scale}
    _L0_xattn_all = _L0_xattn_setup()
    _L0_xattn_in = {k: v for k, v in _L0_xattn_all.items() if k in ('Wq', 'Wkv_expand', 'Wout')}
    del _L0_xattn_all

    def _L0_ffn_setup():
        import jax, jax.numpy as jnp
        import numpy as np
        HIDDEN = 512
        INTER = 2048
        SCALE = 64.0

        def fwht(x):
            orig_shape = x.shape
            n = orig_shape[-1]
            x = x.reshape(-1, n)
            h = 1
            while h < n:
                x = x.reshape(-1, n // (2 * h), 2, h)
                a, b = (x[:, :, 0, :], x[:, :, 1, :])
                x = jnp.stack([a + b, a - b], axis=2).reshape(-1, n)
                h *= 2
            return (x / jnp.sqrt(jnp.asarray(n, x.dtype))).reshape(orig_shape)
        key = jax.random.key(seed)
        ks = jax.random.split(key, 8)
        inp = jax.random.normal(ks[0], (4, 512, HIDDEN), dtype=jnp.float32)
        SU_ug = jnp.where(jax.random.bernoulli(ks[1], 0.5, (HIDDEN,)), 1.0, -1.0).astype(jnp.float32)
        SU_dp = jnp.where(jax.random.bernoulli(ks[2], 0.5, (INTER,)), 1.0, -1.0).astype(jnp.float32)
        Wscale_ug = jax.random.uniform(ks[3], (2 * INTER,), jnp.float32, 0.5, 1.5)
        Wscale_dp = jax.random.uniform(ks[4], (HIDDEN,), jnp.float32, 0.5, 1.5)
        W_up = jax.random.normal(ks[5], (INTER, HIDDEN), dtype=jnp.float32) * 0.02
        W_gate = jax.random.normal(ks[6], (INTER, HIDDEN), dtype=jnp.float32) * 0.02
        W_down = jax.random.normal(ks[7], (HIDDEN, INTER), dtype=jnp.float32) * 0.02
        return {'input': inp, 'SU_ug': SU_ug, 'SU_dp': SU_dp, 'Wscale_ug': Wscale_ug, 'Wscale_dp': Wscale_dp, 'W_up': W_up, 'W_gate': W_gate, 'W_down': W_down}
    _L0_ffn_all = _L0_ffn_setup()
    _L0_ffn_in = {k: v for k, v in _L0_ffn_all.items() if k in ('SU_ug', 'SU_dp', 'Wscale_ug', 'Wscale_dp', 'W_up', 'W_gate', 'W_down')}
    del _L0_ffn_all

    def _L1_attn_setup():
        import jax, jax.numpy as jnp
        import numpy as np
        B, L, E = (2, 512, 512)
        NUM_HEADS = 16
        NUM_KV_HEADS = 2
        HEAD_DIM = E // NUM_HEADS
        THETA = 10000.0

        def apply_rope(x, theta=THETA):
            D = x.shape[-1]
            half = D // 2
            inv_freq = theta ** (-jnp.arange(half, dtype=jnp.float32) / half)
            pos = jnp.arange(x.shape[1], dtype=jnp.float32)
            ang = pos[:, None] * inv_freq[None, :]
            cos = jnp.cos(ang)[None, :, None, :].astype(x.dtype)
            sin = jnp.sin(ang)[None, :, None, :].astype(x.dtype)
            x1, x2 = (x[..., :half], x[..., half:])
            return jnp.concatenate([x1 * cos - x2 * sin, x2 * cos + x1 * sin], axis=-1)
        key = jax.random.key(seed)
        ks = jax.random.split(key, 8)
        s = 0.02
        return {'x': jax.random.normal(ks[0], (B, L, E), dtype=jnp.float32), 'wq': jax.random.normal(ks[1], (NUM_HEADS * HEAD_DIM, E), dtype=jnp.float32) * s, 'wk': jax.random.normal(ks[2], (NUM_KV_HEADS * HEAD_DIM, E), dtype=jnp.float32) * s, 'wv': jax.random.normal(ks[3], (NUM_KV_HEADS * HEAD_DIM, E), dtype=jnp.float32) * s, 'wo': jax.random.normal(ks[4], (E, NUM_HEADS * HEAD_DIM), dtype=jnp.float32) * s, 'bq': jax.random.normal(ks[5], (NUM_HEADS * HEAD_DIM,), dtype=jnp.float32) * s, 'bk': jax.random.normal(ks[6], (NUM_KV_HEADS * HEAD_DIM,), dtype=jnp.float32) * s, 'bv': jax.random.normal(ks[7], (NUM_KV_HEADS * HEAD_DIM,), dtype=jnp.float32) * s}
    _L1_attn_all = _L1_attn_setup()
    _L1_attn_in = {k: v for k, v in _L1_attn_all.items() if k in ('wq', 'wk', 'wv', 'wo', 'bq', 'bk', 'bv')}
    del _L1_attn_all

    def _L1_xattn_setup():
        import jax, jax.numpy as jnp
        import numpy as np
        B, S, L = (2, 256, 256)
        DIM_Q, H, K, D_C, D_CQ, R = (512, 16, 128, 128, 384, 64)

        def _rope_tables(seq_len, dim, dtype):
            inv_freq = 1.0 / 10000.0 ** (jnp.arange(0, dim, 2, dtype=dtype) / dim)
            t = jnp.arange(seq_len, dtype=dtype)
            freqs = t[:, None] * inv_freq[None, :]
            sin = jnp.repeat(jnp.sin(freqs), 2, axis=-1)
            cos = jnp.repeat(jnp.cos(freqs), 2, axis=-1)
            return (sin, cos)

        def _rotate_half(x):
            h = x.shape[-1] // 2
            return jnp.concatenate([-x[..., h:], x[..., :h]], axis=-1)
        key = jax.random.key(seed)
        ks = jax.random.split(key, 8)
        s_in = 1.0 / np.sqrt(DIM_Q)
        s_k = 1.0 / np.sqrt(K)
        s_cq = 1.0 / np.sqrt(D_CQ)
        s_c = 1.0 / np.sqrt(D_C)
        return {'hidden_q': jax.random.normal(ks[0], (B, S, DIM_Q), jnp.float32), 'kv_c': jax.random.normal(ks[1], (B, L, D_C), jnp.float32), 'Wq': jax.random.normal(ks[2], (H * K, DIM_Q), jnp.float32) * s_in, 'w_kc_q': jax.random.normal(ks[3], (H, K, D_CQ), jnp.float32) * s_k, 'w_kc_kv': jax.random.normal(ks[4], (H, K, D_C), jnp.float32) * s_k, 'W_qr': jax.random.normal(ks[5], (H, D_CQ, R), jnp.float32) * s_cq / np.sqrt(R), 'W_kr': jax.random.normal(ks[6], (H, D_C, R), jnp.float32) * s_c, 'Wo': jax.random.normal(ks[7], (DIM_Q, H * K), jnp.float32) * s_k}
    _L1_xattn_all = _L1_xattn_setup()
    _L1_xattn_in = {k: v for k, v in _L1_xattn_all.items() if k in ('Wq', 'w_kc_q', 'w_kc_kv', 'W_qr', 'W_kr', 'Wo')}
    del _L1_xattn_all

    def _L1_ffn_setup():
        import jax, jax.numpy as jnp
        import numpy as np
        B, S, H = (1, 256, 512)
        F = 256
        E = 16
        K = 2
        NS = 1
        ROUTE_SCALE = 1.0
        key = jax.random.key(seed)
        ks = jax.random.split(key, 8)

        def w(k, shape, fan_in):
            return jax.random.normal(k, shape, jnp.float32) * fan_in ** (-0.5)
        return {'hidden_states': jax.random.normal(ks[0], (B, S, H), jnp.float32), 'gate_w': w(ks[1], (H, E), H), 'expert_bias': jnp.zeros((E,), jnp.float32), 'shared_gate_w': w(ks[2], (H, F * NS), H), 'shared_up_w': w(ks[3], (H, F * NS), H), 'shared_down_w': w(ks[4], (F * NS, H), F * NS), 'experts_gate_up': w(ks[5], (E, H, 2 * F), H), 'experts_down': w(ks[6], (E, F, H), F)}
    _L1_ffn_all = _L1_ffn_setup()
    _L1_ffn_in = {k: v for k, v in _L1_ffn_all.items() if k in ('gate_w', 'expert_bias', 'shared_gate_w', 'shared_up_w', 'shared_down_w', 'experts_gate_up', 'experts_down')}
    del _L1_ffn_all

    def _L2_attn_setup():
        import jax, jax.numpy as jnp
        import numpy as np
        D_MODEL = 512
        N_HEAD = 16
        D_HEAD = D_MODEL // N_HEAD
        key = jax.random.key(seed)
        k_x, k_qkv, k_proj = jax.random.split(key, 3)
        x = jax.random.normal(k_x, (2, 512, D_MODEL), dtype=jnp.float32)
        scale = 1.0 / np.sqrt(D_MODEL)
        W_qkv = jax.random.uniform(k_qkv, (3 * D_MODEL, D_MODEL), jnp.float32, -scale, scale)
        W_proj = jax.random.uniform(k_proj, (D_MODEL, D_MODEL), jnp.float32, -scale, scale)
        return {'x': x, 'W_qkv': W_qkv, 'W_proj': W_proj}
    _L2_attn_all = _L2_attn_setup()
    _L2_attn_in = {k: v for k, v in _L2_attn_all.items() if k in ('W_qkv', 'W_proj')}
    del _L2_attn_all

    def _L2_xattn_setup():
        import jax, jax.numpy as jnp
        import numpy as np
        B, S, L = (2, 256, 256)
        DIM_Q, H, K, D_C, D_CQ, R = (512, 16, 128, 128, 384, 64)

        def _rope_tables(length, dim):
            inv = 1.0 / 10000.0 ** (jnp.arange(0, dim, 2, dtype=jnp.float32) / dim)
            f = jnp.arange(length, dtype=jnp.float32)[:, None] * inv[None, :]
            sin = jnp.repeat(jnp.sin(f), 2, axis=-1)
            cos = jnp.repeat(jnp.cos(f), 2, axis=-1)
            return (sin, cos)

        def _rotate_half(x):
            half = x.shape[-1] // 2
            return jnp.concatenate([-x[..., half:], x[..., :half]], axis=-1)

        def _apply_rope(x, sin, cos):
            return x * cos + _rotate_half(x) * sin
        key = jax.random.key(seed)
        ks = jax.random.split(key, 8)
        return {'hidden_q': jax.random.normal(ks[0], (B, S, DIM_Q), jnp.float32), 'kv_c': jax.random.normal(ks[1], (B, L, D_C), jnp.float32), 'Wq': jax.random.normal(ks[2], (H * K, DIM_Q), jnp.float32) / np.sqrt(DIM_Q).astype(np.float32), 'w_kc_q': jax.random.normal(ks[3], (H, K, D_CQ), jnp.float32) / np.sqrt(K).astype(np.float32), 'w_kc_kv': jax.random.normal(ks[4], (H, K, D_C), jnp.float32) / np.sqrt(K).astype(np.float32), 'W_qr': jax.random.normal(ks[5], (H, D_CQ, R), jnp.float32) / np.float32(np.sqrt(D_CQ) * np.sqrt(R)), 'W_kr': jax.random.normal(ks[6], (H, D_C, R), jnp.float32) / np.sqrt(D_C).astype(np.float32), 'Wo': jax.random.normal(ks[7], (DIM_Q, H * K), jnp.float32) / np.sqrt(H * K).astype(np.float32)}
    _L2_xattn_all = _L2_xattn_setup()
    _L2_xattn_in = {k: v for k, v in _L2_xattn_all.items() if k in ('Wq', 'w_kc_q', 'w_kc_kv', 'W_qr', 'W_kr', 'Wo')}
    del _L2_xattn_all

    def _L2_ffn_setup():
        import jax, jax.numpy as jnp
        import numpy as np
        RANK = 64
        SCALING = 1.0 / RANK
        TEMPERATURE = 1.0
        key = jax.random.key(seed)
        k_x, k_a, k_b, k_w = jax.random.split(key, 4)
        B_, S, D = (4, 512, 512)
        E, R, O = (8, RANK, 512)
        x = jax.random.normal(k_x, (B_, S, D), dtype=jnp.float32)
        A = jax.random.normal(k_a, (E, R, D), dtype=jnp.float32) * (1.0 / np.sqrt(D))
        Bw = jax.random.normal(k_b, (E, O, R), dtype=jnp.float32) * 0.02
        Wr = jax.random.normal(k_w, (E, D), dtype=jnp.float32) * (1.0 / np.sqrt(D))
        br = jnp.zeros((E,), dtype=jnp.float32)
        return {'x': x, 'A': A, 'B': Bw, 'Wr': Wr, 'br': br}
    _L2_ffn_all = _L2_ffn_setup()
    _L2_ffn_in = {k: v for k, v in _L2_ffn_all.items() if k in ('A', 'B', 'Wr', 'br')}
    del _L2_ffn_all

    def _L3_attn_setup():
        import jax, jax.numpy as jnp
        import numpy as np
        H = 16
        SB_RATIO = 0.1
        RB_RATIO = 0.5
        ROPE_BASE = 10000.0

        def _rotate_half(x):
            hd = x.shape[-1]
            x1, x2 = (x[..., :hd // 2], x[..., hd // 2:])
            return jnp.concatenate([-x2, x1], axis=-1)
        key = jax.random.key(seed)
        ks = jax.random.split(key, 6)
        B, T, D = (1, 512, 512)
        s = 0.02
        return {'hidden_states': jax.random.normal(ks[0], (B, T, D), jnp.float32), 'wq': jax.random.normal(ks[1], (D, D), jnp.float32) * s, 'wk': jax.random.normal(ks[2], (D, D), jnp.float32) * s, 'wv': jax.random.normal(ks[3], (D, D), jnp.float32) * s, 'wo': jax.random.normal(ks[4], (D, D), jnp.float32) * s, 'bern_u': jax.random.uniform(ks[5], (B, H), jnp.float32)}
    _L3_attn_all = _L3_attn_setup()
    _L3_attn_in = {k: v for k, v in _L3_attn_all.items() if k in ('wq', 'wk', 'wv', 'wo', 'bern_u')}
    del _L3_attn_all

    def _L3_xattn_setup():
        import jax, jax.numpy as jnp
        import numpy as np
        B, S, H, NH, L = (2, 512, 512, 16, 128)
        HD = H // NH
        key = jax.random.key(seed)
        k1, k2, k3, k4, k5 = jax.random.split(key, 5)
        scale = 0.02
        return {'q': jax.random.normal(k1, (B, S, H), dtype=jnp.float32), 'latent_kv': jax.random.normal(k2, (B, S, L), dtype=jnp.float32), 'Wq': jax.random.normal(k3, (H, H), dtype=jnp.float32) * scale, 'Wkv_expand': jax.random.normal(k4, (2 * H, L), dtype=jnp.float32) * scale, 'Wout': jax.random.normal(k5, (H, H), dtype=jnp.float32) * scale}
    _L3_xattn_all = _L3_xattn_setup()
    _L3_xattn_in = {k: v for k, v in _L3_xattn_all.items() if k in ('Wq', 'Wkv_expand', 'Wout')}
    del _L3_xattn_all

    def _L3_ffn_setup():
        import jax, jax.numpy as jnp
        import numpy as np
        H = 512
        E = 64
        I = 128
        SI = 128
        TOP_K = 8
        B, T = (2, 128)
        key = jax.random.key(seed)
        ks = jax.random.split(key, 8)
        s = 0.02
        return {'h': jax.random.normal(ks[0], (B, T, H), jnp.float32), 'gate_w': jax.random.normal(ks[1], (E, H), jnp.float32) * s, 'gu_w': jax.random.normal(ks[2], (E, 2 * I, H), jnp.float32) * s, 'dp_w': jax.random.normal(ks[3], (E, H, I), jnp.float32) * s, 'sh_gate_w': jax.random.normal(ks[4], (SI, H), jnp.float32) * s, 'sh_up_w': jax.random.normal(ks[5], (SI, H), jnp.float32) * s, 'sh_down_w': jax.random.normal(ks[6], (H, SI), jnp.float32) * s, 'sh_gate1_w': jax.random.normal(ks[7], (1, H), jnp.float32) * s}
    _L3_ffn_all = _L3_ffn_setup()
    _L3_ffn_in = {k: v for k, v in _L3_ffn_all.items() if k in ('gate_w', 'gu_w', 'dp_w', 'sh_gate_w', 'sh_up_w', 'sh_down_w', 'sh_gate1_w')}
    del _L3_ffn_all
    return {'x': x, 'ctx_512': ctx_512, 'L0_attn_w_qkv': _L0_attn_in['w_qkv'], 'L0_attn_w_swiglu': _L0_attn_in['w_swiglu'], 'L0_attn_w_out': _L0_attn_in['w_out'], 'L0_xattn_Wq': _L0_xattn_in['Wq'], 'L0_xattn_Wkv_expand': _L0_xattn_in['Wkv_expand'], 'L0_xattn_Wout': _L0_xattn_in['Wout'], 'L0_ffn_SU_ug': _L0_ffn_in['SU_ug'], 'L0_ffn_SU_dp': _L0_ffn_in['SU_dp'], 'L0_ffn_Wscale_ug': _L0_ffn_in['Wscale_ug'], 'L0_ffn_Wscale_dp': _L0_ffn_in['Wscale_dp'], 'L0_ffn_W_up': _L0_ffn_in['W_up'], 'L0_ffn_W_gate': _L0_ffn_in['W_gate'], 'L0_ffn_W_down': _L0_ffn_in['W_down'], 'L1_attn_wq': _L1_attn_in['wq'], 'L1_attn_wk': _L1_attn_in['wk'], 'L1_attn_wv': _L1_attn_in['wv'], 'L1_attn_wo': _L1_attn_in['wo'], 'L1_attn_bq': _L1_attn_in['bq'], 'L1_attn_bk': _L1_attn_in['bk'], 'L1_attn_bv': _L1_attn_in['bv'], 'L1_xattn_Wq': _L1_xattn_in['Wq'], 'L1_xattn_w_kc_q': _L1_xattn_in['w_kc_q'], 'L1_xattn_w_kc_kv': _L1_xattn_in['w_kc_kv'], 'L1_xattn_W_qr': _L1_xattn_in['W_qr'], 'L1_xattn_W_kr': _L1_xattn_in['W_kr'], 'L1_xattn_Wo': _L1_xattn_in['Wo'], 'L1_ffn_gate_w': _L1_ffn_in['gate_w'], 'L1_ffn_expert_bias': _L1_ffn_in['expert_bias'], 'L1_ffn_shared_gate_w': _L1_ffn_in['shared_gate_w'], 'L1_ffn_shared_up_w': _L1_ffn_in['shared_up_w'], 'L1_ffn_shared_down_w': _L1_ffn_in['shared_down_w'], 'L1_ffn_experts_gate_up': _L1_ffn_in['experts_gate_up'], 'L1_ffn_experts_down': _L1_ffn_in['experts_down'], 'L2_attn_W_qkv': _L2_attn_in['W_qkv'], 'L2_attn_W_proj': _L2_attn_in['W_proj'], 'L2_xattn_Wq': _L2_xattn_in['Wq'], 'L2_xattn_w_kc_q': _L2_xattn_in['w_kc_q'], 'L2_xattn_w_kc_kv': _L2_xattn_in['w_kc_kv'], 'L2_xattn_W_qr': _L2_xattn_in['W_qr'], 'L2_xattn_W_kr': _L2_xattn_in['W_kr'], 'L2_xattn_Wo': _L2_xattn_in['Wo'], 'L2_ffn_A': _L2_ffn_in['A'], 'L2_ffn_B': _L2_ffn_in['B'], 'L2_ffn_Wr': _L2_ffn_in['Wr'], 'L2_ffn_br': _L2_ffn_in['br'], 'L3_attn_wq': _L3_attn_in['wq'], 'L3_attn_wk': _L3_attn_in['wk'], 'L3_attn_wv': _L3_attn_in['wv'], 'L3_attn_wo': _L3_attn_in['wo'], 'L3_attn_bern_u': _L3_attn_in['bern_u'], 'L3_xattn_Wq': _L3_xattn_in['Wq'], 'L3_xattn_Wkv_expand': _L3_xattn_in['Wkv_expand'], 'L3_xattn_Wout': _L3_xattn_in['Wout'], 'L3_ffn_gate_w': _L3_ffn_in['gate_w'], 'L3_ffn_gu_w': _L3_ffn_in['gu_w'], 'L3_ffn_dp_w': _L3_ffn_in['dp_w'], 'L3_ffn_sh_gate_w': _L3_ffn_in['sh_gate_w'], 'L3_ffn_sh_up_w': _L3_ffn_in['sh_up_w'], 'L3_ffn_sh_down_w': _L3_ffn_in['sh_down_w'], 'L3_ffn_sh_gate1_w': _L3_ffn_in['sh_gate1_w']}

def reference(x, ctx_512, L0_attn_w_qkv, L0_attn_w_swiglu, L0_attn_w_out, L0_xattn_Wq, L0_xattn_Wkv_expand, L0_xattn_Wout, L0_ffn_SU_ug, L0_ffn_SU_dp, L0_ffn_Wscale_ug, L0_ffn_Wscale_dp, L0_ffn_W_up, L0_ffn_W_gate, L0_ffn_W_down, L1_attn_wq, L1_attn_wk, L1_attn_wv, L1_attn_wo, L1_attn_bq, L1_attn_bk, L1_attn_bv, L1_xattn_Wq, L1_xattn_w_kc_q, L1_xattn_w_kc_kv, L1_xattn_W_qr, L1_xattn_W_kr, L1_xattn_Wo, L1_ffn_gate_w, L1_ffn_expert_bias, L1_ffn_shared_gate_w, L1_ffn_shared_up_w, L1_ffn_shared_down_w, L1_ffn_experts_gate_up, L1_ffn_experts_down, L2_attn_W_qkv, L2_attn_W_proj, L2_xattn_Wq, L2_xattn_w_kc_q, L2_xattn_w_kc_kv, L2_xattn_W_qr, L2_xattn_W_kr, L2_xattn_Wo, L2_ffn_A, L2_ffn_B, L2_ffn_Wr, L2_ffn_br, L3_attn_wq, L3_attn_wk, L3_attn_wv, L3_attn_wo, L3_attn_bern_u, L3_xattn_Wq, L3_xattn_Wkv_expand, L3_xattn_Wout, L3_ffn_gate_w, L3_ffn_gu_w, L3_ffn_dp_w, L3_ffn_sh_gate_w, L3_ffn_sh_up_w, L3_ffn_sh_down_w, L3_ffn_sh_gate1_w):
    import jax
    import jax.numpy as jnp

    def _L0_attn_ref(x, w_qkv, w_swiglu, w_out):
        import jax, jax.numpy as jnp
        import numpy as np
        EPS = 1.1920929e-07

        def _rms(x):
            return x * jax.lax.rsqrt(jnp.mean(x * x, axis=-1, keepdims=True) + EPS)
        qkv = _rms(x) @ w_qkv.T
        q, k, v = jnp.split(qkv, 3, axis=-1)
        q = _rms(q)
        k = _rms(k)
        w = jnp.exp(k)
        kv_cum = jnp.cumsum(w * v, axis=1)
        w_cum = jnp.cumsum(w, axis=1)
        y = jax.nn.sigmoid(q) * (kv_cum / (w_cum + 1e-06))
        uv = y @ w_swiglu.T
        u, g = jnp.split(uv, 2, axis=-1)
        return x + u * jax.nn.silu(g) @ w_out.T

    def _L0_xattn_ref(q, latent_kv, Wq, Wkv_expand, Wout):
        import jax, jax.numpy as jnp
        import numpy as np
        B, S, H, NH, L = (2, 512, 512, 16, 128)
        HD = H // NH
        b, sq, _ = q.shape
        sk = latent_kv.shape[1]
        qp = q @ Wq.T
        kv = latent_kv @ Wkv_expand.T
        k, v = jnp.split(kv, 2, axis=-1)
        qh = qp.reshape(b, sq, NH, HD).transpose(0, 2, 1, 3)
        kh = k.reshape(b, sk, NH, HD).transpose(0, 2, 1, 3)
        vh = v.reshape(b, sk, NH, HD).transpose(0, 2, 1, 3)
        inv_sqrt_d = 1.0 / jnp.sqrt(jnp.float32(HD))
        scores = jnp.einsum('bhqd,bhkd->bhqk', qh, kh) * inv_sqrt_d
        causal = jnp.tril(jnp.ones((sq, sk), dtype=bool))
        scores = jnp.where(causal, scores, jnp.finfo(scores.dtype).min)
        attn = jax.nn.softmax(scores, axis=-1)
        out = jnp.einsum('bhqk,bhkd->bhqd', attn, vh)
        out = out.transpose(0, 2, 1, 3).reshape(b, sq, H)
        return out @ Wout.T

    def _L0_ffn_ref(input, SU_ug, SU_dp, Wscale_ug, Wscale_dp, W_up, W_gate, W_down):
        import jax, jax.numpy as jnp
        import numpy as np
        HIDDEN = 512
        INTER = 2048
        SCALE = 64.0

        def fwht(x):
            orig_shape = x.shape
            n = orig_shape[-1]
            x = x.reshape(-1, n)
            h = 1
            while h < n:
                x = x.reshape(-1, n // (2 * h), 2, h)
                a, b = (x[:, :, 0, :], x[:, :, 1, :])
                x = jnp.stack([a + b, a - b], axis=2).reshape(-1, n)
                h *= 2
            return (x / jnp.sqrt(jnp.asarray(n, x.dtype))).reshape(orig_shape)
        n = SU_ug.shape[0]
        x = input.reshape(-1, n)
        x = fwht(x * SU_ug) / SCALE
        x_up = x @ W_up.T * (Wscale_ug[:INTER] * SCALE)
        x_gate = x @ W_gate.T * (Wscale_ug[INTER:] * SCALE)
        x = jax.nn.silu(x_gate) * x_up
        x = fwht(x * SU_dp) / SCALE
        x = x @ W_down.T * (Wscale_dp * SCALE)
        return x.reshape(input.shape)

    def _L1_attn_ref(x, wq, wk, wv, wo, bq, bk, bv):
        import jax, jax.numpy as jnp
        import numpy as np
        B, L, E = (2, 512, 512)
        NUM_HEADS = 16
        NUM_KV_HEADS = 2
        HEAD_DIM = E // NUM_HEADS
        THETA = 10000.0

        def apply_rope(x, theta=THETA):
            D = x.shape[-1]
            half = D // 2
            inv_freq = theta ** (-jnp.arange(half, dtype=jnp.float32) / half)
            pos = jnp.arange(x.shape[1], dtype=jnp.float32)
            ang = pos[:, None] * inv_freq[None, :]
            cos = jnp.cos(ang)[None, :, None, :].astype(x.dtype)
            sin = jnp.sin(ang)[None, :, None, :].astype(x.dtype)
            x1, x2 = (x[..., :half], x[..., half:])
            return jnp.concatenate([x1 * cos - x2 * sin, x2 * cos + x1 * sin], axis=-1)
        b, l, _ = x.shape
        Hq, Hkv, Dh = (NUM_HEADS, NUM_KV_HEADS, HEAD_DIM)
        G = Hq // Hkv
        scale = 1.0 / Dh ** 0.5
        q = (x @ wq.T + bq).reshape(b, l, Hq, Dh)
        k = (x @ wk.T + bk).reshape(b, l, Hkv, Dh)
        v = (x @ wv.T + bv).reshape(b, l, Hkv, Dh)
        q = apply_rope(q)
        k = apply_rope(k)
        q = q.transpose(0, 2, 1, 3).reshape(b, Hkv, G, l, Dh).astype(jnp.float32)
        k = k.transpose(0, 2, 1, 3).astype(jnp.float32)
        v = v.transpose(0, 2, 1, 3).astype(jnp.float32)
        scores = jnp.einsum('bhgqd,bhkd->bhgqk', q, k) * scale
        causal = jnp.tril(jnp.ones((l, l), dtype=bool))
        scores = jnp.where(causal[None, None, None, :, :], scores, -jnp.inf)
        attn = jax.nn.softmax(scores, axis=-1)
        out = jnp.einsum('bhgqk,bhkd->bhgqd', attn, v)
        out = out.reshape(b, Hq, l, Dh).transpose(0, 2, 1, 3).reshape(b, l, Hq * Dh)
        out = out.astype(x.dtype)
        return out @ wo.T

    def _L1_xattn_ref(hidden_q, kv_c, Wq, w_kc_q, w_kc_kv, W_qr, W_kr, Wo):
        import jax, jax.numpy as jnp
        import numpy as np
        B, S, L = (2, 256, 256)
        DIM_Q, H, K, D_C, D_CQ, R = (512, 16, 128, 128, 384, 64)

        def _rope_tables(seq_len, dim, dtype):
            inv_freq = 1.0 / 10000.0 ** (jnp.arange(0, dim, 2, dtype=dtype) / dim)
            t = jnp.arange(seq_len, dtype=dtype)
            freqs = t[:, None] * inv_freq[None, :]
            sin = jnp.repeat(jnp.sin(freqs), 2, axis=-1)
            cos = jnp.repeat(jnp.cos(freqs), 2, axis=-1)
            return (sin, cos)

        def _rotate_half(x):
            h = x.shape[-1] // 2
            return jnp.concatenate([-x[..., h:], x[..., :h]], axis=-1)
        b, s, _ = hidden_q.shape
        l = kv_c.shape[1]
        q_hk = (hidden_q @ Wq.T).reshape(b, s, H, K)
        q_big = jnp.einsum('bshk,hkq->bshq', q_hk, w_kc_q)
        sin, cos = _rope_tables(l, D_C, kv_c.dtype)
        kv_rope = kv_c * cos[None] + _rotate_half(kv_c) * sin[None]
        q_r = jnp.einsum('bshq,hqr->bhsr', q_big, W_qr)
        k_r = jnp.einsum('bld,hdr->bhlr', kv_rope, W_kr)
        scores = jnp.einsum('bhsr,bhlr->bhsl', q_r, k_r)
        attn = jax.nn.softmax(scores, axis=-1)
        ctx_c = jnp.einsum('bhsl,bld->bhsd', attn, kv_rope)
        ctx_lat = jnp.einsum('bhsd,hkd->bshk', ctx_c, w_kc_kv)
        out = ctx_lat.reshape(b, s, H * K) @ Wo.T
        return out

    def _L1_ffn_ref(hidden_states, gate_w, expert_bias, shared_gate_w, shared_up_w, shared_down_w, experts_gate_up, experts_down):
        import jax, jax.numpy as jnp
        import numpy as np
        B, S, H = (1, 256, 512)
        F = 256
        E = 16
        K = 2
        NS = 1
        ROUTE_SCALE = 1.0
        b, s, h = hidden_states.shape
        x = hidden_states.reshape(-1, h)
        T = x.shape[0]
        router_logits = (x @ gate_w).astype(jnp.float32)
        scores = jax.nn.sigmoid(router_logits)
        _, selected = jax.lax.top_k(scores + expert_bias[None, :], K)
        top_scores = jnp.take_along_axis(scores, selected, axis=1)
        top_scores = top_scores / (top_scores.sum(-1, keepdims=True) + 1e-20)
        top_scores = top_scores * ROUTE_SCALE
        shared = jax.nn.silu(x @ shared_gate_w) * (x @ shared_up_w) @ shared_down_w
        comb = jnp.zeros((T, E), jnp.float32).at[jnp.arange(T)[:, None], selected].add(top_scores)
        routed = jnp.zeros_like(x)
        for e in range(E):
            gu = x @ experts_gate_up[e]
            g, u = jnp.split(gu, 2, axis=-1)
            routed = routed + comb[:, e:e + 1] * (jax.nn.silu(g) * u @ experts_down[e])
        return (shared + routed).reshape(b, s, h)

    def _L2_attn_ref(x, W_qkv, W_proj):
        import jax, jax.numpy as jnp
        import numpy as np
        D_MODEL = 512
        N_HEAD = 16
        D_HEAD = D_MODEL // N_HEAD
        B, T, C = x.shape
        qkv = jnp.einsum('btc,oc->bto', x, W_qkv)
        q, k, v = jnp.split(qkv, 3, axis=-1)

        def heads(t):
            return t.reshape(B, T, N_HEAD, D_HEAD).transpose(0, 2, 1, 3)
        q, k, v = (heads(q), heads(k), heads(v))
        att = jnp.einsum('bhqd,bhkd->bhqk', q, k) / jnp.sqrt(jnp.float32(D_HEAD))
        causal = jnp.tril(jnp.ones((T, T), dtype=bool))
        att = jnp.where(causal, att, -jnp.inf)
        att = jax.nn.softmax(att, axis=-1)
        y = jnp.einsum('bhqk,bhkd->bhqd', att, v)
        y = y.transpose(0, 2, 1, 3).reshape(B, T, C)
        return jnp.einsum('btc,oc->bto', y, W_proj)

    def _L2_xattn_ref(hidden_q, kv_c, Wq, w_kc_q, w_kc_kv, W_qr, W_kr, Wo):
        import jax, jax.numpy as jnp
        import numpy as np
        B, S, L = (2, 256, 256)
        DIM_Q, H, K, D_C, D_CQ, R = (512, 16, 128, 128, 384, 64)

        def _rope_tables(length, dim):
            inv = 1.0 / 10000.0 ** (jnp.arange(0, dim, 2, dtype=jnp.float32) / dim)
            f = jnp.arange(length, dtype=jnp.float32)[:, None] * inv[None, :]
            sin = jnp.repeat(jnp.sin(f), 2, axis=-1)
            cos = jnp.repeat(jnp.cos(f), 2, axis=-1)
            return (sin, cos)

        def _rotate_half(x):
            half = x.shape[-1] // 2
            return jnp.concatenate([-x[..., half:], x[..., :half]], axis=-1)

        def _apply_rope(x, sin, cos):
            return x * cos + _rotate_half(x) * sin
        Bv, Sv, _ = hidden_q.shape
        _, Lv, _ = kv_c.shape
        q_hk = (hidden_q @ Wq.T).reshape(Bv, Sv, H, K)
        q_big = jnp.einsum('bshk,hkq->bshq', q_hk, w_kc_q)
        sin_q, cos_q = _rope_tables(Sv, D_CQ)
        q_big = _apply_rope(q_big, sin_q[None, :, None, :], cos_q[None, :, None, :])
        sin_k, cos_k = _rope_tables(Lv, D_C)
        kv_r = _apply_rope(kv_c, sin_k[None], cos_k[None])
        q_r = jnp.einsum('bshq,hqr->bhsr', q_big, W_qr)
        k_r = jnp.einsum('bld,hdr->bhlr', kv_r, W_kr)
        scores = jnp.einsum('bhsr,bhlr->bhsl', q_r, k_r)
        attn = jax.nn.softmax(scores, axis=-1)
        ctx_c = jnp.einsum('bhsl,bld->bhsd', attn, kv_r)
        ctx_lat = jnp.einsum('bhsd,hkd->bhsk', ctx_c, w_kc_kv)
        ctx = ctx_lat.transpose(0, 2, 1, 3).reshape(Bv, Sv, H * K)
        return ctx @ Wo.T

    def _L2_ffn_ref(x, A, B, Wr, br):
        import jax, jax.numpy as jnp
        import numpy as np
        RANK = 64
        SCALING = 1.0 / RANK
        TEMPERATURE = 1.0
        batch, seq, d = x.shape
        E, out_dim = (B.shape[0], B.shape[1])
        x_flat = x.reshape(-1, d)
        logits = (x_flat @ Wr.T + br) / TEMPERATURE
        probs = jax.nn.softmax(logits, axis=-1)
        expert_idx = jnp.argmax(probs, axis=-1)
        expert_weight = jnp.max(probs, axis=-1)
        h = jnp.einsum('nd,erd->ner', x_flat, A)
        y = jnp.einsum('ner,eor->neo', h, B) * SCALING
        sel = jnp.take_along_axis(y, expert_idx[:, None, None], axis=1)[:, 0, :]
        out_flat = sel * expert_weight[:, None]
        return out_flat.reshape(batch, seq, out_dim)

    def _L3_attn_ref(hidden_states, wq, wk, wv, wo, bern_u):
        import jax, jax.numpy as jnp
        import numpy as np
        H = 16
        SB_RATIO = 0.1
        RB_RATIO = 0.5
        ROPE_BASE = 10000.0

        def _rotate_half(x):
            hd = x.shape[-1]
            x1, x2 = (x[..., :hd // 2], x[..., hd // 2:])
            return jnp.concatenate([-x2, x1], axis=-1)
        B, T, D = hidden_states.shape
        hd = D // H
        h = jnp.nan_to_num(hidden_states, nan=0.0, posinf=10000.0, neginf=-10000.0)

        def proj(w):
            return (h @ w.T).reshape(B, T, H, hd).transpose(0, 2, 1, 3)
        Q, K, V = (proj(wq), proj(wk), proj(wv))
        inv_freq = 1.0 / ROPE_BASE ** (jnp.arange(0, hd, 2, dtype=jnp.float32) / hd)
        pos = jnp.arange(T, dtype=jnp.float32)
        freqs = pos[:, None] * inv_freq[None, :]
        emb = jnp.concatenate([freqs, freqs], axis=-1)
        cos, sin = (jnp.cos(emb)[None, None], jnp.sin(emb)[None, None])
        Q = Q * cos + _rotate_half(Q) * sin
        K = K * cos + _rotate_half(K) * sin
        sb = max(0, min(int(SB_RATIO * T), T))
        rb = max(0, min(int(RB_RATIO * T), T - sb))
        kidx = jnp.arange(T)
        cam = (kidx < sb) | (kidx >= T - rb)
        scores = jnp.einsum('bhqd,bhkd->bhqk', Q, K) / np.sqrt(hd).astype(np.float32)
        neg = jnp.finfo(scores.dtype).min
        scores = jnp.where(cam[None, None, None, :], scores, neg)
        scores = jnp.nan_to_num(scores, nan=neg)
        probs = jax.nn.softmax(scores, axis=-1)
        if 0 < rb < T:
            e = T - rb
            ws = e + 1
            if T - ws > 0:
                last = probs[..., -1, :]
                mean_attn = last[..., ws:].mean(axis=-1) + 1e-06
                p = jnp.clip(last[..., e] / mean_attn, 0.0, 1.0)
                p = jnp.nan_to_num(p, nan=0.0, posinf=1.0, neginf=0.0)
                mask = (bern_u < p).astype(V.dtype)
                v_e = V[..., e, :] * mask[..., None] / rb
                end = min(T, ws + rb)
                V = V.at[..., ws:end, :].add(v_e[..., None, :])
        out = jnp.einsum('bhqk,bhkd->bhqd', probs, V)
        out = out.transpose(0, 2, 1, 3).reshape(B, T, D) @ wo.T
        return jnp.nan_to_num(out, nan=0.0, posinf=10000.0, neginf=-10000.0)

    def _L3_xattn_ref(q, latent_kv, Wq, Wkv_expand, Wout):
        import jax, jax.numpy as jnp
        import numpy as np
        B, S, H, NH, L = (2, 512, 512, 16, 128)
        HD = H // NH
        b, sq, _ = q.shape
        sk = latent_kv.shape[1]
        qp = q @ Wq.T
        kv = latent_kv @ Wkv_expand.T
        k, v = jnp.split(kv, 2, axis=-1)
        qh = qp.reshape(b, sq, NH, HD).transpose(0, 2, 1, 3)
        kh = k.reshape(b, sk, NH, HD).transpose(0, 2, 1, 3)
        vh = v.reshape(b, sk, NH, HD).transpose(0, 2, 1, 3)
        inv_sqrt_d = 1.0 / jnp.sqrt(jnp.float32(HD))
        scores = jnp.einsum('bhqd,bhkd->bhqk', qh, kh) * inv_sqrt_d
        causal = jnp.tril(jnp.ones((sq, sk), dtype=bool))
        scores = jnp.where(causal, scores, jnp.finfo(scores.dtype).min)
        attn = jax.nn.softmax(scores, axis=-1)
        out = jnp.einsum('bhqk,bhkd->bhqd', attn, vh)
        out = out.transpose(0, 2, 1, 3).reshape(b, sq, H)
        return out @ Wout.T

    def _L3_ffn_ref(h, gate_w, gu_w, dp_w, sh_gate_w, sh_up_w, sh_down_w, sh_gate1_w):
        import jax, jax.numpy as jnp
        import numpy as np
        H = 512
        E = 64
        I = 128
        SI = 128
        TOP_K = 8
        B, T = (2, 128)
        Bb, Tt, Hh = h.shape
        x = h.reshape(Bb * Tt, Hh)
        N = x.shape[0]
        logits = x @ gate_w.T
        topv, topi = jax.lax.top_k(logits, TOP_K)
        rw = jax.nn.softmax(topv.astype(jnp.float32), axis=-1).astype(x.dtype)
        W = jnp.zeros((N, E), x.dtype).at[jnp.arange(N)[:, None], topi].set(rw)
        gu = jnp.einsum('nh,eih->nei', x, gu_w)
        gate, up = (gu[..., :I], gu[..., I:])
        inter = jax.nn.silu(gate) * up
        inter_w = inter * W[:, :, None]
        out = jnp.einsum('nei,ehi->nh', inter_w, dp_w)
        sh_inter = jax.nn.silu(x @ sh_gate_w.T) * (x @ sh_up_w.T)
        sh_out = sh_inter @ sh_down_w.T
        sh_g = jax.nn.sigmoid(x @ sh_gate1_w.T)
        out = out + sh_g * sh_out
        return out.reshape(Bb, Tt, Hh)
    x = _layernorm(x + _L0_attn_ref(x, L0_attn_w_qkv, L0_attn_w_swiglu, L0_attn_w_out), axis=-1)
    x = _layernorm(x + _L0_xattn_ref(x, ctx_512, L0_xattn_Wq, L0_xattn_Wkv_expand, L0_xattn_Wout), axis=-1)
    x = _layernorm(x + _L0_ffn_ref(x, L0_ffn_SU_ug, L0_ffn_SU_dp, L0_ffn_Wscale_ug, L0_ffn_Wscale_dp, L0_ffn_W_up, L0_ffn_W_gate, L0_ffn_W_down), axis=-1)
    x = _layernorm(x + _L1_attn_ref(x, L1_attn_wq, L1_attn_wk, L1_attn_wv, L1_attn_wo, L1_attn_bq, L1_attn_bk, L1_attn_bv), axis=-1)
    x = _layernorm(x + _L1_xattn_ref(x, ctx_512, L1_xattn_Wq, L1_xattn_w_kc_q, L1_xattn_w_kc_kv, L1_xattn_W_qr, L1_xattn_W_kr, L1_xattn_Wo), axis=-1)
    x = _layernorm(x + _L1_ffn_ref(x, L1_ffn_gate_w, L1_ffn_expert_bias, L1_ffn_shared_gate_w, L1_ffn_shared_up_w, L1_ffn_shared_down_w, L1_ffn_experts_gate_up, L1_ffn_experts_down), axis=-1)
    x = _layernorm(x + _L2_attn_ref(x, L2_attn_W_qkv, L2_attn_W_proj), axis=-1)
    x = _layernorm(x + _L2_xattn_ref(x, ctx_512, L2_xattn_Wq, L2_xattn_w_kc_q, L2_xattn_w_kc_kv, L2_xattn_W_qr, L2_xattn_W_kr, L2_xattn_Wo), axis=-1)
    x = _layernorm(x + _L2_ffn_ref(x, L2_ffn_A, L2_ffn_B, L2_ffn_Wr, L2_ffn_br), axis=-1)
    x = _layernorm(x + _L3_attn_ref(x, L3_attn_wq, L3_attn_wk, L3_attn_wv, L3_attn_wo, L3_attn_bern_u), axis=-1)
    x = _layernorm(x + _L3_xattn_ref(x, ctx_512, L3_xattn_Wq, L3_xattn_Wkv_expand, L3_xattn_Wout), axis=-1)
    x = _layernorm(x + _L3_ffn_ref(x, L3_ffn_gate_w, L3_ffn_gu_w, L3_ffn_dp_w, L3_ffn_sh_gate_w, L3_ffn_sh_up_w, L3_ffn_sh_down_w, L3_ffn_sh_gate1_w), axis=-1)
    return x

_drawn_inputs = setup_inputs


def setup_inputs(seed=0):
    import zlib

    import numpy as np

    out = dict(_drawn_inputs(seed))
    spreads = {'L1_ffn_expert_bias': (0.0, 0.1), 'L2_ffn_br': (0.0, 0.8)}
    factors = {'L0_attn_w_qkv': 8.0,
     'L0_attn_w_swiglu': 8.0,
     'L0_attn_w_out': 8.0,
     'L0_xattn_Wq': 3.932,
     'L1_attn_wq': 2.827,
     'L1_attn_bq': 23.076,
     'L1_attn_bk': 8.0,
     'L2_ffn_A': 8.0,
     'L2_ffn_B': 8.0,
     'L2_ffn_Wr': 8.0,
     'L3_attn_wq': 8.0,
     'L3_attn_wk': 8.0,
     'L3_attn_bern_u': 200.0,
     'L3_xattn_Wq': 8.0,
     'L3_ffn_gate_w': 6.001,
     'L3_ffn_gu_w': 5.461,
     'L3_ffn_dp_w': 5.398,
     'L3_ffn_sh_gate_w': 4.308,
     'L3_ffn_sh_up_w': 4.058,
     'L3_ffn_sh_down_w': 4.033,
     'L3_ffn_sh_gate1_w': 8.0}
    for name, (base, spread) in spreads.items():
        noise = np.random.default_rng([zlib.crc32(name.encode()), seed]).standard_normal(out[name].shape)
        drawn = base * np.exp(spread * noise) if base else spread * noise
        out[name] = jnp.asarray(drawn.astype(out[name].dtype))
    for name, factor in factors.items():
        out[name] = (out[name] * factor).astype(out[name].dtype)
    return out
```

```python
import numpy as np
import concourse.bass as bass
from concourse import mybir

ALU = mybir.AluOpType
ACT = mybir.ActivationFunctionType
F32 = mybir.dt.float32
U32 = mybir.dt.uint32
AX = mybir.AxisListType

NB, S, L, T, H2 = 8, 100, 361, 800, 400
SLOT, RING = 2048, 6
ARENA = 25600
NEG = -1.0e30



def fm(w):
    o, i = w.shape
    m = min(128, o)
    return w.reshape(o // m, m, i // 128, 128).transpose(3, 0, 2, 1).reshape(128, -1)


def tm(w):
    o, i = w.shape
    return w.T.reshape(i // 128, 128, o).transpose(1, 0, 2).reshape(128, -1)


def col(v):
    return v.reshape(-1, 128).T


def rows(v):
    return np.broadcast_to(v.reshape(1, -1), (128, v.size))


def hadamard(n):
    h = np.ones((1, 1), np.float32)
    while h.shape[0] < n:
        h = np.block([[h, h], [h, -h]])
    return h.astype(np.float32)


def swap_matrix(width):
    m = np.zeros((128, 128), np.float32)
    for p in range(128):
        m[p - p % width + (p % width + width // 2) % width, p] = 1.0
    return m


def rope32(pos, div):
    half = 16
    if div:
        inv = (np.float32(1.0) / np.float32(10000.0) ** (np.arange(0, 32, 2, dtype=np.float32) / np.float32(32))).astype(np.float32)
    else:
        inv = (np.float32(10000.0) ** (-np.arange(half, dtype=np.float32) / np.float32(half))).astype(np.float32)
    ang = (np.asarray(pos, np.float32)[None, :] * inv[:, None]).astype(np.float32)
    c, s = np.cos(ang), np.sin(ang)
    c = np.tile(np.concatenate([c, c], 0), (4, 1))
    s = np.tile(np.concatenate([-s, s], 0), (4, 1))
    return c.astype(np.float32), s.astype(np.float32)


def rope_mla(n, dim):
    inv = (np.float32(1.0) / np.float32(10000.0) ** (np.arange(0, dim, 2, dtype=np.float32) / np.float32(dim))).astype(np.float32)
    f = (np.arange(n, dtype=np.float32)[:, None] * inv[None, :]).astype(np.float32)
    return np.repeat(np.cos(f), 2, -1).T.astype(np.float32), np.repeat(np.sin(f), 2, -1).T.astype(np.float32)


def shape_constants():
    c = {}
    c["ident"] = np.eye(128, dtype=np.float32)
    c["mean"] = np.full((128, 128), 1.0 / 512, np.float32)
    c["had"] = hadamard(128)
    c["nhad"] = -hadamard(128)
    c["swap32"] = swap_matrix(32)
    c["swap128"] = swap_matrix(128)
    c["cos1"], c["sin1"] = rope32(range(S), False)
    c["cos3"], c["sin3"] = rope32(range(S), True)
    co, si = rope_mla(L, 128)
    sg = np.where(np.arange(128) < 64, -1.0, 1.0).astype(np.float32)[:, None]
    c["cosk"], c["sink"] = co, si * sg
    co, si = rope_mla(S, 384)
    perm = q384()
    partner = (np.arange(384) + 192) % 384
    sign = np.where(partner < 192, -1.0, 1.0).astype(np.float32)[:, None]
    c["cosq"] = co[perm].reshape(3, 128, S).transpose(1, 0, 2).reshape(128, -1)
    c["sinq"] = (si[partner] * sign)[perm].reshape(3, 128, S).transpose(1, 0, 2).reshape(128, -1)
    cm = np.zeros((128, S), np.float32)
    cm[:S] = np.where(np.arange(S)[:, None] >= np.arange(S)[None, :], 0.0, NEG)
    c["causal"] = cm
    e = np.zeros((128, S), np.float32)
    e[S - 1] = 1.0
    c["lastrow"] = e
    c["iota"] = rows(np.arange(64, dtype=np.float32))
    sel = np.zeros((128, 4, 128), np.float32)
    for k in range(4):
        for p in range(128):
            sel[2 * k + p // 64, k, p] = 1.0
    c["sel8"] = sel.reshape(128, -1)
    m = np.ones((128, H2), np.float32)
    m[:, ::S] = 0.0
    c["restart"] = m
    c["eps"] = rows(np.array([1.1920929e-07, 1e-05, 0.0, 1.0], np.float32))
    return c


def q384():
    b = np.arange(384).reshape(6, 64)
    return np.concatenate([np.concatenate([b[t], b[t + 3]]) for t in range(3)])


PARAMS = {
    "su": (4, lambda i: col(i["L0_ffn_SU_ug"])),
    "sud": (16, lambda i: col(i["L0_ffn_SU_dp"])),
    "wsu": (16, lambda i: col(i["L0_ffn_Wscale_ug"][:2048])),
    "wsg": (16, lambda i: col(i["L0_ffn_Wscale_ug"][2048:])),
    "wsd": (4, lambda i: col(i["L0_ffn_Wscale_dp"])),
    "bq": (4, lambda i: col(i["L1_attn_bq"])),
    "bk": (2, lambda i: col(np.tile(i["L1_attn_bk"].reshape(2, 1, 32), (1, 4, 1)).reshape(-1))),
    "bv": (64, lambda i: rows(i["L1_attn_bv"])),
    "g1w": (64, lambda i: tm(i["L1_ffn_gate_w"].T)),
    "g1b": (16, lambda i: rows(i["L1_ffn_expert_bias"])),
    "wr": (32, lambda i: tm(i["L2_ffn_Wr"])),
    "br": (8, lambda i: rows(i["L2_ffn_br"])),
    "bern": (16, lambda i: rows(i["L3_attn_bern_u"])),
    "g3w": (260, lambda i: tm(np.concatenate([i["L3_ffn_gate_w"], i["L3_ffn_sh_gate1_w"]]))),
}



class Tok:

    def __init__(self, sem, val):
        self.sem, self.val = sem, val


class Eng:

    def __init__(self, name, sem):
        self.name, self.sem, self.n, self.q, self.met = name, sem, 0, [], {}

    def wait(self, *toks):
        for t in toks:
            if t is None:
                continue
            if isinstance(t, (list, tuple)):
                self.wait(*t)
                continue
            if self.met.get(id(t.sem), 0) < t.val:
                self.met[id(t.sem)] = t.val
                self.q.append((t, None, False))

    def do(self, fn, *toks, inc=True):
        self.wait(*toks)
        self.q.append((None, fn, inc))
        if inc:
            self.n += 1
            return Tok(self.sem, self.n)

    def now(self):
        return Tok(self.sem, self.n) if self.n else None

    def flush(self, eng):
        for t, fn, inc in self.q:
            if t is not None:
                eng.wait_ge(t.sem, t.val)
            else:
                i = fn(eng)
                if inc:
                    i.then_inc(self.sem, 1)


class Piece:
    def __init__(self, ap, tok, n, pack):
        self.ap, self.tok, self.n, self.pack, self.rel = ap, tok, n, pack, None


def pipeline(n, *stages):
    for t in range(n + len(stages) - 1):
        for s in range(len(stages) - 1, -1, -1):
            if 0 <= t - s < n:
                stages[s](t - s)


def bc(ap, shape, axis=1):
    return ap.unsqueeze(axis).to_broadcast(shape)


class K:
    def __init__(self, nc, stack, layers):
        self.nc, self.layers = nc, layers
        en = stack.enter_context
        self.sem = lambda name: en(nc.semaphore(name))
        self.pe, self.act, self.dve, self.pool = (Eng(n, self.sem("s_" + n)) for n in ("pe", "act", "dve", "pool"))
        self.sp = Eng("sp", self.sem("s_sp"))
        sb = lambda name, n: en(nc.sbuf_tensor(name, [128, n], F32))
        self.W = sb("W", RING * SLOT)
        self.wsem = [self.sem(f"s_w{i}") for i in range(RING)]
        self.loads = []
        self.consts = shape_constants()
        self.cw = sum(v.shape[1] for v in self.consts.values()) + sum(n for n, _ in PARAMS.values())
        self.C = sb("C", self.cw)
        self.c, at = {}, 0
        for k, v in self.consts.items():
            self.c[k] = self.C[:, at:at + v.shape[1]]
            at += v.shape[1]
        for k, (n, _) in PARAMS.items():
            self.c[k] = self.C[:, at:at + n]
            at += n
        self.X = sb("X", 4 * T)
        self.x = self.X[:, :].rearrange("p (c t) -> p c t", c=4)
        self.CX = sb("CX", T)
        self.KF = sb("KF", NB * L)
        self.KT = sb("KT", NB * 3 * 128)
        self.A = sb("A", ARENA)
        self.small = sb("small", 832)
        self.P = [en(nc.psum_tensor(f"P{i}", [128, 512], F32)) for i in range(8)]
        self.free = [None] * 8
        self.nb = 0
        self.s_in = [self.sem(f"s_in{i}") for i in range(4)]
        self.s_out = self.sem("s_out")
        self.ic, self.ix, self.ik, self.ik2 = (Tok(s, 16) for s in self.s_in)
        self.xt = [self.ix, self.ix]

    def ar(self, at, *shape):
        n = int(np.prod(shape))
        assert at + n <= ARENA, (at, n)
        v = self.A[:, at:at + n]
        if len(shape) == 2:
            return v.rearrange("p (a b) -> p a b", a=shape[0])
        if len(shape) == 3:
            return v.rearrange("p (a b c) -> p a b c", a=shape[0], b=shape[1])
        return v

    def load(self, n, pack):
        assert n <= SLOT
        i = len(self.loads)
        s = i % RING
        if i >= RING:
            assert self.loads[i - RING].rel is not None, "the ring's slot is not released"
        p = Piece(self.W[:, s * SLOT:s * SLOT + n], Tok(self.wsem[s], 16 * (i // RING + 1)), n, pack)
        self.loads.append(p)
        return p

    def bank(self):
        b = self.nb % 8
        self.nb += 1
        assert self.free[b] != "busy", b
        self.pe.wait(self.free[b])
        self.free[b] = "busy"
        return b

    def barrier(self):
        es = (self.pe, self.act, self.dve, self.pool)
        now = [e.now() for e in es]
        for e in es:
            e.wait(*now)

    def mm(self, out, lhsT, rhs, start, stop, *toks, inc=False):
        return self.pe.do(lambda e: e.matmul(out, lhsT, rhs, start=start, stop=stop), *toks, inc=inc)

    def tr(self, out, in_, n, *toks, inc=False):
        idn = self.c["ident"][0:n, 0:n]
        return self.pe.do(lambda e: e.transpose(out, in_, idn), *toks, inc=inc)

    def chain(self, out, pairs, *toks):
        self.pe.wait(*toks)
        n = len(pairs)
        for i, (a, b) in enumerate(pairs):
            t = self.mm(out, a, b, i == 0, i == n - 1, inc=i == n - 1)
        return t

    def copy(self, eng, out, in_, *toks):
        if eng is self.act:
            return eng.do(lambda e: e.activation(out, in_, ACT.Copy), *toks)
        return eng.do(lambda e: e.tensor_copy(out, in_), *toks)

    def af(self, out, in_, func, *toks, **kw):
        return self.act.do(lambda e: e.activation(out, in_, func, **kw), *toks)

    def tt(self, out, a, b, op, *toks, eng=None):
        return (eng or self.dve).do(lambda e: e.tensor_tensor(out, a, b, op), *toks)

    def ts(self, out, a, s1, s2, o0, o1, *toks, eng=None):
        if o1 is None:
            return (eng or self.dve).do(lambda e: e.tensor_scalar(out, a, s1, None, o0), *toks)
        return (eng or self.dve).do(lambda e: e.tensor_scalar(out, a, s1, s2, o0, o1), *toks)

    def stt(self, out, a, s, b, o0, o1, *toks):
        return self.dve.do(lambda e: e.scalar_tensor_tensor(out=out, in0=a, scalar=s, in1=b, op0=o0, op1=o1), *toks)

    def rec(self, out, a, *toks):
        return self.dve.do(lambda e: e.reciprocal(out, a), *toks)

    def red(self, out, a, op, *toks, negate=None):
        return self.dve.do(lambda e: e.tensor_reduce(out, a, AX.X, op, negate=negate), *toks)

    def hs(self, h):
        return slice(H2 * h, H2 * h + H2)

    def rstd(self, src, sq, r, eps, h, *toks):
        hs = self.hs(h)
        t = self.af(sq[:, :, hs], src[:, :, hs], ACT.Square, *toks)
        b = self.bank()
        t = self.chain(self.P[b][:, 0:H2], [(self.c["mean"], sq[:, c, hs]) for c in range(4)], t, self.ic)
        t = self.af(r[:, hs], self.P[b][:, 0:H2], ACT.Sqrt, t, bias=self.c["eps"][:, eps:eps + 1])
        self.free[b] = t
        return self.rec(r[:, hs], r[:, hs], t)

    def layernorm(self, z, sq, r, zt):
        for h in range(2):
            hs = self.hs(h)
            b = self.bank()
            t = self.chain(self.P[b][:, 0:H2], [(self.c["mean"], z[:, c, hs]) for c in range(4)], zt[h])
            t = self.tt(z[:, :, hs], z[:, :, hs], bc(self.P[b][:, 0:H2], [128, 4, H2]), ALU.subtract, t)
            self.free[b] = t
            t = self.rstd(z, sq, r, 1, h, t)
            self.xt[h] = self.tt(self.x[:, :, hs], z[:, :, hs], bc(r[:, hs], [128, 4, H2]), ALU.mult, t)

    def project(self, w, rhs, rt, kc, ms, evac, wt=None):
        for m in ms:
            for h in range(2):
                b = self.bank()
                t = self.chain(self.P[b][:, 0:H2], [(w(m, k), rhs(k, h)) for k in range(kc)], rt[h], wt)
                self.free[b] = evac(m, h, self.P[b][:, 0:H2], t)
        return self.pe.now()

    def full(self, name, sel, src, rt, evac, nm=4):
        for g in range(0, nm, 4):
            p = self.load(2048, lambda i, g=g: fm(sel(i[name])[g * 128:(g + 4) * 128]))
            w = p.ap.rearrange("p (m k c) -> p m k c", m=4, k=4)
            p.rel = self.project(lambda m, k: w[:, m - g, k, :], lambda k, h: src[:, k, self.hs(h)], rt, 4,
                                 range(g, g + 4), evac, p.tok)

    def add_residual(self, z, zt):
        def evac(m, h, ps, t):
            zt[h] = self.tt(z[:, m, self.hs(h)], ps, self.x[:, m, self.hs(h)], ALU.add, t)
            return zt[h]
        return evac

    def l0_attn(self):
        self.barrier()
        x = self.x
        SQ, R, XN = self.ar(0, 4, T), self.ar(3200, T), self.ar(4000, 4, T)
        Q, Kk, V = self.ar(7200, 4, T), self.ar(10400, 4, T), self.ar(13600, 4, T)
        xn = [None, None]
        for h in range(2):
            hs = self.hs(h)
            t = self.rstd(x, SQ, R, 0, h, self.xt[h])
            xn[h] = self.tt(XN[:, :, hs], x[:, :, hs], bc(R[:, hs], [128, 4, H2]), ALU.mult, t)
        dst = [Q, Kk, V]
        done = {}

        def evac(m, h, ps, t):
            t = self.copy(self.act if m % 2 else self.dve, dst[m // 4][:, m % 4, self.hs(h)], ps, t)
            done.setdefault((m // 4, h), []).append(t)
            return t
        self.full("L0_attn_w_qkv", lambda w: w, XN, xn, evac, 12)
        yt = [None, None]
        self.barrier()
        for h in range(2):
            hs = self.hs(h)
            v3 = lambda a: a[:, :, hs]
            rb = bc(R[:, hs], [128, 4, H2])
            t = self.rstd(Q, SQ, R, 0, h)
            t = self.tt(v3(Q), v3(Q), rb, ALU.mult, t)
            tq = self.af(v3(Q), v3(Q), ACT.Sigmoid, t)
            t = self.rstd(Kk, SQ, R, 0, h, tq)
            t = self.tt(v3(Kk), v3(Kk), rb, ALU.mult, t)
            t = self.af(v3(Kk), v3(Kk), ACT.Exp, t)
            t = self.tt(v3(V), v3(V), v3(Kk), ALU.mult, t)
            for c in range(4):
                for src in (V, Kk):
                    ap = src[:, c, hs]
                    t = self.dve.do(lambda e, ap=ap, o=(SQ if src is V else XN)[:, c, hs]: e.tensor_tensor_scan(
                        o, self.c["restart"], ap, 0.0, ALU.mult, ALU.add), t)
            t = self.ts(v3(XN), v3(XN), 1e-6, None, ALU.add, None, t)
            t = self.rec(v3(XN), v3(XN), t)
            t = self.tt(v3(XN), v3(XN), v3(SQ), ALU.mult, t)
            yt[h] = self.tt(v3(Q), v3(XN), v3(Q), ALU.mult, t, tq)
        H = self.ar(10400, 16, T)
        G = self.ar(23200, 2, H2)
        self.barrier()
        ht = [None, None]
        gfree = [None, None]
        n = 0
        for g in range(8):
            p = self.load(2048, lambda i, g=g: np.concatenate(
                [fm(i["L0_attn_w_swiglu"][256 * g:256 * g + 256]), fm(i["L0_attn_w_swiglu"][2048 + 256 * g:2304 + 256 * g])], 1))
            w = p.ap.rearrange("p (m k c) -> p m k c", m=4, k=4)
            for m in range(2):
                for h in range(2):
                    hs = self.hs(h)
                    bu, bg = self.bank(), self.bank()
                    tu = self.chain(self.P[bu][:, 0:H2], [(w[:, m, k, :], Q[:, k, hs]) for k in range(4)], yt[h], p.tok)
                    tg = self.chain(self.P[bg][:, 0:H2], [(w[:, 2 + m, k, :], Q[:, k, hs]) for k in range(4)])
                    t = self.af(G[:, n % 2, :], self.P[bg][:, 0:H2], ACT.Silu, tg, gfree[n % 2])
                    self.free[bg] = t
                    t = self.tt(H[:, 2 * g + m, hs], self.P[bu][:, 0:H2], G[:, n % 2, :], ALU.mult, tu, t)
                    self.free[bu] = gfree[n % 2] = ht[h] = t
                    n += 1
            p.rel = self.pe.now()
        Z, zt = self.ar(4000, 4, T), [None, None]
        for m in range(4):
            p = self.load(2048, lambda i, m=m: fm(i["L0_attn_w_out"][128 * m:128 * m + 128]))
            w = p.ap.rearrange("p (k c) -> p k c", k=16)

            def evac(m, h, ps, t):
                zt[h] = self.stt(Z[:, m, self.hs(h)], x[:, m, self.hs(h)], 2.0, ps, ALU.mult, ALU.add, t)
                return zt[h]
            p.rel = self.project(lambda m, k: w[:, k, :], lambda k, h: H[:, k, self.hs(h)], ht, 16, [m], evac, p.tok)
        self.layernorm(Z, SQ, R, zt)

    def heads32(self, name, qt, kt, V, vt, nk, mask, at, out, group, special=None):
        scale = float(np.float32(1.0) / np.sqrt(np.float32(32)))
        E = [self.ar(at + 1600 * i, 16, S) for i in range(2)]
        PT = [self.ar(at + 3200 + 1600 * i, 16, S) for i in range(2)]
        O = [self.ar(at + 6400 + 512 * i, 16, 32) for i in range(2)]
        M = [self.small[:, 64 * i:64 * i + 64] for i in range(2)]
        st = {}

        def scores(b):
            e, m = E[b % 2], M[b % 2]
            prev = st.get(("pt", b - 2))
            ks = [self.bank() for _ in range(4)]
            tk = {}
            for g in range(4):
                for j in range(4):
                    q = qt[32 * j:32 * j + 32, g, S * b:S * b + S]
                    tk[j] = self.mm(self.P[ks[j]][0:S, nk * g:nk * g + nk], q, kt(4 * g + j, b), True, True, inc=g == 3)
            for j in range(4):
                o = e[0:S, j:16:4, 0:nk]
                ps = self.P[ks[j]][0:S, 0:4 * nk].rearrange("p (a b) -> p a b", a=4)
                if mask is None:
                    t = self.copy(self.act, o, ps, tk[j], prev)
                else:
                    t = self.tt(o, ps, bc(mask[0:S, 0:nk], [S, 4, nk]), ALU.add, tk[j], prev)
                self.free[ks[j]] = t
            v = e[0:S, :, 0:nk]
            t = self.red(m[0:S, 0:16], v, ALU.max, t)
            t = self.tt(v, v, bc(m[0:S, 0:16], [S, 16, nk], 2), ALU.subtract, t)
            t = self.af(v, v, ACT.Exp, t, scale=scale)
            if special is not None:
                t = special(e, m, t)
            st["e", b] = t

        def turn(b):
            e, pt = E[b % 2], PT[b % 2]
            for g in range(4):
                k = self.bank()
                ps = self.P[k][0:nk, 0:4 * S].rearrange("p (a b) -> p a b", a=4)
                for j in range(4):
                    t = self.tr(ps[:, j, :], e[0:S, 4 * g + j, 0:nk], S, st["e", b], inc=j == 3)
                st["pt", b] = t
                t = self.copy(self.act if g % 2 else self.dve, pt[0:nk, 4 * g:4 * g + 4, :], ps, t, st.get(("pv", b - 2)))
                self.free[k] = t
                st["c", b, g] = t

        def values(b):
            pt, o, m = PT[b % 2], O[b % 2], M[b % 2]
            for half in range(2):
                k = self.bank()
                ps = self.P[k][0:S, 0:264].rearrange("p (a b) -> p a b", a=8)
                for j in range(8):
                    h = 8 * half + j
                    t = self.mm(ps[:, j, :], pt[0:nk, h, :], V[0:nk, b, h // group, :], True, True,
                                st["c", b, h // 4], vt(b), inc=j == 7)
                st["pv", b] = t
                if special is None:
                    r = m[0:S, 16 + 8 * half:24 + 8 * half]
                    t = self.rec(r, ps[:, :, 32], t)
                else:
                    r = m[0:S, 48 + 8 * half:56 + 8 * half]
                t = self.tt(o[0:S, 8 * half:8 * half + 8, :], ps[:, :, 0:32], bc(r, [S, 8, 32], 2), ALU.mult, t,
                            st.get(("ot", b - 2)))
                self.free[k] = t
            st["o", b] = t

        def back(b):
            k = self.bank()
            o = O[b % 2]
            ps = self.P[k][:, 0:4 * S].rearrange("p (a b) -> p a b", a=4)
            for c in range(4):
                t = self.tr(ps[:, c, :], o[0:S, 4 * c:4 * c + 4, :].rearrange("p a b -> p (a b)"), S, st["o", b], inc=c == 3)
            st["ot", b] = t
            t = self.copy(self.act, out[:, :, S * b:S * b + S], ps, t)
            self.free[k] = t
            ot[b // 4] = t
        ot = [None, None]
        pipeline(NB, scores, turn, values, back)
        return ot

    def values_tm(self, V, w, wt, src, heads, rt, bias=None, nk=S):
        ones = self.dve.do(lambda e: e.memset(V[0:nk, :, :, 32], 1.0))
        vt = {}
        for b in range(NB):
            k = self.bank()
            n = heads * 32
            t = self.chain(self.P[k][0:nk, 0:n], [(src(c, b), w(c)) for c in range(4)] if w(1) is not None else
                           [(src(0, b), w(0))], rt[b // 4], wt)
            o = V[0:nk, b, :, 0:32]
            ps = self.P[k][0:nk, 0:n].rearrange("p (a b) -> p a b", b=32)
            if bias is None:
                t = self.copy(self.act if b % 2 else self.dve, o, ps, t)
            else:
                t = self.tt(o, ps, bias[0:nk, :].rearrange("p (a b) -> p a b", b=32), ALU.add, t)
            self.free[k] = t
            vt[b] = [t, ones]
        return lambda b: vt[b]

    def xattn(self, pre):
        self.barrier()
        Q, Kk, V = self.ar(0, 4, T), self.ar(3200, 4, T), self.ar(6400, NB, 16 * 33)
        V = V.rearrange("p b (h d) -> p b h d", h=16)
        cx = self.CX
        p = self.load(1024, lambda i: np.concatenate([fm(i[pre + "Wkv_expand"][:512]), tm(i[pre + "Wkv_expand"][512:])], 1))
        wk = p.ap[:, 0:512].rearrange("p (m c) -> p m c", m=4)
        wv = p.ap[:, 512:1024]
        kd, qd = [], []

        def ek(m, h, ps, t):
            t = self.copy(self.act, Kk[:, m, self.hs(h)], ps, t)
            kd.append(t)
            return t

        def eq(m, h, ps, t):
            t = self.copy(self.dve, Q[:, m, self.hs(h)], ps, t)
            qd.append(t)
            return t
        self.project(lambda m, k: wk[:, m, :], lambda k, h: cx[:, self.hs(h)], [self.ik, self.ik], 1, range(4), ek, p.tok)
        vt = self.values_tm(V, lambda c: wv if c == 0 else None, p.tok, lambda c, b: cx[:, S * b:S * b + S], 16,
                            [self.ik, self.ik])
        p.rel = self.pe.now()
        self.full(pre + "Wq", lambda w: w, self.x, self.xt, eq)
        self.pe.wait(qd[-1], kd[-1])
        OT = self.ar(10624, 4, T)
        kt = lambda h, b: Kk[32 * (h % 4):32 * (h % 4) + 32, h // 4, S * b:S * b + S]
        ot = self.heads32(pre, Q, kt, V, vt, S, self.c["causal"], 13824, OT, 1)
        self.out_proj(pre + "Wout", OT, ot)

    def out_proj(self, name, OT, ot):
        Z, zt = self.ar(0, 4, T), [None, None]
        self.dve.wait(self.pe.now())
        self.full(name, lambda w: w, OT, ot, self.add_residual(Z, zt))
        self.act.wait(self.pe.now())
        self.layernorm(Z, self.ar(3200, 4, T), self.ar(6400, T), zt)

    def rope(self, src, n, cos, sin, tmp, st, width):
        out = []
        for m in range(n):
            for h in range(2):
                hs = self.hs(h)
                b = self.bank()
                t = self.mm(self.P[b][:, 0:H2], self.c[width], src[:, m, hs], True, True, st[m, h], inc=True)
                s4 = src[:, m, hs].rearrange("p (b s) -> p b s", b=4)
                p4 = self.P[b][:, 0:H2].rearrange("p (b s) -> p b s", b=4)
                i = (2 * m + h) % 2
                tm4 = tmp[:, H2 * i:H2 * i + H2].rearrange("p (b s) -> p b s", b=4)
                t1 = self.tt(tm4, p4, bc(sin, [128, 4, S]), ALU.mult, t)
                self.free[b] = t1
                t2 = self.tt(s4, s4, bc(cos, [128, 4, S]), ALU.mult, t)
                t = self.tt(s4, s4, tm4, ALU.add, t1, t2)
                out.append(t)
        return t

    def l1_attn(self):
        self.barrier()
        pre = "L1_attn_"
        Q, Kk, V = self.ar(0, 4, T), self.ar(3200, 2, T), self.ar(6400, NB, 66)
        V = V.rearrange("p b (h d) -> p b h d", h=2)
        p = self.load(1280, lambda i: np.concatenate(
            [fm(np.tile(i[pre + "wk"].reshape(2, 1, 32, 512), (1, 4, 1, 1)).reshape(256, 512)), tm(i[pre + "wv"])], 1))
        wk = p.ap[:, 0:1024].rearrange("p (m k c) -> p m k c", m=2, k=4)
        wv = p.ap[:, 1024:1280].rearrange("p (k c) -> p k c", k=4)
        kd, qd = {}, {}

        def ek(m, h, ps, t):
            kd[m, h] = self.af(Kk[:, m, self.hs(h)], ps, ACT.Identity, t, bias=self.c["bk"][:, m:m + 1])
            return kd[m, h]

        def eq(m, h, ps, t):
            qd[m, h] = self.af(Q[:, m, self.hs(h)], ps, ACT.Identity, t, bias=self.c["bq"][:, m:m + 1])
            return qd[m, h]
        self.project(lambda m, k: wk[:, m, k, :], lambda k, h: self.x[:, k, self.hs(h)], self.xt, 4, range(2), ek, p.tok)
        vt = self.values_tm(V, lambda c: wv[:, c, :], p.tok, lambda c, b: self.x[:, c, S * b:S * b + S], 2,
                            self.xt, bias=self.c["bv"])
        p.rel = self.pe.now()
        self.full(pre + "wq", lambda w: w, self.x, self.xt, eq)
        tmp = self.ar(7000, T)
        self.rope(Kk, 2, self.c["cos1"], self.c["sin1"], tmp, kd, "swap32")
        t = self.rope(Q, 4, self.c["cos1"], self.c["sin1"], tmp, qd, "swap32")
        self.pe.wait(t)
        OT = self.ar(10624, 4, T)
        kt = lambda h, b: Kk[32 * (h % 4):32 * (h % 4) + 32, h // 8, S * b:S * b + S]
        ot = self.heads32(pre, Q, kt, V, vt, S, self.c["causal"], 13824, OT, 8)
        self.out_proj(pre + "wo", OT, ot)

    def l2_attn(self):
        self.barrier()
        pre = "L2_attn_"
        Q, Kk, V = self.ar(0, 4, T), self.ar(3200, 4, T), self.ar(6400, NB, 16 * 33)
        V = V.rearrange("p b (h d) -> p b h d", h=16)
        dst, done = [Q, Kk], []

        def evac(m, h, ps, t):
            t = self.copy(self.act, dst[m // 4][:, m % 4, self.hs(h)], ps, t)
            done.append(t)
            return t
        self.full(pre + "W_qkv", lambda w: w[:1024], self.x, self.xt, evac, 8)
        p = self.load(2048, lambda i: tm(i[pre + "W_qkv"][1024:]))
        wv = p.ap.rearrange("p (k c) -> p k c", k=4)
        vt = self.values_tm(V, lambda c: wv[:, c, :], p.tok, lambda c, b: self.x[:, c, S * b:S * b + S], 16, self.xt)
        p.rel = self.pe.now()
        self.pe.wait(done[-1])
        OT = self.ar(10624, 4, T)
        kt = lambda h, b: Kk[32 * (h % 4):32 * (h % 4) + 32, h // 4, S * b:S * b + S]
        ot = self.heads32(pre, Q, kt, V, vt, S, self.c["causal"], 13824, OT, 1)
        self.out_proj(pre + "W_proj", OT, ot)

    def l3_attn(self):
        self.barrier()
        pre = "L3_attn_"
        SB, NK = 10, 60
        Q, Kk, V = self.ar(0, 4, T), self.ar(3200, 4, T), self.ar(6400, NB, 16 * 33)
        V = V.rearrange("p b (h d) -> p b h d", h=16)
        dst, done = [Q, Kk], {}

        def evac(m, h, ps, t):
            done[m, h] = self.copy(self.act, dst[m // 4][:, m % 4, self.hs(h)], ps, t)
            return done[m, h]
        self.full(pre + "wq", lambda w: w, self.x, self.xt, evac, 4)
        self.full(pre + "wk", lambda w: w, self.x, self.xt, lambda m, h, ps, t: evac(m + 4, h, ps, t), 4)
        XK = self.ar(12544, 4, NB * NK).rearrange("p c (b k) -> p c b k", b=NB)
        xs = self.x.rearrange("p c (b s) -> p c b s", b=NB)
        tx = []
        for c in range(4):
            tx.append(self.copy(self.dve, XK[:, c, :, 0:SB], xs[:, c, :, 0:SB], self.xt))
            tx.append(self.copy(self.dve, XK[:, c, :, SB:NK], xs[:, c, :, 50:S], self.xt))
        p = self.load(2048, lambda i: tm(i[pre + "wv"]))
        wv = p.ap.rearrange("p (k c) -> p k c", k=4)
        vt = self.values_tm(V, lambda c: wv[:, c, :], p.tok, lambda c, b: XK[:, c, b, :], 16, [tx, tx], nk=NK)
        p.rel = self.pe.now()
        tmp = self.ar(14464, T)
        sel = lambda o: {(m, h): done[m + o, h] for m in range(4) for h in range(2)}
        self.rope(Kk, 4, self.c["cos3"], self.c["sin3"], tmp, sel(4), "swap32")
        t = self.rope(Q, 4, self.c["cos3"], self.c["sin3"], tmp, sel(0), "swap32")
        KS = self.ar(10624, 4, NB * NK).rearrange("p c (b k) -> p c b k", b=NB)
        ks = Kk.rearrange("p c (b s) -> p c b s", b=NB)
        for c in range(4):
            self.copy(self.dve, KS[:, c, :, 0:SB], ks[:, c, :, 0:SB], t)
            t2 = self.copy(self.dve, KS[:, c, :, SB:NK], ks[:, c, :, 50:S], t)
        self.pe.wait(t2)
        OT = self.ar(3200, 4, T)
        kt = lambda h, b: KS[32 * (h % 4):32 * (h % 4) + 32, h // 4, b, :]

        def special(e, m, t):
            a, r, u, w = (m[0:S, 16 * i:16 * i + 16] for i in range(4))
            e50 = e[0:S, :, SB]
            t = self.red(a, e[0:S, :, 0:NK], ALU.add, t)
            t = self.rec(w, a, t)
            t = self.red(r, e[0:S, :, SB + 1:NK], ALU.add, t)
            t = self.tt(a, r, w, ALU.mult, t)
            t = self.ts(a, a, 1.0 / 49, 1e-6, ALU.mult, ALU.add, t)
            t = self.rec(a, a, t)
            t = self.tt(a, a, w, ALU.mult, t)
            t = self.tt(a, a, e50, ALU.mult, t)
            t = self.ts(a, a, 0.0, 1.0, ALU.max, ALU.min, t)
            t = self.tt(a, self.c["bern"][0:S, :], a, ALU.is_lt, t)
            k = self.bank()
            t = self.mm(self.P[k][0:S, 0:16], self.c["lastrow"][0:S, :], a, True, True, t, inc=True)
            t = self.stt(u, self.P[k][0:S, 0:16], 1.0 / 50, r, ALU.mult, ALU.mult, t)
            self.free[k] = t
            return self.tt(e50, e50, u, ALU.add, t)
        ot = self.heads32(pre, Q, kt, V, vt, NK, None, 15264, OT, 1, special)
        self.out_proj(pre + "wo", OT, ot)

    def prep(self):
        CF = self.ar(0, NB, L)
        kf = self.KF[:, :].rearrange("p (b l) -> p b l", b=NB)
        kt = self.KT[:, :].rearrange("p (b j d) -> p b j d", b=NB, j=3)
        tmp = self.ar(3200, 2, L)
        self.pe.wait(self.ic)
        last = {}
        for b in range(NB):
            k = self.bank()
            t = self.mm(self.P[k][:, 0:L], self.c["swap128"], CF[:, b, :], True, True, self.ik2, inc=True)
            t1 = self.tt(tmp[:, b % 2, :], self.P[k][:, 0:L], self.c["sink"], ALU.mult, t)
            self.free[k] = t1
            t2 = self.tt(kf[:, b, :], CF[:, b, :], self.c["cosk"], ALU.mult, t)
            t = self.tt(kf[:, b, :], kf[:, b, :], tmp[:, b % 2, :], ALU.add, t1, t2)
            k = self.bank()
            ps = self.P[k][:, 0:384].rearrange("p (j d) -> p j d", j=3)
            for j in range(3):
                n = min(128, L - 128 * j)
                t3 = self.tr(ps[0:n, j, :], kf[:, b, 128 * j:128 * j + n], 128, t, inc=j == 2)
            self.copy(self.act, kt[:, b, 0:2, :], ps[:, 0:2, :], t3)
            self.free[k] = self.copy(self.act, kt[0:L - 256, b, 2, :], ps[0:L - 256, 2, :])

    def mla(self, pre, roped):
        self.barrier()
        kf = self.KF[:, :].rearrange("p (b l) -> p b l", b=NB)
        kt = self.KT[:, :].rearrange("p (b j d) -> p b j d", b=NB, j=3)
        x = self.x
        Z = self.ar(0, 4, T)
        QE = self.ar(3200, 4, T)
        CT = self.ar(6400, 4, T)
        CL = self.ar(9600, 4, T)
        QH = self.ar(12800, 2, T)
        PQ = self.ar(14400, 2, 768)
        MH = self.ar(15936, 2, 128)
        QB = self.ar(16192, 2, 2400)
        Pm = self.ar(16192, 2, 4 * L)
        PT = self.ar(16192 + 8 * L, 2, 3 * H2)
        sm = self.small
        perm = q384() if roped else np.arange(384)
        part = (perm + 192) % 384
        zt = [None, None]
        for hg in range(4):
            wq = self.load(2048, lambda i, hg=hg: fm(i[pre + "Wq"][512 * hg:512 * hg + 512]))
            wqt = wq.ap.rearrange("p (m k c) -> p m k c", m=4, k=4)
            qt = {}
            self.barrier()
            for hh in range(4):
                h = 4 * hg + hh
                if roped:
                    p = self.load(384 + 384 + 128 + 384, lambda i, h=h: pad_rows(
                        [i[pre + "W_qr"][h][perm].T, i[pre + "W_qr"][h][part].T, i[pre + "W_kr"][h].T,
                         i[pre + "w_kc_q"][h][:, perm]]))
                    w1, w2, w3, w4 = p.ap[0:64, 0:384], p.ap[0:64, 384:768], p.ap[0:64, 768:896], p.ap[:, 896:1280]
                else:
                    p = self.load(384 + 128 + 384, lambda i, h=h: pad_rows(
                        [i[pre + "W_qr"][h].T, i[pre + "W_kr"][h].T,
                         i[pre + "w_kc_q"][h].T.reshape(3, 128, 128).transpose(1, 0, 2).reshape(128, 384)]))
                    w1, w3, w4 = p.ap[0:64, 0:384], p.ap[0:64, 384:512], p.ap[:, 512:896]
                    w2 = None
                pq = PQ[:, h % 2, :].rearrange("p (s j d) -> p s j d", s=2, j=3)
                for s, w in enumerate((w1, w2)):
                    if w is None:
                        continue
                    k = self.bank()
                    ps = self.P[k][:, 0:384].rearrange("p (j d) -> p j d", j=3)
                    for j in range(3):
                        t = self.mm(ps[:, j, :], w[:, 128 * j:128 * j + 128], w3, True, True, p.tok, inc=j == 2)
                    tp = self.copy(self.act, pq[:, s, :, :], ps, t)
                    self.free[k] = tp
                qh = QH[:, h % 2, :]
                tq = [None, None]
                for hf in range(2):
                    hs = self.hs(hf)
                    k = self.bank()
                    t = self.chain(self.P[k][:, 0:H2], [(wqt[:, hh, c, :], x[:, c, hs]) for c in range(4)], self.xt[hf], wq.tok)
                    tq[hf] = self.copy(self.act, qh[:, hs], self.P[k][:, 0:H2], t)
                    self.free[k] = tq[hf]
                if not roped:
                    k = self.bank()
                    w4j = w4.rearrange("p (j c) -> p j c", j=3)
                    t = self.chain(self.P[k][:, 0:128], [(w4j[:, j, :], pq[:, 0, j, :]) for j in range(3)], tp)
                    tm_ = self.copy(self.dve, MH[:, h % 2, :], self.P[k][:, 0:128], t)
                    self.free[k] = tm_
                    for hf in range(2):
                        hs = self.hs(hf)
                        k = self.bank()
                        t = self.mm(self.P[k][:, 0:H2], MH[:, h % 2, :], qh[:, hs], True, True, tm_, tq[hf], inc=True)
                        qt[hh, hf] = self.copy(self.dve, QE[:, hh, hs], self.P[k][:, 0:H2], t)
                        self.free[k] = qt[hh, hf]
                else:
                    w4j = w4.rearrange("p (j c) -> p j c", j=3)
                    for hf in range(2):
                        hs = self.hs(hf)
                        qb = QB[:, hf, :].rearrange("p (s j t) -> p s j t", s=2, j=3)
                        tb = None
                        for j in range(3):
                            k = self.bank()
                            t = self.mm(self.P[k][:, 0:H2], w4j[:, j, :], qh[:, hs], True, True, tq[hf], inc=True)
                            p4 = self.P[k][:, 0:H2].rearrange("p (b s) -> p b s", b=4)
                            for s, tab in enumerate(("cosq", "sinq")):
                                tb = self.tt(qb[:, s, j, :].rearrange("p (b s) -> p b s", b=4), p4,
                                             bc(self.c[tab][:, S * j:S * j + S], [128, 4, S]), ALU.mult, t,
                                             qt.get((hh - 1, hf)))
                            self.free[k] = tb
                        k = self.bank()
                        t = self.chain(self.P[k][:, 0:H2], [(pq[:, s, j, :], qb[:, s, j, :]) for s in range(2) for j in range(3)],
                                       tb, tp)
                        qt[hh, hf] = self.copy(self.act, QE[:, hh, hs], self.P[k][:, 0:H2], t)
                        self.free[k] = qt[hh, hf]
                p.rel = self.pe.now()
            wq.rel = self.pe.now()
            self.barrier()
            st = {}

            def scores(b):
                pm = Pm[:, b % 2, :].rearrange("p (a l) -> p a l", a=4)
                m = sm[:, 64 * (b % 2):64 * (b % 2) + 64]
                for hh in range(4):
                    k = self.bank()
                    t = self.mm(self.P[k][0:S, 0:L], QE[:, hh, S * b:S * b + S], kf[:, b, :], True, True, inc=True)
                    t = self.red(m[0:S, hh:hh + 1], self.P[k][0:S, 0:L], ALU.max, t, st.get(("pt", b - 2)), negate=True)
                    t = self.af(pm[0:S, hh, :], self.P[k][0:S, 0:L], ACT.Exp, t, st.get(("pt", b - 2)),
                                bias=m[0:S, hh:hh + 1], accum_out=m[0:S, 4 + hh:5 + hh])
                    self.free[k] = t
                t = self.rec(m[0:S, 8:12], m[0:S, 4:8], t)
                t = self.tt(pm[0:S, :, :], pm[0:S, :, :], bc(m[0:S, 8:12], [S, 4, L], 2), ALU.mult, t)
                st["p", b] = t

            def turn(b):
                pm = Pm[:, b % 2, :].rearrange("p (a l) -> p a l", a=4)
                pt = PT[:, b % 2, :].rearrange("p (j c) -> p j c", j=3)
                for j in range(3):
                    n = min(128, L - 128 * j)
                    k = self.bank()
                    for hh in range(4):
                        t = self.tr(self.P[k][0:n, S * hh:S * hh + S], pm[0:S, hh, 128 * j:128 * j + n], S, st["p", b], inc=hh == 3)
                    st["pt", b] = t
                    t = self.copy(self.act if j == 1 else self.dve, pt[0:n, j, :], self.P[k][0:n, 0:H2], t, st.get(("pv", b - 2)))
                    self.free[k] = t
                    st["c", b, j] = t

            def values(b):
                pt = PT[:, b % 2, :].rearrange("p (j c) -> p j c", j=3)
                k = self.bank()
                for j in range(3):
                    n = min(128, L - 128 * j)
                    t = self.mm(self.P[k][:, 0:H2], kt[0:n, b, j, :], pt[0:n, j, :], j == 0, j == 2, st["c", b, j], inc=j == 2)
                st["pv", b] = t
                t = self.copy(self.act, CT[:, :, S * b:S * b + S], self.P[k][:, 0:H2].rearrange("p (a s) -> p a s", a=4), t)
                self.free[k] = t
                ctt[b // 4] = t
            ctt = [None, None]
            pipeline(NB, scores, turn, values)
            wl = self.load(512, lambda i, hg=hg: i[pre + "w_kc_kv"][4 * hg:4 * hg + 4].transpose(2, 0, 1).reshape(128, 512))
            clt = [None, None]
            for hh in range(4):
                for hf in range(2):
                    k = self.bank()
                    t = self.mm(self.P[k][:, 0:H2], wl.ap[:, 128 * hh:128 * hh + 128], CT[:, hh, self.hs(hf)], True, True,
                                wl.tok, ctt[hf], inc=True)
                    clt[hf] = self.copy(self.dve, CL[:, hh, self.hs(hf)], self.P[k][:, 0:H2], t)
                    self.free[k] = clt[hf]
            wl.rel = self.pe.now()
            wo = self.load(2048, lambda i, hg=hg: fm(i[pre + "Wo"][:, 512 * hg:512 * hg + 512]))
            wot = wo.ap.rearrange("p (m k c) -> p m k c", m=4, k=4)
            base = x if hg == 0 else Z

            def evac(m, h, ps, t):
                zt[h] = self.tt(Z[:, m, self.hs(h)], ps, base[:, m, self.hs(h)], ALU.add, t)
                return zt[h]
            wo.rel = self.project(lambda m, k: wot[:, m, k, :], lambda k, h: CL[:, k, self.hs(h)], clt, 4, range(4), evac, wo.tok)
        self.barrier()
        self.layernorm(Z, self.ar(3200, 4, T), self.ar(6400, T), zt)

    def l0_ffn(self):
        self.barrier()
        x = self.x
        B1, B2 = self.ar(0, 16, 512), self.ar(8192, 16, 512)
        H = self.ar(8192, 16, T)
        XH = self.ar(20992, 4, T)
        had, nhad = self.c["had"], self.c["nhad"]
        bt = []
        for g in range(4):
            p = self.load(2048, lambda i, g=g: tm(i["L0_ffn_W_down"][:, 512 * g:512 * g + 512]))
            w = p.ap.rearrange("p (k c) -> p k c", k=4)
            for k in range(4):
                b = self.bank()
                t = self.mm(self.P[b][:, :], had, w[:, k, :], True, True, p.tok, inc=True)
                t = self.copy(self.act if k % 2 else self.dve, B1[:, 4 * g + k, :], self.P[b][:, :], t)
                self.free[b] = t
                bt.append(t)
            p.rel = self.pe.now()
        src, dst = B1, B2
        t = bt[-2:]
        for lev in range(4):
            s = 1 << lev
            for base in range(0, 16, 2 * s):
                a, b_ = src[:, base:base + s, :], src[:, base + s:base + 2 * s, :]
                self.tt(dst[:, base:base + s, :], a, b_, ALU.add, t)
                t1 = self.tt(dst[:, base + s:base + 2 * s, :], a, b_, ALU.subtract)
            t = t1
            src, dst = dst, src
        wdt = t
        XS = self.ar(16384, 4, T)
        xs = [None, None]
        for c in range(4):
            for h in range(2):
                xs[h] = self.ts(XS[:, c, self.hs(h)], x[:, c, self.hs(h)], self.c["su"][:, c:c + 1], None, ALU.mult, None, self.xt[h])
        h4 = hadamard(4)
        xh = [None, None]
        r512 = float(np.float32(1.0) / np.sqrt(np.float32(512)))

        def evac(m, h, ps, t):
            xh[h] = self.af(XH[:, m, self.hs(h)], ps, ACT.Copy, t, scale=r512)
            return xh[h]
        self.project(lambda m, k: had if h4[m, k] > 0 else nhad, lambda k, h: XS[:, k, self.hs(h)], xs, 4, range(4), evac)
        sm = self.small
        ws = self.ts(sm[:, 0:16], self.c["wsu"], 1.0, None, ALU.mult, None)
        ws = self.tt(sm[:, 0:16], sm[:, 0:16], self.c["sud"], ALU.mult, ws)
        wd = self.ts(sm[:, 16:20], self.c["wsd"], float(np.float32(1.0) / np.sqrt(np.float32(2048))), None, ALU.mult, None)
        self.barrier()
        G = sm[:, 32:832].rearrange("p (a t) -> p a t", a=2)
        ht, gfree, n = [None, None], [None, None], 0
        for g in range(8):
            p = self.load(2048, lambda i, g=g: np.concatenate(
                [fm(i["L0_ffn_W_up"][256 * g:256 * g + 256]), fm(i["L0_ffn_W_gate"][256 * g:256 * g + 256])], 1))
            w = p.ap.rearrange("p (m k c) -> p m k c", m=4, k=4)
            for m in range(2):
                f = 2 * g + m
                for h in range(2):
                    hs = self.hs(h)
                    bu, bg = self.bank(), self.bank()
                    tu = self.chain(self.P[bu][:, 0:H2], [(w[:, m, k, :], XH[:, k, hs]) for k in range(4)], xh[h], p.tok)
                    tg = self.chain(self.P[bg][:, 0:H2], [(w[:, 2 + m, k, :], XH[:, k, hs]) for k in range(4)])
                    t = self.af(G[:, n % 2, :], self.P[bg][:, 0:H2], ACT.Silu, tg, gfree[n % 2], scale=self.c["wsg"][:, f:f + 1])
                    self.free[bg] = t
                    t = self.stt(H[:, f, hs], self.P[bu][:, 0:H2], sm[:, f:f + 1], G[:, n % 2, :], ALU.mult, ALU.mult, tu, t, ws)
                    self.free[bu] = gfree[n % 2] = ht[h] = t
                    n += 1
            p.rel = self.pe.now()
        self.dve.wait(self.pe.now())
        Z, zt = XH, [None, None]

        def evacz(m, h, ps, t):
            zt[h] = self.stt(Z[:, m, self.hs(h)], ps, sm[:, 16 + m:17 + m], x[:, m, self.hs(h)], ALU.mult, ALU.add, t, wd)
            return zt[h]
        self.project(lambda m, k: B1[:, k, 128 * m:128 * m + 128], lambda k, h: H[:, k, self.hs(h)],
                     [[ht[0], wdt], [ht[1], wdt]], 16, range(4), evacz)
        self.act.wait(self.pe.now())
        self.dve.wait(self.pe.now())
        self.layernorm(Z, self.ar(8192, 4, T), self.ar(12000, T), zt)

    def router(self, w, n, bias, sm, width):
        t = None
        for b in range(NB):
            k = self.bank()
            t = self.chain(self.P[k][0:S, 0:n], [(self.x[:, c, S * b:S * b + S], w[:, c, :]) for c in range(4)], self.xt[b // 4])
            if bias is None:
                t = self.copy(self.dve, sm[0:S, b, 0:n], self.P[k][0:S, 0:n], t)
            else:
                t = self.tt(sm[0:S, b, 0:n], self.P[k][0:S, 0:n], bias[0:S, :], ALU.add, t)
            self.free[k] = t
        return t

    def top(self, vals, b, n, mx, ix, ixf, *toks):
        v, m, i, f = vals[0:S, b, 0:n], mx[0:S, b, :], ix[0:S, b, :], ixf[0:S, b, :]
        t = self.dve.do(lambda e: e.max(m, v), *toks)
        t = self.dve.do(lambda e: e.max_index(i, m, v), t)
        return self.dve.do(lambda e: e.tensor_copy(f, i), t)

    def experts(self, ne, nf, load_gu, load_d, gate, at):
        x = self.x
        ACC = self.ar(at, NB, 512)
        G = self.ar(at + 4096, 2, nf * T)
        HI = self.ar(at + 4096 + 2 * nf * T, 2, nf * T)
        st = {}

        def up(e):
            p = load_gu(e)
            w = p.ap.rearrange("p (m k c) -> p m k c", m=2 * nf, k=4) if nf == 2 else \
                p.ap[:, 0:1024].rearrange("p (m k c) -> p m k c", m=2, k=4)
            g, hi = (a[:, e % 2, :].rearrange("p (f t) -> p f t", f=nf) for a in (G, HI))
            for f in range(nf):
                for h in range(2):
                    hs = self.hs(h)
                    bg, bu = self.bank(), self.bank()
                    tg = self.chain(self.P[bg][:, 0:H2], [(w[:, f, k, :], x[:, k, hs]) for k in range(4)], p.tok)
                    tu = self.chain(self.P[bu][:, 0:H2], [(w[:, nf + f, k, :], x[:, k, hs]) for k in range(4)])
                    t = self.af(g[:, f, hs], self.P[bg][:, 0:H2], ACT.Silu, tg, st.get(("h", e - 2)))
                    self.free[bg] = t
                    t = self.tt(hi[:, f, hs], self.P[bu][:, 0:H2], g[:, f, hs], ALU.mult, tu, t, st.get(("d", e - 2)))
                    self.free[bu] = t
            st["h", e] = t
            if nf == 2:
                p.rel = self.pe.now()
            else:
                st["p", e] = p

        def down(e):
            hi = HI[:, e % 2, :].rearrange("p (f t) -> p f t", f=nf)
            if nf == 2:
                p = load_d(e)
                w = p.ap.rearrange("p (f n) -> p f n", f=2)
                wt = p.tok
            else:
                p = st["p", e]
                w = p.ap[:, 1024:1536].rearrange("p (f n) -> p f n", f=1)
                wt = None
            for b in range(NB):
                k = self.bank()
                t = self.chain(self.P[k][0:S, :], [(hi[:, f, S * b:S * b + S], w[:, f, :]) for f in range(nf)], st["h", e], wt)
                st["d", e] = t
                a = ACC[0:S, b, :]
                if e == 0:
                    t = self.ts(a, self.P[k][0:S, :], gate(b, e), None, ALU.mult, None, t)
                else:
                    t = self.stt(a, self.P[k][0:S, :], gate(b, e), a, ALU.mult, ALU.add, t, st["acc", b])
                st["acc", b] = t
                self.free[k] = t
            p.rel = self.pe.now()
        pipeline(ne, up, down)
        Z, zt = self.ar(at + 4096, 4, T), [None, None]
        self.dve.wait(self.pe.now())
        for b in range(NB):
            k = self.bank()
            ps = self.P[k][:, 0:4 * S].rearrange("p (c s) -> p c s", c=4)
            for c in range(4):
                t = self.tr(ps[:, c, :], ACC[0:S, b, 128 * c:128 * c + 128], S, st["acc", b], inc=c == 3)
            sl = slice(S * b, S * b + S)
            zt[b // 4] = self.tt(Z[:, :, sl], ps, x[:, :, sl], ALU.add, t)
            self.free[k] = zt[b // 4]
        self.barrier()
        self.layernorm(Z, self.ar(0, 4, T), self.ar(3200, T), zt)

    def l1_ffn(self):
        self.barrier()
        pre = "L1_ffn_"
        E = 16
        SC, CB, OH = self.ar(0, NB, E), self.ar(128, NB, E + 1), self.ar(300, NB, E)
        BI = self.ar(500, NB, E)
        MX, IX, IF = self.ar(700, NB, 8), self.ar(800, NB, 8).bitcast(U32), self.ar(900, NB, 8)
        SS = self.ar(1000, NB)
        w = self.c["g1w"].rearrange("p (k e) -> p k e", k=4)
        t = self.router(w, E, None, SC, E)
        t = self.af(SC[0:S], SC[0:S], ACT.Sigmoid, t)
        t = self.tt(BI[0:S], SC[0:S], bc(self.c["g1b"][0:S, :], [S, NB, E]), ALU.add, t)
        for b in range(NB):
            t = self.top(BI, b, E, MX, IX, IF, t)
        iota = bc(self.c["iota"][0:S, 0:E], [S, NB, E])
        t = self.tt(CB[0:S, :, 0:E], iota, IF[0:S, :, 0:1].to_broadcast([S, NB, E]), ALU.is_equal, t)
        t = self.tt(OH[0:S], iota, IF[0:S, :, 1:2].to_broadcast([S, NB, E]), ALU.is_equal, t)
        t = self.tt(CB[0:S, :, 0:E], CB[0:S, :, 0:E], OH[0:S], ALU.add, t)
        t = self.tt(CB[0:S, :, 0:E], CB[0:S, :, 0:E], SC[0:S], ALU.mult, t)
        t = self.red(SS[0:S], CB[0:S, :, 0:E], ALU.add, t)
        t = self.ts(SS[0:S], SS[0:S], 1e-20, None, ALU.add, None, t)
        t = self.rec(SS[0:S], SS[0:S], t)
        t = self.tt(CB[0:S, :, 0:E], CB[0:S, :, 0:E], bc(SS[0:S], [S, NB, E], 2), ALU.mult, t)
        t = self.dve.do(lambda e: e.memset(CB[0:S, :, E:E + 1], 1.0), t)

        def gu(e):
            if e == E:
                return self.load(2048, lambda i: np.concatenate([fm(i[pre + "shared_gate_w"].T), fm(i[pre + "shared_up_w"].T)], 1))
            return self.load(2048, lambda i: fm(i[pre + "experts_gate_up"][e].T))

        def dn(e):
            if e == E:
                return self.load(1024, lambda i: tm(i[pre + "shared_down_w"].T))
            return self.load(1024, lambda i: tm(i[pre + "experts_down"][e].T))
        self.dve.wait(t)
        self.pe.wait(*self.xt)
        self.experts(E + 1, 2, gu, dn, lambda b, e: CB[0:S, b, e:e + 1], 4400)

    def l3_ffn(self):
        self.barrier()
        pre = "L3_ffn_"
        E = 64
        LG, CB, WK = self.ar(0, NB, E + 1), self.ar(600, NB, E + 1), self.ar(1200, NB, E)
        MX, NM, SS = self.ar(1800, NB, 8), self.ar(1900, NB), self.ar(1950, NB)
        w = self.c["g3w"].rearrange("p (k e) -> p k e", k=4)
        t = self.router(w, E + 1, None, LG, E + 1)
        tl = t
        for b in range(NB):
            lg = LG[0:S, b, 0:E]
            t = self.dve.do(lambda e, b=b, lg=lg: e.max(MX[0:S, b, :], lg), t)
            t = self.dve.do(lambda e, b=b, lg=lg: e.match_replace(WK[0:S, b, :], MX[0:S, b, :], lg, -3.0e38), t)
        cb = CB[0:S, :, 0:E]
        t = self.tt(cb, WK[0:S], LG[0:S, :, 0:E], ALU.not_equal, t)
        t = self.tt(WK[0:S], LG[0:S, :, 0:E], bc(MX[0:S, :, 0], [S, NB, E], 2), ALU.subtract, t)
        t = self.af(WK[0:S], WK[0:S], ACT.Exp, t)
        t = self.tt(cb, cb, WK[0:S], ALU.mult, t)
        t = self.red(SS[0:S], cb, ALU.add, t)
        t = self.rec(SS[0:S], SS[0:S], t)
        t = self.tt(cb, cb, bc(SS[0:S], [S, NB, E], 2), ALU.mult, t)
        t2 = self.af(CB[0:S, :, E:E + 1], LG[0:S, :, E:E + 1], ACT.Sigmoid, tl)

        def gu(e):
            if e == E:
                return self.load(1536, lambda i: np.concatenate(
                    [fm(i[pre + "sh_gate_w"]), fm(i[pre + "sh_up_w"]), i[pre + "sh_down_w"].T], 1))
            return self.load(1536, lambda i: np.concatenate([fm(i[pre + "gu_w"][e]), i[pre + "dp_w"][e].T], 1))
        self.dve.wait(t, t2)
        self.pe.wait(*self.xt)
        self.experts(E + 1, 1, gu, None, lambda b, e: CB[0:S, b, e:e + 1], 4400)

    def l2_ffn(self):
        self.barrier()
        E = 8
        LG, PR, OH = self.ar(0, NB, E), self.ar(64, NB, E), self.ar(128, NB, E)
        MX, IX, IF = self.ar(192, NB, 8), self.ar(256, NB, 8).bitcast(U32), self.ar(320, NB, 8)
        NM, SS = self.ar(384, NB), self.ar(392, NB)
        GT = self.ar(400, T)
        GB = self.ar(1200, 4, T)
        Hh = self.ar(4400, 4, T)
        w = self.c["wr"].rearrange("p (k e) -> p k e", k=4)
        t = self.router(w, E, self.c["br"], LG, E)
        t = self.red(NM[0:S], LG[0:S], ALU.max, t)
        t = self.tt(LG[0:S], LG[0:S], bc(NM[0:S], [S, NB, E], 2), ALU.subtract, t)
        t = self.af(PR[0:S], LG[0:S], ACT.Exp, t)
        t = self.red(SS[0:S], PR[0:S], ALU.add, t)
        t = self.rec(SS[0:S], SS[0:S], t)
        t = self.tt(PR[0:S], PR[0:S], bc(SS[0:S], [S, NB, E], 2), ALU.mult, t)
        for b in range(NB):
            t = self.top(PR, b, E, MX, IX, IF, t)
        t = self.tt(OH[0:S], bc(self.c["iota"][0:S, 0:E], [S, NB, E]), IF[0:S, :, 0:1].to_broadcast([S, NB, E]), ALU.is_equal, t)
        t = self.tt(OH[0:S], OH[0:S], MX[0:S, :, 0:1].to_broadcast([S, NB, E]), ALU.mult, t)
        t = self.ts(OH[0:S], OH[0:S], 1.0 / 64, None, ALU.mult, None, t)
        gt = [None, None]
        for b in range(NB):
            k = self.bank()
            t1 = self.tr(self.P[k][0:E, 0:S], OH[0:S, b, :], S, t, inc=True)
            gt[b // 4] = self.copy(self.act, GT[0:E, S * b:S * b + S], self.P[k][0:E, 0:S], t1)
            self.free[k] = gt[b // 4]
        gb = {}
        sel = self.c["sel8"].rearrange("p (k c) -> p k c", k=4)
        for m in range(4):
            for h in range(2):
                k = self.bank()
                t1 = self.mm(self.P[k][:, 0:H2], sel[0:E, m, :], GT[0:E, self.hs(h)], True, True, gt[h], inc=True)
                gb[m, h] = self.copy(self.act, GB[:, m, self.hs(h)], self.P[k][:, 0:H2], t1)
                self.free[k] = gb[m, h]
        ht = [None, None]

        def evac(m, h, ps, t):
            ht[h] = self.tt(Hh[:, m, self.hs(h)], ps, GB[:, m, self.hs(h)], ALU.mult, t, gb[m, h])
            return ht[h]
        self.full("L2_ffn_A", lambda a: a.reshape(512, 512), self.x, self.xt, evac)
        Z, zt = self.ar(7600, 4, T), [None, None]
        self.full("L2_ffn_B", lambda a: a.transpose(1, 0, 2).reshape(512, 512), Hh, ht, self.add_residual(Z, zt))
        self.layernorm(Z, self.ar(10800, 4, T), self.ar(14000, T), zt)

    def layer(self, n):
        [self.l0_attn, lambda: self.xattn("L0_xattn_"), self.l0_ffn, self.l1_attn, lambda: self.mla("L1_xattn_", False),
         self.l1_ffn, self.l2_attn, lambda: self.mla("L2_xattn_", True), self.l2_ffn, self.l3_attn,
         lambda: self.xattn("L3_xattn_"), self.l3_ffn][n]()


def pad_rows(parts):
    out = []
    for a in parts:
        b = np.zeros((128, a.shape[1]), np.float32)
        b[:a.shape[0]] = a
        out.append(b)
    return np.concatenate(out, 1)


def build(nc, layers=range(12)):
    from contextlib import ExitStack
    with ExitStack() as stack:
        k = K(nc, stack, layers)
        k.act.wait(k.ic)
        k.dve.wait(k.ic)
        k.prep()
        for n in layers:
            k.layer(n)
        total = sum(128 * p.n for p in k.loads)
        wd = nc.dram_tensor("weights", [total], F32, kind="ExternalInput").ap()
        cd = nc.dram_tensor("constants", [128, k.cw], F32, kind="ExternalInput").ap()
        xd = nc.dram_tensor("xt", [128, 4 * T], F32, kind="ExternalInput").ap()
        kd = nc.dram_tensor("ctx", [128, NB * L], F32, kind="ExternalInput").ap()
        od = nc.dram_tensor("out", [128, 4 * T], F32, kind="ExternalOutput").ap()
        block = stack.enter_context(nc.Block())

        @block.sync
        def _(e):
            e.dma_start(k.C[:, :], cd).then_inc(k.s_in[0], 16)
            e.dma_start(k.A[:, 0:NB * L], kd).then_inc(k.s_in[3], 16)
            e.dma_start(k.X[:, :], xd).then_inc(k.s_in[1], 16)
            e.dma_start(k.CX[:, :].rearrange("p (b s) -> p b s", b=NB),
                        kd.rearrange("p (b l) -> p b l", b=NB)[:, :, 0:S]).then_inc(k.s_in[2], 16)
            at = 0
            sp = Eng("sp", None)
            for i, p in enumerate(k.loads):
                if i >= RING:
                    sp.wait(k.loads[i - RING].rel)
                src = wd[at:at + 128 * p.n].rearrange("(p n) -> p n", n=p.n)
                at += 128 * p.n
                sem = p.tok.sem
                sp.q.append((None, lambda e, p=p, src=src, sem=sem: e.dma_start(p.ap, src).then_inc(sem, 16), False))
            sp.flush(e)
            for t in k.xt:
                e.wait_ge(t.sem, t.val)
            e.dma_start(od, k.X[:, :]).then_inc(k.s_out, 16)
            e.wait_ge(k.s_out, 16)

        @block.tensor
        def _(e):
            k.pe.flush(e)

        @block.scalar
        def _(e):
            k.act.flush(e)

        @block.vector
        def _(e):
            k.dve.flush(e)
    return k


def pack(k, inputs):
    x = np.asarray(inputs["x"])
    xt = x.reshape(T, 4, 128).transpose(2, 1, 0).reshape(128, 4 * T)
    cx = np.asarray(inputs["ctx_512"]).transpose(2, 0, 1).reshape(128, NB * L)
    cc = np.concatenate([v for v in k.consts.values()] + [f(inputs) for _, f in PARAMS.values()], 1)
    parts = [np.ascontiguousarray(p.pack(inputs)) for p in k.loads]
    for p, a in zip(k.loads, parts):
        assert a.shape == (128, p.n), (a.shape, p.n)
    ws = np.concatenate([a.reshape(-1) for a in parts])
    return {"xt": np.ascontiguousarray(xt), "ctx": np.ascontiguousarray(cx), "constants": np.ascontiguousarray(cc),
            "weights": ws}


def kernel(**inputs):
    import numpy as _np
    import concourse.bacc as _bacc
    from concourse.bass_utils import run_bass_kernel_spmd as _run

    nc = _bacc.Bacc("TRN2", target_bir_lowering=False, num_devices=1)
    k = build(nc)
    r = _run(nc, [pack(k, inputs)], core_ids=[0])
    o = r.results[0]["out"]
    return _np.ascontiguousarray(o.reshape(128, 4, NB, S).transpose(2, 3, 1, 0).reshape(NB, S, 512))
```

```python
import numpy as np
import concourse.bass as bass
from concourse import mybir

ALU = mybir.AluOpType
ACT = mybir.ActivationFunctionType
F32 = mybir.dt.float32
U32 = mybir.dt.uint32
AX = mybir.AxisListType

NB, S, L, T, H2 = 8, 100, 361, 800, 400
SLOT, RING = 2048, 6
ARENA = 25600
NEG = -1.0e30



def fm(w):
    o, i = w.shape
    m = min(128, o)
    return w.reshape(o // m, m, i // 128, 128).transpose(3, 0, 2, 1).reshape(128, -1)


def tm(w):
    o, i = w.shape
    return w.T.reshape(i // 128, 128, o).transpose(1, 0, 2).reshape(128, -1)


def col(v):
    return v.reshape(-1, 128).T


def rows(v):
    return np.broadcast_to(v.reshape(1, -1), (128, v.size))


def hadamard(n):
    h = np.ones((1, 1), np.float32)
    while h.shape[0] < n:
        h = np.block([[h, h], [h, -h]])
    return h.astype(np.float32)


def swap_matrix(width):
    m = np.zeros((128, 128), np.float32)
    for p in range(128):
        m[p - p % width + (p % width + width // 2) % width, p] = 1.0
    return m


def rope32(pos, div):
    half = 16
    if div:
        inv = (np.float32(1.0) / np.float32(10000.0) ** (np.arange(0, 32, 2, dtype=np.float32) / np.float32(32))).astype(np.float32)
    else:
        inv = (np.float32(10000.0) ** (-np.arange(half, dtype=np.float32) / np.float32(half))).astype(np.float32)
    ang = (np.asarray(pos, np.float32)[None, :] * inv[:, None]).astype(np.float32)
    c, s = np.cos(ang), np.sin(ang)
    c = np.tile(np.concatenate([c, c], 0), (4, 1))
    s = np.tile(np.concatenate([-s, s], 0), (4, 1))
    return c.astype(np.float32), s.astype(np.float32)


def rope_mla(n, dim):
    inv = (np.float32(1.0) / np.float32(10000.0) ** (np.arange(0, dim, 2, dtype=np.float32) / np.float32(dim))).astype(np.float32)
    f = (np.arange(n, dtype=np.float32)[:, None] * inv[None, :]).astype(np.float32)
    return np.repeat(np.cos(f), 2, -1).T.astype(np.float32), np.repeat(np.sin(f), 2, -1).T.astype(np.float32)


def shape_constants():
    c = {}
    c["ident"] = np.eye(128, dtype=np.float32)
    c["mean"] = np.full((128, 128), 1.0 / 512, np.float32)
    c["had"] = hadamard(128)
    c["nhad"] = -hadamard(128)
    c["swap32"] = swap_matrix(32)
    c["swap128"] = swap_matrix(128)
    c["cos1"], c["sin1"] = rope32(range(S), False)
    c["cos3"], c["sin3"] = rope32(range(S), True)
    co, si = rope_mla(L, 128)
    sg = np.where(np.arange(128) < 64, -1.0, 1.0).astype(np.float32)[:, None]
    c["cosk"], c["sink"] = co, si * sg
    co, si = rope_mla(S, 384)
    perm = q384()
    partner = (np.arange(384) + 192) % 384
    sign = np.where(partner < 192, -1.0, 1.0).astype(np.float32)[:, None]
    c["cosq"] = co[perm].reshape(3, 128, S).transpose(1, 0, 2).reshape(128, -1)
    c["sinq"] = (si[partner] * sign)[perm].reshape(3, 128, S).transpose(1, 0, 2).reshape(128, -1)
    cm = np.zeros((128, S), np.float32)
    cm[:S] = np.where(np.arange(S)[:, None] >= np.arange(S)[None, :], 0.0, NEG)
    c["causal"] = cm
    e = np.zeros((128, S), np.float32)
    e[S - 1] = 1.0
    c["lastrow"] = e
    c["iota"] = rows(np.arange(64, dtype=np.float32))
    sel = np.zeros((128, 4, 128), np.float32)
    for k in range(4):
        for p in range(128):
            sel[2 * k + p // 64, k, p] = 1.0
    c["sel8"] = sel.reshape(128, -1)
    m = np.ones((128, H2), np.float32)
    m[:, ::S] = 0.0
    c["restart"] = m
    c["tri"] = np.zeros((128, 64), np.float32)
    c["tri"][:64] = np.triu(np.ones((64, 64), np.float32), 1)
    c["thr"] = rows(128.0 * np.arange(7, dtype=np.float32))
    c["tiles"] = rows(np.arange(113, dtype=np.float32))
    c["lane"] = np.arange(128, dtype=np.float32)[:, None]
    c["token"] = np.arange(128, dtype=np.float32)[:, None] + 100 * np.arange(8, dtype=np.float32)[None, :]
    c["eps"] = rows(np.array([1.1920929e-07, 1e-05, 0.0, 1.0], np.float32))
    return c


def q384():
    b = np.arange(384).reshape(6, 64)
    return np.concatenate([np.concatenate([b[t], b[t + 3]]) for t in range(3)])


PARAMS = {
    "su": (4, lambda i: col(i["L0_ffn_SU_ug"])),
    "sud": (16, lambda i: col(i["L0_ffn_SU_dp"])),
    "wsu": (16, lambda i: col(i["L0_ffn_Wscale_ug"][:2048])),
    "wsg": (16, lambda i: col(i["L0_ffn_Wscale_ug"][2048:])),
    "wsd": (4, lambda i: col(i["L0_ffn_Wscale_dp"])),
    "bq": (4, lambda i: col(i["L1_attn_bq"])),
    "bk": (2, lambda i: col(np.tile(i["L1_attn_bk"].reshape(2, 1, 32), (1, 4, 1)).reshape(-1))),
    "bv": (64, lambda i: rows(i["L1_attn_bv"])),
    "g1w": (64, lambda i: tm(i["L1_ffn_gate_w"].T)),
    "g1b": (16, lambda i: rows(i["L1_ffn_expert_bias"])),
    "wr": (32, lambda i: tm(i["L2_ffn_Wr"])),
    "br": (8, lambda i: rows(i["L2_ffn_br"])),
    "bern": (16, lambda i: rows(i["L3_attn_bern_u"])),
    "g3w": (260, lambda i: tm(np.concatenate([i["L3_ffn_gate_w"], i["L3_ffn_sh_gate1_w"]]))),
}



class Tok:

    def __init__(self, sem, val):
        self.sem, self.val = sem, val


class Eng:

    def __init__(self, name, sem):
        self.name, self.sem, self.n, self.q, self.met = name, sem, 0, [], {}

    def wait(self, *toks):
        for t in toks:
            if t is None:
                continue
            if isinstance(t, (list, tuple)):
                self.wait(*t)
                continue
            if self.met.get(id(t.sem), 0) < t.val:
                self.met[id(t.sem)] = t.val
                self.q.append((t, None, False))

    def do(self, fn, *toks, inc=True):
        self.wait(*toks)
        self.q.append((None, fn, inc))
        if inc:
            self.n += 1
            return Tok(self.sem, self.n)

    def now(self):
        return Tok(self.sem, self.n) if self.n else None

    def flush(self, eng):
        for t, fn, inc in self.q:
            if t is not None:
                eng.wait_ge(t.sem, t.val)
            else:
                i = fn(eng)
                if inc:
                    i.then_inc(self.sem, 1)


class Piece:
    def __init__(self, ap, tok, n, pack):
        self.ap, self.tok, self.n, self.pack, self.rel = ap, tok, n, pack, None


def pipeline(n, *stages):
    for t in range(n + len(stages) - 1):
        for s in range(len(stages) - 1, -1, -1):
            if 0 <= t - s < n:
                stages[s](t - s)


def wants(layers, n):
    return (5 if n == 28 else 11) in layers


def bc(ap, shape, axis=1):
    return ap.unsqueeze(axis).to_broadcast(shape)


class K:
    def __init__(self, nc, stack, layers):
        self.nc, self.layers = nc, layers
        en = stack.enter_context
        self.sem = lambda name: en(nc.semaphore(name))
        self.pe, self.act, self.dve, self.pool = (Eng(n, self.sem("s_" + n)) for n in ("pe", "act", "dve", "pool"))
        self.sp = Eng("sp", self.sem("s_sp"))
        sb = lambda name, n: en(nc.sbuf_tensor(name, [128, n], F32))
        self.W = sb("W", RING * SLOT)
        self.wsem = [self.sem(f"s_w{i}") for i in range(RING)]
        self.loads = []
        self.consts = shape_constants()
        self.cw = sum(v.shape[1] for v in self.consts.values()) + sum(n for n, _ in PARAMS.values())
        self.C = sb("C", self.cw)
        self.c, at = {}, 0
        for k, v in self.consts.items():
            self.c[k] = self.C[:, at:at + v.shape[1]]
            at += v.shape[1]
        for k, (n, _) in PARAMS.items():
            self.c[k] = self.C[:, at:at + n]
            at += n
        self.X = sb("X", 4 * T)
        self.x = self.X[:, :].rearrange("p (c t) -> p c t", c=4)
        self.CX = sb("CX", T)
        self.KF = sb("KF", NB * L)
        self.KT = sb("KT", NB * 3 * 128)
        self.A = sb("A", ARENA)
        self.small = sb("small", 832)
        self.P = [en(nc.psum_tensor(f"P{i}", [128, 512], F32)) for i in range(8)]
        self.free = [None] * 8
        self.nb = 0
        self.s_in = [self.sem(f"s_in{i}") for i in range(4)]
        self.s_out = self.sem("s_out")
        self.ic, self.ix, self.ik, self.ik2 = (Tok(s, 16) for s in self.s_in)
        self.xt = [self.ix, self.ix]
        self.gsem = [self.sem(f"s_g{i}") for i in range(16)]
        self.ssem = [self.sem(f"s_s{i}") for i in range(4)]
        self.s_list = [self.sem(f"s_l{i}") for i in range(2)]
        self.ng = self.ns = self.nl = 0
        dram = lambda name, shape, dt, kind: nc.dram_tensor(name, shape, dt, kind=kind).ap()
        self.XD = dram("x_by_token", [T, 512], F32, "Internal")
        self.TD = {n: dram(f"slot_tokens{n}", [128 * n, 1], U32, "Internal") for n in (28, 113) if wants(layers, n)}
        self.YD = {n: dram(f"slot_outputs{n}", [128 * n, 512], F32, "Internal") for n in (28, 113) if wants(layers, n)}
        self.E1 = dram("experts1", [16 * 128, 3072], F32, "ExternalInput")
        self.E3 = dram("experts3", [64 * 128, 1536], F32, "ExternalInput")

    def ar(self, at, *shape):
        n = int(np.prod(shape))
        assert at + n <= ARENA, (at, n)
        v = self.A[:, at:at + n]
        if len(shape) == 2:
            return v.rearrange("p (a b) -> p a b", a=shape[0])
        if len(shape) == 3:
            return v.rearrange("p (a b c) -> p a b c", a=shape[0], b=shape[1])
        return v

    def load(self, n, pack):
        assert n <= SLOT
        i = len(self.loads)
        s = i % RING
        if i >= RING:
            assert self.loads[i - RING].rel is not None, "the ring's slot is not released"
        p = Piece(self.W[:, s * SLOT:s * SLOT + n], Tok(self.wsem[s], 16 * (i // RING + 1)), n, pack)
        self.loads.append(p)
        return p

    def bank(self):
        b = self.nb % 8
        self.nb += 1
        assert self.free[b] != "busy", b
        self.pe.wait(self.free[b])
        self.free[b] = "busy"
        return b

    def barrier(self):
        es = (self.pe, self.act, self.dve, self.pool)
        now = [e.now() for e in es]
        for e in es:
            e.wait(*now)

    def mm(self, out, lhsT, rhs, start, stop, *toks, inc=False):
        return self.pe.do(lambda e: e.matmul(out, lhsT, rhs, start=start, stop=stop), *toks, inc=inc)

    def tr(self, out, in_, n, *toks, inc=False):
        idn = self.c["ident"][0:n, 0:n]
        return self.pe.do(lambda e: e.transpose(out, in_, idn), *toks, inc=inc)

    def chain(self, out, pairs, *toks):
        self.pe.wait(*toks)
        n = len(pairs)
        for i, (a, b) in enumerate(pairs):
            t = self.mm(out, a, b, i == 0, i == n - 1, inc=i == n - 1)
        return t

    def copy(self, eng, out, in_, *toks):
        if eng is self.act:
            return eng.do(lambda e: e.activation(out, in_, ACT.Copy), *toks)
        return eng.do(lambda e: e.tensor_copy(out, in_), *toks)

    def af(self, out, in_, func, *toks, **kw):
        return self.act.do(lambda e: e.activation(out, in_, func, **kw), *toks)

    def tt(self, out, a, b, op, *toks, eng=None):
        return (eng or self.dve).do(lambda e: e.tensor_tensor(out, a, b, op), *toks)

    def ts(self, out, a, s1, s2, o0, o1, *toks, eng=None):
        if o1 is None:
            return (eng or self.dve).do(lambda e: e.tensor_scalar(out, a, s1, None, o0), *toks)
        return (eng or self.dve).do(lambda e: e.tensor_scalar(out, a, s1, s2, o0, o1), *toks)

    def stt(self, out, a, s, b, o0, o1, *toks):
        return self.dve.do(lambda e: e.scalar_tensor_tensor(out=out, in0=a, scalar=s, in1=b, op0=o0, op1=o1), *toks)

    def rec(self, out, a, *toks):
        return self.dve.do(lambda e: e.reciprocal(out, a), *toks)

    def red(self, out, a, op, *toks, negate=None):
        return self.dve.do(lambda e: e.tensor_reduce(out, a, AX.X, op, negate=negate), *toks)

    def hs(self, h):
        return slice(H2 * h, H2 * h + H2)

    def rstd(self, src, sq, r, eps, h, *toks):
        hs = self.hs(h)
        t = self.af(sq[:, :, hs], src[:, :, hs], ACT.Square, *toks)
        b = self.bank()
        t = self.chain(self.P[b][:, 0:H2], [(self.c["mean"], sq[:, c, hs]) for c in range(4)], t, self.ic)
        t = self.af(r[:, hs], self.P[b][:, 0:H2], ACT.Sqrt, t, bias=self.c["eps"][:, eps:eps + 1])
        self.free[b] = t
        return self.rec(r[:, hs], r[:, hs], t)

    def layernorm(self, z, sq, r, zt):
        for h in range(2):
            hs = self.hs(h)
            b = self.bank()
            t = self.chain(self.P[b][:, 0:H2], [(self.c["mean"], z[:, c, hs]) for c in range(4)], zt[h])
            t = self.tt(z[:, :, hs], z[:, :, hs], bc(self.P[b][:, 0:H2], [128, 4, H2]), ALU.subtract, t)
            self.free[b] = t
            t = self.rstd(z, sq, r, 1, h, t)
            self.xt[h] = self.tt(self.x[:, :, hs], z[:, :, hs], bc(r[:, hs], [128, 4, H2]), ALU.mult, t)

    def project(self, w, rhs, rt, kc, ms, evac, wt=None):
        for m in ms:
            for h in range(2):
                b = self.bank()
                t = self.chain(self.P[b][:, 0:H2], [(w(m, k), rhs(k, h)) for k in range(kc)], rt[h], wt)
                self.free[b] = evac(m, h, self.P[b][:, 0:H2], t)
        return self.pe.now()

    def full(self, name, sel, src, rt, evac, nm=4):
        for g in range(0, nm, 4):
            p = self.load(2048, lambda i, g=g: fm(sel(i[name])[g * 128:(g + 4) * 128]))
            w = p.ap.rearrange("p (m k c) -> p m k c", m=4, k=4)
            p.rel = self.project(lambda m, k: w[:, m - g, k, :], lambda k, h: src[:, k, self.hs(h)], rt, 4,
                                 range(g, g + 4), evac, p.tok)

    def add_residual(self, z, zt):
        def evac(m, h, ps, t):
            zt[h] = self.tt(z[:, m, self.hs(h)], ps, self.x[:, m, self.hs(h)], ALU.add, t)
            return zt[h]
        return evac

    def l0_attn(self):
        self.barrier()
        x = self.x
        SQ, R, XN = self.ar(0, 4, T), self.ar(3200, T), self.ar(4000, 4, T)
        Q, Kk, V = self.ar(7200, 4, T), self.ar(10400, 4, T), self.ar(13600, 4, T)
        xn = [None, None]
        for h in range(2):
            hs = self.hs(h)
            t = self.rstd(x, SQ, R, 0, h, self.xt[h])
            xn[h] = self.tt(XN[:, :, hs], x[:, :, hs], bc(R[:, hs], [128, 4, H2]), ALU.mult, t)
        dst = [Q, Kk, V]
        done = {}

        def evac(m, h, ps, t):
            t = self.copy(self.act if m % 2 else self.dve, dst[m // 4][:, m % 4, self.hs(h)], ps, t)
            done.setdefault((m // 4, h), []).append(t)
            return t
        self.full("L0_attn_w_qkv", lambda w: w, XN, xn, evac, 12)
        yt = [None, None]
        self.barrier()
        for h in range(2):
            hs = self.hs(h)
            v3 = lambda a: a[:, :, hs]
            rb = bc(R[:, hs], [128, 4, H2])
            t = self.rstd(Q, SQ, R, 0, h)
            t = self.tt(v3(Q), v3(Q), rb, ALU.mult, t)
            tq = self.af(v3(Q), v3(Q), ACT.Sigmoid, t)
            t = self.rstd(Kk, SQ, R, 0, h, tq)
            t = self.tt(v3(Kk), v3(Kk), rb, ALU.mult, t)
            t = self.af(v3(Kk), v3(Kk), ACT.Exp, t)
            t = self.tt(v3(V), v3(V), v3(Kk), ALU.mult, t)
            for c in range(4):
                for src in (V, Kk):
                    ap = src[:, c, hs]
                    t = self.dve.do(lambda e, ap=ap, o=(SQ if src is V else XN)[:, c, hs]: e.tensor_tensor_scan(
                        o, self.c["restart"], ap, 0.0, ALU.mult, ALU.add), t)
            t = self.ts(v3(XN), v3(XN), 1e-6, None, ALU.add, None, t)
            t = self.rec(v3(XN), v3(XN), t)
            t = self.tt(v3(XN), v3(XN), v3(SQ), ALU.mult, t)
            yt[h] = self.tt(v3(Q), v3(XN), v3(Q), ALU.mult, t, tq)
        H = self.ar(10400, 16, T)
        G = self.ar(23200, 2, H2)
        self.barrier()
        ht = [None, None]
        gfree = [None, None]
        n = 0
        for g in range(8):
            p = self.load(2048, lambda i, g=g: np.concatenate(
                [fm(i["L0_attn_w_swiglu"][256 * g:256 * g + 256]), fm(i["L0_attn_w_swiglu"][2048 + 256 * g:2304 + 256 * g])], 1))
            w = p.ap.rearrange("p (m k c) -> p m k c", m=4, k=4)
            for m in range(2):
                for h in range(2):
                    hs = self.hs(h)
                    bu, bg = self.bank(), self.bank()
                    tu = self.chain(self.P[bu][:, 0:H2], [(w[:, m, k, :], Q[:, k, hs]) for k in range(4)], yt[h], p.tok)
                    tg = self.chain(self.P[bg][:, 0:H2], [(w[:, 2 + m, k, :], Q[:, k, hs]) for k in range(4)])
                    t = self.af(G[:, n % 2, :], self.P[bg][:, 0:H2], ACT.Silu, tg, gfree[n % 2])
                    self.free[bg] = t
                    t = self.tt(H[:, 2 * g + m, hs], self.P[bu][:, 0:H2], G[:, n % 2, :], ALU.mult, tu, t)
                    self.free[bu] = gfree[n % 2] = ht[h] = t
                    n += 1
            p.rel = self.pe.now()
        Z, zt = self.ar(4000, 4, T), [None, None]
        for m in range(4):
            p = self.load(2048, lambda i, m=m: fm(i["L0_attn_w_out"][128 * m:128 * m + 128]))
            w = p.ap.rearrange("p (k c) -> p k c", k=16)

            def evac(m, h, ps, t):
                zt[h] = self.stt(Z[:, m, self.hs(h)], x[:, m, self.hs(h)], 2.0, ps, ALU.mult, ALU.add, t)
                return zt[h]
            p.rel = self.project(lambda m, k: w[:, k, :], lambda k, h: H[:, k, self.hs(h)], ht, 16, [m], evac, p.tok)
        self.layernorm(Z, SQ, R, zt)

    def heads32(self, name, qt, kt, V, vt, nk, mask, at, out, group, special=None):
        scale = float(np.float32(1.0) / np.sqrt(np.float32(32)))
        E = [self.ar(at + 1600 * i, 16, S) for i in range(2)]
        PT = [self.ar(at + 3200 + 1600 * i, 16, S) for i in range(2)]
        O = [self.ar(at + 6400 + 512 * i, 16, 32) for i in range(2)]
        M = [self.small[:, 64 * i:64 * i + 64] for i in range(2)]
        st = {}

        def scores(b):
            e, m = E[b % 2], M[b % 2]
            prev = st.get(("pt", b - 2))
            ks = [self.bank() for _ in range(4)]
            tk = {}
            for g in range(4):
                for j in range(4):
                    q = qt[32 * j:32 * j + 32, g, S * b:S * b + S]
                    tk[j] = self.mm(self.P[ks[j]][0:S, nk * g:nk * g + nk], q, kt(4 * g + j, b), True, True, inc=g == 3)
            for j in range(4):
                o = e[0:S, j:16:4, 0:nk]
                ps = self.P[ks[j]][0:S, 0:4 * nk].rearrange("p (a b) -> p a b", a=4)
                if mask is None:
                    t = self.copy(self.act, o, ps, tk[j], prev)
                else:
                    t = self.tt(o, ps, bc(mask[0:S, 0:nk], [S, 4, nk]), ALU.add, tk[j], prev)
                self.free[ks[j]] = t
            v = e[0:S, :, 0:nk]
            t = self.red(m[0:S, 0:16], v, ALU.max, t)
            t = self.tt(v, v, bc(m[0:S, 0:16], [S, 16, nk], 2), ALU.subtract, t)
            t = self.af(v, v, ACT.Exp, t, scale=scale)
            if special is not None:
                t = special(e, m, t)
            st["e", b] = t

        def turn(b):
            e, pt = E[b % 2], PT[b % 2]
            for g in range(4):
                k = self.bank()
                ps = self.P[k][0:nk, 0:4 * S].rearrange("p (a b) -> p a b", a=4)
                for j in range(4):
                    t = self.tr(ps[:, j, :], e[0:S, 4 * g + j, 0:nk], S, st["e", b], inc=j == 3)
                st["pt", b] = t
                t = self.copy(self.act if g % 2 else self.dve, pt[0:nk, 4 * g:4 * g + 4, :], ps, t, st.get(("pv", b - 2)))
                self.free[k] = t
                st["c", b, g] = t

        def values(b):
            pt, o, m = PT[b % 2], O[b % 2], M[b % 2]
            for half in range(2):
                k = self.bank()
                ps = self.P[k][0:S, 0:264].rearrange("p (a b) -> p a b", a=8)
                for j in range(8):
                    h = 8 * half + j
                    t = self.mm(ps[:, j, :], pt[0:nk, h, :], V[0:nk, b, h // group, :], True, True,
                                st["c", b, h // 4], vt(b), inc=j == 7)
                st["pv", b] = t
                if special is None:
                    r = m[0:S, 16 + 8 * half:24 + 8 * half]
                    t = self.rec(r, ps[:, :, 32], t)
                else:
                    r = m[0:S, 48 + 8 * half:56 + 8 * half]
                t = self.tt(o[0:S, 8 * half:8 * half + 8, :], ps[:, :, 0:32], bc(r, [S, 8, 32], 2), ALU.mult, t,
                            st.get(("ot", b - 2)))
                self.free[k] = t
            st["o", b] = t

        def back(b):
            k = self.bank()
            o = O[b % 2]
            ps = self.P[k][:, 0:4 * S].rearrange("p (a b) -> p a b", a=4)
            for c in range(4):
                t = self.tr(ps[:, c, :], o[0:S, 4 * c:4 * c + 4, :].rearrange("p a b -> p (a b)"), S, st["o", b], inc=c == 3)
            st["ot", b] = t
            t = self.copy(self.act, out[:, :, S * b:S * b + S], ps, t)
            self.free[k] = t
            ot[b // 4] = t
        ot = [None, None]
        pipeline(NB, scores, turn, values, back)
        return ot

    def values_tm(self, V, w, wt, src, heads, rt, bias=None, nk=S):
        ones = self.dve.do(lambda e: e.memset(V[0:nk, :, :, 32], 1.0))
        vt = {}
        for b in range(NB):
            k = self.bank()
            n = heads * 32
            t = self.chain(self.P[k][0:nk, 0:n], [(src(c, b), w(c)) for c in range(4)] if w(1) is not None else
                           [(src(0, b), w(0))], rt[b // 4], wt)
            o = V[0:nk, b, :, 0:32]
            ps = self.P[k][0:nk, 0:n].rearrange("p (a b) -> p a b", b=32)
            if bias is None:
                t = self.copy(self.act if b % 2 else self.dve, o, ps, t)
            else:
                t = self.tt(o, ps, bias[0:nk, :].rearrange("p (a b) -> p a b", b=32), ALU.add, t)
            self.free[k] = t
            vt[b] = [t, ones]
        return lambda b: vt[b]

    def xattn(self, pre):
        self.barrier()
        Q, Kk, V = self.ar(0, 4, T), self.ar(3200, 4, T), self.ar(6400, NB, 16 * 33)
        V = V.rearrange("p b (h d) -> p b h d", h=16)
        cx = self.CX
        p = self.load(1024, lambda i: np.concatenate([fm(i[pre + "Wkv_expand"][:512]), tm(i[pre + "Wkv_expand"][512:])], 1))
        wk = p.ap[:, 0:512].rearrange("p (m c) -> p m c", m=4)
        wv = p.ap[:, 512:1024]
        kd, qd = [], []

        def ek(m, h, ps, t):
            t = self.copy(self.act, Kk[:, m, self.hs(h)], ps, t)
            kd.append(t)
            return t

        def eq(m, h, ps, t):
            t = self.copy(self.dve, Q[:, m, self.hs(h)], ps, t)
            qd.append(t)
            return t
        self.project(lambda m, k: wk[:, m, :], lambda k, h: cx[:, self.hs(h)], [self.ik, self.ik], 1, range(4), ek, p.tok)
        vt = self.values_tm(V, lambda c: wv if c == 0 else None, p.tok, lambda c, b: cx[:, S * b:S * b + S], 16,
                            [self.ik, self.ik])
        p.rel = self.pe.now()
        self.full(pre + "Wq", lambda w: w, self.x, self.xt, eq)
        self.pe.wait(qd[-1], kd[-1])
        OT = self.ar(10624, 4, T)
        kt = lambda h, b: Kk[32 * (h % 4):32 * (h % 4) + 32, h // 4, S * b:S * b + S]
        ot = self.heads32(pre, Q, kt, V, vt, S, self.c["causal"], 13824, OT, 1)
        self.out_proj(pre + "Wout", OT, ot)

    def out_proj(self, name, OT, ot):
        Z, zt = self.ar(0, 4, T), [None, None]
        self.dve.wait(self.pe.now())
        self.full(name, lambda w: w, OT, ot, self.add_residual(Z, zt))
        self.act.wait(self.pe.now())
        self.layernorm(Z, self.ar(3200, 4, T), self.ar(6400, T), zt)

    def rope(self, src, n, cos, sin, tmp, st, width):
        out = []
        for m in range(n):
            for h in range(2):
                hs = self.hs(h)
                b = self.bank()
                t = self.mm(self.P[b][:, 0:H2], self.c[width], src[:, m, hs], True, True, st[m, h], inc=True)
                s4 = src[:, m, hs].rearrange("p (b s) -> p b s", b=4)
                p4 = self.P[b][:, 0:H2].rearrange("p (b s) -> p b s", b=4)
                i = (2 * m + h) % 2
                tm4 = tmp[:, H2 * i:H2 * i + H2].rearrange("p (b s) -> p b s", b=4)
                t1 = self.tt(tm4, p4, bc(sin, [128, 4, S]), ALU.mult, t)
                self.free[b] = t1
                t2 = self.tt(s4, s4, bc(cos, [128, 4, S]), ALU.mult, t)
                t = self.tt(s4, s4, tm4, ALU.add, t1, t2)
                out.append(t)
        return t

    def l1_attn(self):
        self.barrier()
        pre = "L1_attn_"
        Q, Kk, V = self.ar(0, 4, T), self.ar(3200, 2, T), self.ar(6400, NB, 66)
        V = V.rearrange("p b (h d) -> p b h d", h=2)
        p = self.load(1280, lambda i: np.concatenate(
            [fm(np.tile(i[pre + "wk"].reshape(2, 1, 32, 512), (1, 4, 1, 1)).reshape(256, 512)), tm(i[pre + "wv"])], 1))
        wk = p.ap[:, 0:1024].rearrange("p (m k c) -> p m k c", m=2, k=4)
        wv = p.ap[:, 1024:1280].rearrange("p (k c) -> p k c", k=4)
        kd, qd = {}, {}

        def ek(m, h, ps, t):
            kd[m, h] = self.af(Kk[:, m, self.hs(h)], ps, ACT.Identity, t, bias=self.c["bk"][:, m:m + 1])
            return kd[m, h]

        def eq(m, h, ps, t):
            qd[m, h] = self.af(Q[:, m, self.hs(h)], ps, ACT.Identity, t, bias=self.c["bq"][:, m:m + 1])
            return qd[m, h]
        self.project(lambda m, k: wk[:, m, k, :], lambda k, h: self.x[:, k, self.hs(h)], self.xt, 4, range(2), ek, p.tok)
        vt = self.values_tm(V, lambda c: wv[:, c, :], p.tok, lambda c, b: self.x[:, c, S * b:S * b + S], 2,
                            self.xt, bias=self.c["bv"])
        p.rel = self.pe.now()
        self.full(pre + "wq", lambda w: w, self.x, self.xt, eq)
        tmp = self.ar(7000, T)
        self.rope(Kk, 2, self.c["cos1"], self.c["sin1"], tmp, kd, "swap32")
        t = self.rope(Q, 4, self.c["cos1"], self.c["sin1"], tmp, qd, "swap32")
        self.pe.wait(t)
        OT = self.ar(10624, 4, T)
        kt = lambda h, b: Kk[32 * (h % 4):32 * (h % 4) + 32, h // 8, S * b:S * b + S]
        ot = self.heads32(pre, Q, kt, V, vt, S, self.c["causal"], 13824, OT, 8)
        self.out_proj(pre + "wo", OT, ot)

    def l2_attn(self):
        self.barrier()
        pre = "L2_attn_"
        Q, Kk, V = self.ar(0, 4, T), self.ar(3200, 4, T), self.ar(6400, NB, 16 * 33)
        V = V.rearrange("p b (h d) -> p b h d", h=16)
        dst, done = [Q, Kk], []

        def evac(m, h, ps, t):
            t = self.copy(self.act, dst[m // 4][:, m % 4, self.hs(h)], ps, t)
            done.append(t)
            return t
        self.full(pre + "W_qkv", lambda w: w[:1024], self.x, self.xt, evac, 8)
        p = self.load(2048, lambda i: tm(i[pre + "W_qkv"][1024:]))
        wv = p.ap.rearrange("p (k c) -> p k c", k=4)
        vt = self.values_tm(V, lambda c: wv[:, c, :], p.tok, lambda c, b: self.x[:, c, S * b:S * b + S], 16, self.xt)
        p.rel = self.pe.now()
        self.pe.wait(done[-1])
        OT = self.ar(10624, 4, T)
        kt = lambda h, b: Kk[32 * (h % 4):32 * (h % 4) + 32, h // 4, S * b:S * b + S]
        ot = self.heads32(pre, Q, kt, V, vt, S, self.c["causal"], 13824, OT, 1)
        self.out_proj(pre + "W_proj", OT, ot)

    def l3_attn(self):
        self.barrier()
        pre = "L3_attn_"
        SB, NK = 10, 60
        Q, Kk, V = self.ar(0, 4, T), self.ar(3200, 4, T), self.ar(6400, NB, 16 * 33)
        V = V.rearrange("p b (h d) -> p b h d", h=16)
        dst, done = [Q, Kk], {}

        def evac(m, h, ps, t):
            done[m, h] = self.copy(self.act, dst[m // 4][:, m % 4, self.hs(h)], ps, t)
            return done[m, h]
        self.full(pre + "wq", lambda w: w, self.x, self.xt, evac, 4)
        self.full(pre + "wk", lambda w: w, self.x, self.xt, lambda m, h, ps, t: evac(m + 4, h, ps, t), 4)
        XK = self.ar(12544, 4, NB * NK).rearrange("p c (b k) -> p c b k", b=NB)
        xs = self.x.rearrange("p c (b s) -> p c b s", b=NB)
        tx = []
        for c in range(4):
            tx.append(self.copy(self.dve, XK[:, c, :, 0:SB], xs[:, c, :, 0:SB], self.xt))
            tx.append(self.copy(self.dve, XK[:, c, :, SB:NK], xs[:, c, :, 50:S], self.xt))
        p = self.load(2048, lambda i: tm(i[pre + "wv"]))
        wv = p.ap.rearrange("p (k c) -> p k c", k=4)
        vt = self.values_tm(V, lambda c: wv[:, c, :], p.tok, lambda c, b: XK[:, c, b, :], 16, [tx, tx], nk=NK)
        p.rel = self.pe.now()
        tmp = self.ar(14464, T)
        sel = lambda o: {(m, h): done[m + o, h] for m in range(4) for h in range(2)}
        self.rope(Kk, 4, self.c["cos3"], self.c["sin3"], tmp, sel(4), "swap32")
        t = self.rope(Q, 4, self.c["cos3"], self.c["sin3"], tmp, sel(0), "swap32")
        KS = self.ar(10624, 4, NB * NK).rearrange("p c (b k) -> p c b k", b=NB)
        ks = Kk.rearrange("p c (b s) -> p c b s", b=NB)
        for c in range(4):
            self.copy(self.dve, KS[:, c, :, 0:SB], ks[:, c, :, 0:SB], t)
            t2 = self.copy(self.dve, KS[:, c, :, SB:NK], ks[:, c, :, 50:S], t)
        self.pe.wait(t2)
        OT = self.ar(3200, 4, T)
        kt = lambda h, b: KS[32 * (h % 4):32 * (h % 4) + 32, h // 4, b, :]

        def special(e, m, t):
            a, r, u, w = (m[0:S, 16 * i:16 * i + 16] for i in range(4))
            e50 = e[0:S, :, SB]
            t = self.red(a, e[0:S, :, 0:NK], ALU.add, t)
            t = self.rec(w, a, t)
            t = self.red(r, e[0:S, :, SB + 1:NK], ALU.add, t)
            t = self.tt(a, r, w, ALU.mult, t)
            t = self.ts(a, a, 1.0 / 49, 1e-6, ALU.mult, ALU.add, t)
            t = self.rec(a, a, t)
            t = self.tt(a, a, w, ALU.mult, t)
            t = self.tt(a, a, e50, ALU.mult, t)
            t = self.ts(a, a, 0.0, 1.0, ALU.max, ALU.min, t)
            t = self.tt(a, self.c["bern"][0:S, :], a, ALU.is_lt, t)
            k = self.bank()
            t = self.mm(self.P[k][0:S, 0:16], self.c["lastrow"][0:S, :], a, True, True, t, inc=True)
            t = self.stt(u, self.P[k][0:S, 0:16], 1.0 / 50, r, ALU.mult, ALU.mult, t)
            self.free[k] = t
            return self.tt(e50, e50, u, ALU.add, t)
        ot = self.heads32(pre, Q, kt, V, vt, NK, None, 15264, OT, 1, special)
        self.out_proj(pre + "wo", OT, ot)

    def prep(self):
        CF = self.ar(0, NB, L)
        kf = self.KF[:, :].rearrange("p (b l) -> p b l", b=NB)
        kt = self.KT[:, :].rearrange("p (b j d) -> p b j d", b=NB, j=3)
        tmp = self.ar(3200, 2, L)
        self.pe.wait(self.ic)
        last = {}
        for b in range(NB):
            k = self.bank()
            t = self.mm(self.P[k][:, 0:L], self.c["swap128"], CF[:, b, :], True, True, self.ik2, inc=True)
            t1 = self.tt(tmp[:, b % 2, :], self.P[k][:, 0:L], self.c["sink"], ALU.mult, t)
            self.free[k] = t1
            t2 = self.tt(kf[:, b, :], CF[:, b, :], self.c["cosk"], ALU.mult, t)
            t = self.tt(kf[:, b, :], kf[:, b, :], tmp[:, b % 2, :], ALU.add, t1, t2)
            k = self.bank()
            ps = self.P[k][:, 0:384].rearrange("p (j d) -> p j d", j=3)
            for j in range(3):
                n = min(128, L - 128 * j)
                t3 = self.tr(ps[0:n, j, :], kf[:, b, 128 * j:128 * j + n], 128, t, inc=j == 2)
            self.copy(self.act, kt[:, b, 0:2, :], ps[:, 0:2, :], t3)
            self.free[k] = self.copy(self.act, kt[0:L - 256, b, 2, :], ps[0:L - 256, 2, :])

    def mla(self, pre, roped):
        self.barrier()
        kf = self.KF[:, :].rearrange("p (b l) -> p b l", b=NB)
        kt = self.KT[:, :].rearrange("p (b j d) -> p b j d", b=NB, j=3)
        x = self.x
        Z = self.ar(0, 4, T)
        QE = self.ar(3200, 4, T)
        CT = self.ar(6400, 4, T)
        CL = self.ar(9600, 4, T)
        QH = self.ar(12800, 2, T)
        PQ = self.ar(14400, 2, 768)
        MH = self.ar(15936, 2, 128)
        QB = self.ar(16192, 2, 2400)
        Pm = self.ar(16192, 2, 4 * L)
        PT = self.ar(16192 + 8 * L, 2, 3 * H2)
        sm = self.small
        perm = q384() if roped else np.arange(384)
        part = (perm + 192) % 384
        zt = [None, None]
        for hg in range(4):
            wq = self.load(2048, lambda i, hg=hg: fm(i[pre + "Wq"][512 * hg:512 * hg + 512]))
            wqt = wq.ap.rearrange("p (m k c) -> p m k c", m=4, k=4)
            qt = {}
            self.barrier()
            for hh in range(4):
                h = 4 * hg + hh
                if roped:
                    p = self.load(384 + 384 + 128 + 384, lambda i, h=h: pad_rows(
                        [i[pre + "W_qr"][h][perm].T, i[pre + "W_qr"][h][part].T, i[pre + "W_kr"][h].T,
                         i[pre + "w_kc_q"][h][:, perm]]))
                    w1, w2, w3, w4 = p.ap[0:64, 0:384], p.ap[0:64, 384:768], p.ap[0:64, 768:896], p.ap[:, 896:1280]
                else:
                    p = self.load(384 + 128 + 384, lambda i, h=h: pad_rows(
                        [i[pre + "W_qr"][h].T, i[pre + "W_kr"][h].T,
                         i[pre + "w_kc_q"][h].T.reshape(3, 128, 128).transpose(1, 0, 2).reshape(128, 384)]))
                    w1, w3, w4 = p.ap[0:64, 0:384], p.ap[0:64, 384:512], p.ap[:, 512:896]
                    w2 = None
                pq = PQ[:, h % 2, :].rearrange("p (s j d) -> p s j d", s=2, j=3)
                for s, w in enumerate((w1, w2)):
                    if w is None:
                        continue
                    k = self.bank()
                    ps = self.P[k][:, 0:384].rearrange("p (j d) -> p j d", j=3)
                    for j in range(3):
                        t = self.mm(ps[:, j, :], w[:, 128 * j:128 * j + 128], w3, True, True, p.tok, inc=j == 2)
                    tp = self.copy(self.act, pq[:, s, :, :], ps, t)
                    self.free[k] = tp
                qh = QH[:, h % 2, :]
                tq = [None, None]
                for hf in range(2):
                    hs = self.hs(hf)
                    k = self.bank()
                    t = self.chain(self.P[k][:, 0:H2], [(wqt[:, hh, c, :], x[:, c, hs]) for c in range(4)], self.xt[hf], wq.tok)
                    tq[hf] = self.copy(self.act, qh[:, hs], self.P[k][:, 0:H2], t)
                    self.free[k] = tq[hf]
                if not roped:
                    k = self.bank()
                    w4j = w4.rearrange("p (j c) -> p j c", j=3)
                    t = self.chain(self.P[k][:, 0:128], [(w4j[:, j, :], pq[:, 0, j, :]) for j in range(3)], tp)
                    tm_ = self.copy(self.dve, MH[:, h % 2, :], self.P[k][:, 0:128], t)
                    self.free[k] = tm_
                    for hf in range(2):
                        hs = self.hs(hf)
                        k = self.bank()
                        t = self.mm(self.P[k][:, 0:H2], MH[:, h % 2, :], qh[:, hs], True, True, tm_, tq[hf], inc=True)
                        qt[hh, hf] = self.copy(self.dve, QE[:, hh, hs], self.P[k][:, 0:H2], t)
                        self.free[k] = qt[hh, hf]
                else:
                    w4j = w4.rearrange("p (j c) -> p j c", j=3)
                    for hf in range(2):
                        hs = self.hs(hf)
                        qb = QB[:, hf, :].rearrange("p (s j t) -> p s j t", s=2, j=3)
                        tb = None
                        for j in range(3):
                            k = self.bank()
                            t = self.mm(self.P[k][:, 0:H2], w4j[:, j, :], qh[:, hs], True, True, tq[hf], inc=True)
                            p4 = self.P[k][:, 0:H2].rearrange("p (b s) -> p b s", b=4)
                            for s, tab in enumerate(("cosq", "sinq")):
                                tb = self.tt(qb[:, s, j, :].rearrange("p (b s) -> p b s", b=4), p4,
                                             bc(self.c[tab][:, S * j:S * j + S], [128, 4, S]), ALU.mult, t,
                                             qt.get((hh - 1, hf)))
                            self.free[k] = tb
                        k = self.bank()
                        t = self.chain(self.P[k][:, 0:H2], [(pq[:, s, j, :], qb[:, s, j, :]) for s in range(2) for j in range(3)],
                                       tb, tp)
                        qt[hh, hf] = self.copy(self.act, QE[:, hh, hs], self.P[k][:, 0:H2], t)
                        self.free[k] = qt[hh, hf]
                p.rel = self.pe.now()
            wq.rel = self.pe.now()
            self.barrier()
            st = {}

            def scores(b):
                pm = Pm[:, b % 2, :].rearrange("p (a l) -> p a l", a=4)
                m = sm[:, 64 * (b % 2):64 * (b % 2) + 64]
                for hh in range(4):
                    k = self.bank()
                    t = self.mm(self.P[k][0:S, 0:L], QE[:, hh, S * b:S * b + S], kf[:, b, :], True, True, inc=True)
                    t = self.red(m[0:S, hh:hh + 1], self.P[k][0:S, 0:L], ALU.max, t, st.get(("pt", b - 2)), negate=True)
                    t = self.af(pm[0:S, hh, :], self.P[k][0:S, 0:L], ACT.Exp, t, st.get(("pt", b - 2)),
                                bias=m[0:S, hh:hh + 1], accum_out=m[0:S, 4 + hh:5 + hh])
                    self.free[k] = t
                t = self.rec(m[0:S, 8:12], m[0:S, 4:8], t)
                t = self.tt(pm[0:S, :, :], pm[0:S, :, :], bc(m[0:S, 8:12], [S, 4, L], 2), ALU.mult, t)
                st["p", b] = t

            def turn(b):
                pm = Pm[:, b % 2, :].rearrange("p (a l) -> p a l", a=4)
                pt = PT[:, b % 2, :].rearrange("p (j c) -> p j c", j=3)
                for j in range(3):
                    n = min(128, L - 128 * j)
                    k = self.bank()
                    for hh in range(4):
                        t = self.tr(self.P[k][0:n, S * hh:S * hh + S], pm[0:S, hh, 128 * j:128 * j + n], S, st["p", b], inc=hh == 3)
                    st["pt", b] = t
                    t = self.copy(self.act if j == 1 else self.dve, pt[0:n, j, :], self.P[k][0:n, 0:H2], t, st.get(("pv", b - 2)))
                    self.free[k] = t
                    st["c", b, j] = t

            def values(b):
                pt = PT[:, b % 2, :].rearrange("p (j c) -> p j c", j=3)
                k = self.bank()
                for j in range(3):
                    n = min(128, L - 128 * j)
                    t = self.mm(self.P[k][:, 0:H2], kt[0:n, b, j, :], pt[0:n, j, :], j == 0, j == 2, st["c", b, j], inc=j == 2)
                st["pv", b] = t
                t = self.copy(self.act, CT[:, :, S * b:S * b + S], self.P[k][:, 0:H2].rearrange("p (a s) -> p a s", a=4), t)
                self.free[k] = t
                ctt[b // 4] = t
            ctt = [None, None]
            pipeline(NB, scores, turn, values)
            wl = self.load(512, lambda i, hg=hg: i[pre + "w_kc_kv"][4 * hg:4 * hg + 4].transpose(2, 0, 1).reshape(128, 512))
            clt = [None, None]
            for hh in range(4):
                for hf in range(2):
                    k = self.bank()
                    t = self.mm(self.P[k][:, 0:H2], wl.ap[:, 128 * hh:128 * hh + 128], CT[:, hh, self.hs(hf)], True, True,
                                wl.tok, ctt[hf], inc=True)
                    clt[hf] = self.copy(self.dve, CL[:, hh, self.hs(hf)], self.P[k][:, 0:H2], t)
                    self.free[k] = clt[hf]
            wl.rel = self.pe.now()
            wo = self.load(2048, lambda i, hg=hg: fm(i[pre + "Wo"][:, 512 * hg:512 * hg + 512]))
            wot = wo.ap.rearrange("p (m k c) -> p m k c", m=4, k=4)
            base = x if hg == 0 else Z

            def evac(m, h, ps, t):
                zt[h] = self.tt(Z[:, m, self.hs(h)], ps, base[:, m, self.hs(h)], ALU.add, t)
                return zt[h]
            wo.rel = self.project(lambda m, k: wot[:, m, k, :], lambda k, h: CL[:, k, self.hs(h)], clt, 4, range(4), evac, wo.tok)
        self.barrier()
        self.layernorm(Z, self.ar(3200, 4, T), self.ar(6400, T), zt)

    def l0_ffn(self):
        self.barrier()
        x = self.x
        B1, B2 = self.ar(0, 16, 512), self.ar(8192, 16, 512)
        H = self.ar(8192, 16, T)
        XH = self.ar(20992, 4, T)
        had, nhad = self.c["had"], self.c["nhad"]
        bt = []
        for g in range(4):
            p = self.load(2048, lambda i, g=g: tm(i["L0_ffn_W_down"][:, 512 * g:512 * g + 512]))
            w = p.ap.rearrange("p (k c) -> p k c", k=4)
            for k in range(4):
                b = self.bank()
                t = self.mm(self.P[b][:, :], had, w[:, k, :], True, True, p.tok, inc=True)
                t = self.copy(self.act if k % 2 else self.dve, B1[:, 4 * g + k, :], self.P[b][:, :], t)
                self.free[b] = t
                bt.append(t)
            p.rel = self.pe.now()
        src, dst = B1, B2
        t = bt[-2:]
        for lev in range(4):
            s = 1 << lev
            for base in range(0, 16, 2 * s):
                a, b_ = src[:, base:base + s, :], src[:, base + s:base + 2 * s, :]
                self.tt(dst[:, base:base + s, :], a, b_, ALU.add, t)
                t1 = self.tt(dst[:, base + s:base + 2 * s, :], a, b_, ALU.subtract)
            t = t1
            src, dst = dst, src
        wdt = t
        XS = self.ar(16384, 4, T)
        xs = [None, None]
        for c in range(4):
            for h in range(2):
                xs[h] = self.ts(XS[:, c, self.hs(h)], x[:, c, self.hs(h)], self.c["su"][:, c:c + 1], None, ALU.mult, None, self.xt[h])
        h4 = hadamard(4)
        xh = [None, None]
        r512 = float(np.float32(1.0) / np.sqrt(np.float32(512)))

        def evac(m, h, ps, t):
            xh[h] = self.af(XH[:, m, self.hs(h)], ps, ACT.Copy, t, scale=r512)
            return xh[h]
        self.project(lambda m, k: had if h4[m, k] > 0 else nhad, lambda k, h: XS[:, k, self.hs(h)], xs, 4, range(4), evac)
        sm = self.small
        ws = self.ts(sm[:, 0:16], self.c["wsu"], 1.0, None, ALU.mult, None)
        ws = self.tt(sm[:, 0:16], sm[:, 0:16], self.c["sud"], ALU.mult, ws)
        wd = self.ts(sm[:, 16:20], self.c["wsd"], float(np.float32(1.0) / np.sqrt(np.float32(2048))), None, ALU.mult, None)
        self.barrier()
        G = sm[:, 32:832].rearrange("p (a t) -> p a t", a=2)
        ht, gfree, n = [None, None], [None, None], 0
        for g in range(8):
            p = self.load(2048, lambda i, g=g: np.concatenate(
                [fm(i["L0_ffn_W_up"][256 * g:256 * g + 256]), fm(i["L0_ffn_W_gate"][256 * g:256 * g + 256])], 1))
            w = p.ap.rearrange("p (m k c) -> p m k c", m=4, k=4)
            for m in range(2):
                f = 2 * g + m
                for h in range(2):
                    hs = self.hs(h)
                    bu, bg = self.bank(), self.bank()
                    tu = self.chain(self.P[bu][:, 0:H2], [(w[:, m, k, :], XH[:, k, hs]) for k in range(4)], xh[h], p.tok)
                    tg = self.chain(self.P[bg][:, 0:H2], [(w[:, 2 + m, k, :], XH[:, k, hs]) for k in range(4)])
                    t = self.af(G[:, n % 2, :], self.P[bg][:, 0:H2], ACT.Silu, tg, gfree[n % 2], scale=self.c["wsg"][:, f:f + 1])
                    self.free[bg] = t
                    t = self.stt(H[:, f, hs], self.P[bu][:, 0:H2], sm[:, f:f + 1], G[:, n % 2, :], ALU.mult, ALU.mult, tu, t, ws)
                    self.free[bu] = gfree[n % 2] = ht[h] = t
                    n += 1
            p.rel = self.pe.now()
        self.dve.wait(self.pe.now())
        Z, zt = XH, [None, None]

        def evacz(m, h, ps, t):
            zt[h] = self.stt(Z[:, m, self.hs(h)], ps, sm[:, 16 + m:17 + m], x[:, m, self.hs(h)], ALU.mult, ALU.add, t, wd)
            return zt[h]
        self.project(lambda m, k: B1[:, k, 128 * m:128 * m + 128], lambda k, h: H[:, k, self.hs(h)],
                     [[ht[0], wdt], [ht[1], wdt]], 16, range(4), evacz)
        self.act.wait(self.pe.now())
        self.dve.wait(self.pe.now())
        self.layernorm(Z, self.ar(8192, 4, T), self.ar(12000, T), zt)

    def router(self, w, n, bias, sm, width):
        t = None
        for b in range(NB):
            k = self.bank()
            t = self.chain(self.P[k][0:S, 0:n], [(self.x[:, c, S * b:S * b + S], w[:, c, :]) for c in range(4)], self.xt[b // 4])
            if bias is None:
                t = self.copy(self.dve, sm[0:S, b, 0:n], self.P[k][0:S, 0:n], t)
            else:
                t = self.tt(sm[0:S, b, 0:n], self.P[k][0:S, 0:n], bias[0:S, :], ALU.add, t)
            self.free[k] = t
        return t

    def top(self, vals, b, n, mx, ix, ixf, *toks):
        v, m, i, f = vals[0:S, b, 0:n], mx[0:S, b, :], ix[0:S, b, :], ixf[0:S, b, :]
        t = self.dve.do(lambda e: e.max(m, v), *toks)
        t = self.dve.do(lambda e: e.max_index(i, m, v), t)
        return self.dve.do(lambda e: e.tensor_copy(f, i), t)

    def shared(self, nf, load, gate, ACC, G, HI):
        x = self.x
        p, q = load()
        w = p.ap[:, 0:1024 * nf].rearrange("p (m k c) -> p m k c", m=2 * nf, k=4)
        wd = (q.ap if q else p.ap[:, 1024:1536]).rearrange("p (f n) -> p f n", f=nf)
        for f in range(nf):
            for h in range(2):
                hs = self.hs(h)
                bg, bu = self.bank(), self.bank()
                tg = self.chain(self.P[bg][:, 0:H2], [(w[:, f, k, :], x[:, k, hs]) for k in range(4)], p.tok, self.xt[h])
                tu = self.chain(self.P[bu][:, 0:H2], [(w[:, nf + f, k, :], x[:, k, hs]) for k in range(4)])
                t = self.af(G[:, f, hs], self.P[bg][:, 0:H2], ACT.Silu, tg)
                self.free[bg] = t
                t = self.tt(HI[:, f, hs], self.P[bu][:, 0:H2], G[:, f, hs], ALU.mult, tu, t)
                self.free[bu] = t
        acc = {}
        for b in range(NB):
            k = self.bank()
            t1 = self.chain(self.P[k][0:S, :], [(HI[:, f, S * b:S * b + S], wd[:, f, :]) for f in range(nf)], t,
                            q.tok if q else None)
            self.free[k] = acc[b] = gate(ACC[0:S, b, :], self.P[k][0:S, :], b, t1)
        p.rel = self.pe.now()
        if q:
            q.rel = p.rel
        return acc

    def gather(self, out, table, idx, *toks):
        sem = self.gsem[self.ng % len(self.gsem)]
        self.ng += 1
        val = 16 * ((self.ng - 1) // len(self.gsem) + 1)
        self.pool.wait(*toks)
        if val > 16:
            self.pool.wait(Tok(sem, val - 16))
        self.pool.q.append((None, lambda e: e.indirect_dma_start(
            out, None, table, bass.IndirectOffsetOnAxis(ap=idx, axis=0)).then_inc(sem, 16), False))
        return Tok(sem, val)

    def scatter(self, table, idx, src, *toks):
        sem = self.gsem[self.ng % len(self.gsem)]
        self.ng += 1
        val = 16 * ((self.ng - 1) // len(self.gsem) + 1)
        self.pool.wait(*toks)
        if val > 16:
            self.pool.wait(Tok(sem, val - 16))
        self.pool.q.append((None, lambda e: e.indirect_dma_start(
            table, bass.IndirectOffsetOnAxis(ap=idx, axis=0), src, None).then_inc(sem, 16), False))
        return Tok(sem, val)

    def store(self, out, in_, *toks):
        sem = self.ssem[self.ns % len(self.ssem)]
        self.ns += 1
        val = 16 * ((self.ns - 1) // len(self.ssem) + 1)
        self.act.wait(*toks)
        if val > 16:
            self.act.wait(Tok(sem, val - 16))
        self.act.q.append((None, lambda e: e.dma_start(out, in_).then_inc(sem, 16), False))
        return Tok(sem, val)

    def sparse(self, E, kk, nf, MK, CB, mt, ct, wd, shared):
        NT = (T * kk + 127 * E) // 128
        x = self.x
        ACC = self.ar(8000, NB, 512)
        XT = self.ar(12096, NB, 512)
        nw = 1536 * nf
        WT = [self.ar(a, nw) for a in ((12096, 15168, 0) if nf == 2 else (12096, 13632, 15168, 16704, 0, 1536, 3072))]
        R = len(WT)
        XG = self.ar(18240, 4, 512)
        XF = self.ar(20288, 2, 512)
        G, HI = self.ar(21312, 2, 256), self.ar(21824, 2, 256)
        Y = self.ar(22336, 3, 512)
        XD, TD, YD = self.XD, self.TD[NT], self.YD[NT]
        U = lambda a: a.bitcast(U32)
        sx = []
        for b in range(NB):
            k = self.bank()
            for c in range(4):
                t = self.tr(self.P[k][0:S, 128 * c:128 * c + 128], x[:, c, S * b:S * b + S], 128, self.xt[b // 4], inc=c == 3)
            t = self.copy(self.act, XT[0:S, b, :], self.P[k][0:S, :], t)
            self.free[k] = t
            sx.append(self.store(XD[S * b:S * b + S, :], XT[0:S, b, :], t))
        MT, RK = self.ar(4000, T), self.ar(4800, T)
        sm = self.small
        for g in range(2):
            k = self.bank()
            for b in range(4):
                t = self.tr(self.P[k][0:E, S * b:S * b + S], MK[0:S, 4 * g + b, :], S, mt, inc=b == 3)
            t = self.copy(self.dve, MT[0:E, self.hs(g)], self.P[k][0:E, 0:H2], t)
            self.free[k] = t
        t = self.dve.do(lambda e: e.tensor_tensor_scan(RK[0:E, :], MT[0:E, :], MT[0:E, :], 0.0, ALU.add, ALU.max), t)
        cmp7, tl, base, end = sm[0:E, 0:7], sm[0:E, 8:9], sm[0:E, 9:10], sm[0:E, 10:11]
        t = self.ts(cmp7, self.c["thr"][0:E, :], RK[0:E, T - 1:T], None, ALU.is_lt, None, t)
        t = self.red(tl, cmp7, ALU.add, t)
        k = self.bank()
        t = self.mm(self.P[k][0:E, 0:1], self.c["tri"][0:E, 0:E], tl, True, True, t, inc=True)
        t1 = self.ts(base, self.P[k][0:E, 0:1], 128.0, None, ALU.mult, None, t)
        t2 = self.tt(end, self.P[k][0:E, 0:1], tl, ALU.add, t)
        self.free[k] = t2
        t = self.stt(RK[0:E, :], RK[0:E, :], base, MT[0:E, :], ALU.add, ALU.mult, t1, t2)
        CM = self.ar(5600, 113)
        tc = self.ts(CM[0:E, 0:NT], self.c["tiles"][0:E, 0:NT], end, None, ALU.is_ge, None, t)
        SLT = self.ar(6400, NB, E)
        g_ = 512 // E
        ts_ = t
        for g in range(0, NB, min(g_, NB)):
            n = min(g_, NB)
            k = self.bank()
            for b in range(n):
                t = self.tr(self.P[k][0:S, E * b:E * b + E], RK[0:E, S * (g + b):S * (g + b) + S], E, ts_, inc=b == n - 1)
            t = self.copy(self.dve, SLT[0:S, g:g + n, :], self.P[k][0:S, 0:E * n].rearrange("p (b e) -> p b e", b=n), t)
            self.free[k] = t
        SV, SI = self.ar(5720, NB, 8), U(self.ar(5784, NB, 8))
        TK = U(self.ar(5850, NB))
        for b in range(NB):
            t = self.dve.do(lambda e, b=b: e.max(SV[0:S, b, :], SLT[0:S, b, :]), t)
        SF = self.ar(5860, NB, 8)
        t = self.ts(SF[0:S, :, 0:kk], SV[0:S, :, 0:kk], -1.0, None, ALU.add, None, t)
        t = self.dve.do(lambda e: e.tensor_copy(SI[0:S, :, 0:kk], SF[0:S, :, 0:kk]), t)
        t = self.dve.do(lambda e: e.tensor_copy(TK[0:S, :], self.c["token"][0:S, :]), t)
        ZR = U(self.ar(6924, 128))
        tz = self.dve.do(lambda e: e.memset(ZR[:, :], 0))
        tz = self.store(TD[0:128 * NT, :].rearrange("(t r) o -> t (r o)", r=128), ZR[0:NT, :], tz)
        sc = [self.scatter(TD[:, :], SI[0:S, b, j:j + 1], TK[0:S, b:b + 1], t, tz) for b in range(NB) for j in range(kk)]
        k = self.bank()
        t = self.mm(self.P[k][:, 0:NT], self.c["mean"][0:E, :], CM[0:E, 0:NT], True, True, tc, inc=True)
        WF, WI = self.ar(7060, NT), U(self.ar(7180, NT))
        t = self.ts(WF, self.P[k][:, 0:NT], 512.0, float(E - 1), ALU.mult, ALU.min, t)
        self.free[k] = t
        t = self.ts(WF, WF, 128.0, self.c["lane"], ALU.mult, ALU.add, t)
        wi = self.dve.do(lambda e: e.tensor_copy(WI[:, :], WF[:, :]), t)
        GP, EQ = self.ar(7300, NB, 8), self.ar(3400, NB, E)
        t = ct
        for j in range(kk):
            t = self.tt(EQ[0:S], SLT[0:S], SV[0:S, :, j:j + 1].to_broadcast([S, NB, E]), ALU.is_equal, t)
            t = self.tt(EQ[0:S], EQ[0:S], CB[0:S, :, 0:E], ALU.mult, t)
            t = self.red(GP[0:S, :, j], EQ[0:S], ALU.add, t)
        gp = t
        acc = shared(ACC, self.ar(18240, nf, T), self.ar(18240 + nf * T, nf, T))
        TU, TF, TI = U(self.ar(7370, 128)), self.ar(7500, 128), U(self.ar(7630, NT))
        sem = self.s_list[self.nl]
        self.nl += 1
        self.act.wait(sc)
        self.act.q.append((None, lambda e: e.dma_start(
            TU[0:NT, :], TD[0:128 * NT, :].rearrange("(t r) o -> t (r o)", r=128)).then_inc(sem, 16), False))
        t = self.dve.do(lambda e: e.tensor_copy(TF[0:NT, :], TU[0:NT, :]), Tok(sem, 16))
        k = self.bank()
        t = self.tr(self.P[k][:, 0:NT], TF[0:NT, :], NT, t, inc=True)
        ti = self.copy(self.dve, TI[:, :], self.P[k][:, 0:NT], t)
        self.free[k] = ti
        over = [self.pe.now(), self.dve.now(), self.act.now()]
        st = {}

        def fetch(i):
            st["w", i] = self.gather(WT[i % R], wd, WI[:, i:i + 1], wi, sx, over, st.get(("d", i - R)))
            st["x", i] = self.gather(XG[:, i % 4, :], XD[:, :], TI[:, i:i + 1], ti, sx, over, st.get(("t", i - 4)))

        def turn(i):
            k = self.bank()
            for c in range(4):
                t = self.tr(self.P[k][:, 128 * c:128 * c + 128], XG[:, i % 4, 128 * c:128 * c + 128], 128, st["x", i], inc=c == 3)
            st["t", i] = t
            t = self.copy(self.dve, XF[:, i % 2, :], self.P[k][:, :], t, st.get(("u", i - 2)))
            self.free[k] = t
            st["f", i] = t

        def up(i):
            w = WT[i % R][:, 0:1024 * nf].rearrange("p (m k c) -> p m k c", m=2 * nf, k=4)
            xf = XF[:, i % 2, :].rearrange("p (c t) -> p c t", c=4)
            k = self.bank()
            for m in range(2 * nf):
                t = self.chain(self.P[k][:, 128 * m:128 * m + 128], [(w[:, m, c, :], xf[:, c, :]) for c in range(4)],
                               st["f", i], st["w", i])
            st["u", i] = t
            n = 128 * nf
            t = self.af(G[:, i % 2, 0:n], self.P[k][:, 0:n], ACT.Silu, t, st.get(("h", i - 2)))
            t = self.tt(HI[:, i % 2, 0:n], self.P[k][:, n:2 * n], G[:, i % 2, 0:n], ALU.mult, t, st.get(("d", i - 2)))
            self.free[k] = t
            st["h", i] = t

        def down(i):
            w = WT[i % R][:, 1024 * nf:1536 * nf].rearrange("p (f n) -> p f n", f=nf)
            k = self.bank()
            t = self.chain(self.P[k][:, :], [(HI[:, i % 2, 128 * f:128 * f + 128], w[:, f, :]) for f in range(nf)], st["h", i])
            st["d", i] = t
            t = self.copy(self.act, Y[:, i % 3, :], self.P[k][:, :], t, st.get(("s", i - 3)))
            self.free[k] = t
            st["s", i] = self.store(YD[128 * i:128 * i + 128, :], Y[:, i % 3, :], t)
        idle = [lambda i: None] * (2 if nf == 1 else 0)
        pipeline(NT, fetch, *idle, turn, up, down)
        done = [st["s", i] for i in range(NT - min(NT, len(self.ssem)), NT)]
        YG = self.ar(12096, 8, 512)
        pe = self.pe.now()
        Z, zt = self.ar(18240, 4, T), [None, None]
        n = 0
        for b in range(NB):
            for j in range(kk):
                t = self.gather(YG[0:S, n % 8, :], YD[:, :], SI[0:S, b, j:j + 1], done, pe, st.get(("y", n - 8)))
                a = ACC[0:S, b, :]
                acc[b] = self.stt(a, YG[0:S, n % 8, :], GP[0:S, b, j:j + 1], a, ALU.mult, ALU.add, t, gp, acc[b])
                st["y", n] = acc[b]
                n += 1
            k = self.bank()
            ps = self.P[k][:, 0:4 * S].rearrange("p (c s) -> p c s", c=4)
            for c in range(4):
                t = self.tr(ps[:, c, :], ACC[0:S, b, 128 * c:128 * c + 128], S, acc[b], inc=c == 3)
            sl = slice(S * b, S * b + S)
            zt[b // 4] = self.tt(Z[:, :, sl], ps, x[:, :, sl], ALU.add, t, done)
            self.free[k] = zt[b // 4]
        self.layernorm(Z, self.ar(0, 4, T), self.ar(3200, T), zt)

    def l1_ffn(self):
        self.barrier()
        pre = "L1_ffn_"
        E = 16
        SC, CB, OH = self.ar(0, NB, E), self.ar(128, NB, E + 1), self.ar(300, NB, E)
        BI = self.ar(500, NB, E)
        MX, IX, IF = self.ar(700, NB, 8), self.ar(800, NB, 8).bitcast(U32), self.ar(900, NB, 8)
        SS = self.ar(1000, NB)
        w = self.c["g1w"].rearrange("p (k e) -> p k e", k=4)
        t = self.router(w, E, None, SC, E)
        t = self.af(SC[0:S], SC[0:S], ACT.Sigmoid, t)
        t = self.tt(BI[0:S], SC[0:S], bc(self.c["g1b"][0:S, :], [S, NB, E]), ALU.add, t)
        for b in range(NB):
            t = self.top(BI, b, E, MX, IX, IF, t)
        iota = bc(self.c["iota"][0:S, 0:E], [S, NB, E])
        t = self.tt(CB[0:S, :, 0:E], iota, IF[0:S, :, 0:1].to_broadcast([S, NB, E]), ALU.is_equal, t)
        t = self.tt(OH[0:S], iota, IF[0:S, :, 1:2].to_broadcast([S, NB, E]), ALU.is_equal, t)
        t = tm_ = self.tt(OH[0:S], CB[0:S, :, 0:E], OH[0:S], ALU.add, t)
        t = self.tt(CB[0:S, :, 0:E], OH[0:S], SC[0:S], ALU.mult, t)
        t = self.red(SS[0:S], CB[0:S, :, 0:E], ALU.add, t)
        t = self.ts(SS[0:S], SS[0:S], 1e-20, None, ALU.add, None, t)
        t = self.rec(SS[0:S], SS[0:S], t)
        t = self.tt(CB[0:S, :, 0:E], CB[0:S, :, 0:E], bc(SS[0:S], [S, NB, E], 2), ALU.mult, t)
        self.sparse(E, 2, 2, OH, CB, tm_, t, self.E1, lambda ACC, G, HI: self.shared(2, lambda: (
            self.load(2048, lambda i: np.concatenate([fm(i[pre + "shared_gate_w"].T), fm(i[pre + "shared_up_w"].T)], 1)),
            self.load(1024, lambda i: tm(i[pre + "shared_down_w"].T))), lambda a, ps, b, t: self.copy(self.act, a, ps, t),
            ACC, G, HI))

    def l3_ffn(self):
        self.barrier()
        pre = "L3_ffn_"
        E = 64
        LG, CB, WK = self.ar(0, NB, E + 1), self.ar(600, NB, E + 1), self.ar(1200, NB, E)
        MX, NM, SS = self.ar(1800, NB, 8), self.ar(1900, NB), self.ar(1950, NB)
        w = self.c["g3w"].rearrange("p (k e) -> p k e", k=4)
        t = self.router(w, E + 1, None, LG, E + 1)
        tl = t
        for b in range(NB):
            lg = LG[0:S, b, 0:E]
            t = self.dve.do(lambda e, b=b, lg=lg: e.max(MX[0:S, b, :], lg), t)
            t = self.dve.do(lambda e, b=b, lg=lg: e.match_replace(WK[0:S, b, :], MX[0:S, b, :], lg, -3.0e38), t)
        cb = CB[0:S, :, 0:E]
        MK = self.ar(2000, NB, E)
        t = mt = self.tt(MK[0:S], WK[0:S], LG[0:S, :, 0:E], ALU.not_equal, t)
        t = self.tt(WK[0:S], LG[0:S, :, 0:E], bc(MX[0:S, :, 0], [S, NB, E], 2), ALU.subtract, t)
        t = self.af(WK[0:S], WK[0:S], ACT.Exp, t)
        t = self.tt(cb, MK[0:S], WK[0:S], ALU.mult, t)
        t = self.red(SS[0:S], cb, ALU.add, t)
        t = self.rec(SS[0:S], SS[0:S], t)
        t = self.tt(cb, cb, bc(SS[0:S], [S, NB, E], 2), ALU.mult, t)
        t2 = self.af(CB[0:S, :, E:E + 1], LG[0:S, :, E:E + 1], ACT.Sigmoid, tl)

        self.sparse(E, 8, 1, MK, CB, mt, t, self.E3, lambda ACC, G, HI: self.shared(1, lambda: (self.load(1536, lambda i: np.concatenate(
            [fm(i[pre + "sh_gate_w"]), fm(i[pre + "sh_up_w"]), i[pre + "sh_down_w"].T], 1)), None),
            lambda a, ps, b, t: self.ts(a, ps, CB[0:S, b, E:E + 1], None, ALU.mult, None, t, t2), ACC, G, HI))

    def l2_ffn(self):
        self.barrier()
        E = 8
        LG, PR, OH = self.ar(0, NB, E), self.ar(64, NB, E), self.ar(128, NB, E)
        MX, IX, IF = self.ar(192, NB, 8), self.ar(256, NB, 8).bitcast(U32), self.ar(320, NB, 8)
        NM, SS = self.ar(384, NB), self.ar(392, NB)
        GT = self.ar(400, T)
        GB = self.ar(1200, 4, T)
        Hh = self.ar(4400, 4, T)
        w = self.c["wr"].rearrange("p (k e) -> p k e", k=4)
        t = self.router(w, E, self.c["br"], LG, E)
        t = self.red(NM[0:S], LG[0:S], ALU.max, t)
        t = self.tt(LG[0:S], LG[0:S], bc(NM[0:S], [S, NB, E], 2), ALU.subtract, t)
        t = self.af(PR[0:S], LG[0:S], ACT.Exp, t)
        t = self.red(SS[0:S], PR[0:S], ALU.add, t)
        t = self.rec(SS[0:S], SS[0:S], t)
        t = self.tt(PR[0:S], PR[0:S], bc(SS[0:S], [S, NB, E], 2), ALU.mult, t)
        for b in range(NB):
            t = self.top(PR, b, E, MX, IX, IF, t)
        t = self.tt(OH[0:S], bc(self.c["iota"][0:S, 0:E], [S, NB, E]), IF[0:S, :, 0:1].to_broadcast([S, NB, E]), ALU.is_equal, t)
        t = self.tt(OH[0:S], OH[0:S], MX[0:S, :, 0:1].to_broadcast([S, NB, E]), ALU.mult, t)
        t = self.ts(OH[0:S], OH[0:S], 1.0 / 64, None, ALU.mult, None, t)
        gt = [None, None]
        for b in range(NB):
            k = self.bank()
            t1 = self.tr(self.P[k][0:E, 0:S], OH[0:S, b, :], S, t, inc=True)
            gt[b // 4] = self.copy(self.act, GT[0:E, S * b:S * b + S], self.P[k][0:E, 0:S], t1)
            self.free[k] = gt[b // 4]
        gb = {}
        sel = self.c["sel8"].rearrange("p (k c) -> p k c", k=4)
        for m in range(4):
            for h in range(2):
                k = self.bank()
                t1 = self.mm(self.P[k][:, 0:H2], sel[0:E, m, :], GT[0:E, self.hs(h)], True, True, gt[h], inc=True)
                gb[m, h] = self.copy(self.act, GB[:, m, self.hs(h)], self.P[k][:, 0:H2], t1)
                self.free[k] = gb[m, h]
        ht = [None, None]

        def evac(m, h, ps, t):
            ht[h] = self.tt(Hh[:, m, self.hs(h)], ps, GB[:, m, self.hs(h)], ALU.mult, t, gb[m, h])
            return ht[h]
        self.full("L2_ffn_A", lambda a: a.reshape(512, 512), self.x, self.xt, evac)
        Z, zt = self.ar(7600, 4, T), [None, None]
        self.full("L2_ffn_B", lambda a: a.transpose(1, 0, 2).reshape(512, 512), Hh, ht, self.add_residual(Z, zt))
        self.layernorm(Z, self.ar(10800, 4, T), self.ar(14000, T), zt)

    def layer(self, n):
        [self.l0_attn, lambda: self.xattn("L0_xattn_"), self.l0_ffn, self.l1_attn, lambda: self.mla("L1_xattn_", False),
         self.l1_ffn, self.l2_attn, lambda: self.mla("L2_xattn_", True), self.l2_ffn, self.l3_attn,
         lambda: self.xattn("L3_xattn_"), self.l3_ffn][n]()


def pad_rows(parts):
    out = []
    for a in parts:
        b = np.zeros((128, a.shape[1]), np.float32)
        b[:a.shape[0]] = a
        out.append(b)
    return np.concatenate(out, 1)


def build(nc, layers=range(12)):
    from contextlib import ExitStack
    with ExitStack() as stack:
        k = K(nc, stack, layers)
        k.act.wait(k.ic)
        k.dve.wait(k.ic)
        k.prep()
        for n in layers:
            k.layer(n)
        total = sum(128 * p.n for p in k.loads)
        wd = nc.dram_tensor("weights", [total], F32, kind="ExternalInput").ap()
        cd = nc.dram_tensor("constants", [128, k.cw], F32, kind="ExternalInput").ap()
        xd = nc.dram_tensor("xt", [128, 4 * T], F32, kind="ExternalInput").ap()
        kd = nc.dram_tensor("ctx", [128, NB * L], F32, kind="ExternalInput").ap()
        od = nc.dram_tensor("out", [128, 4 * T], F32, kind="ExternalOutput").ap()
        block = stack.enter_context(nc.Block())

        @block.sync
        def _(e):
            e.dma_start(k.C[:, :], cd).then_inc(k.s_in[0], 16)
            e.dma_start(k.A[:, 0:NB * L], kd).then_inc(k.s_in[3], 16)
            e.dma_start(k.X[:, :], xd).then_inc(k.s_in[1], 16)
            e.dma_start(k.CX[:, :].rearrange("p (b s) -> p b s", b=NB),
                        kd.rearrange("p (b l) -> p b l", b=NB)[:, :, 0:S]).then_inc(k.s_in[2], 16)
            at = 0
            sp = Eng("sp", None)
            for i, p in enumerate(k.loads):
                if i >= RING:
                    sp.wait(k.loads[i - RING].rel)
                src = wd[at:at + 128 * p.n].rearrange("(p n) -> p n", n=p.n)
                at += 128 * p.n
                sem = p.tok.sem
                sp.q.append((None, lambda e, p=p, src=src, sem=sem: e.dma_start(p.ap, src).then_inc(sem, 16), False))
            sp.flush(e)
            for t in k.xt:
                e.wait_ge(t.sem, t.val)
            e.dma_start(od, k.X[:, :]).then_inc(k.s_out, 16)
            e.wait_ge(k.s_out, 16)

        @block.tensor
        def _(e):
            k.pe.flush(e)

        @block.scalar
        def _(e):
            k.act.flush(e)

        @block.vector
        def _(e):
            k.dve.flush(e)

        @block.gpsimd
        def _(e):
            k.pool.flush(e)
    return k


def experts1(i):
    g = np.asarray(i["L1_ffn_experts_gate_up"]).reshape(16, 4, 128, 4, 128).transpose(0, 2, 3, 1, 4).reshape(16 * 128, 2048)
    d = np.asarray(i["L1_ffn_experts_down"]).reshape(16, 2, 128, 512).transpose(0, 2, 1, 3).reshape(16 * 128, 1024)
    return np.concatenate([g, d], 1)


def experts3(i):
    g = np.asarray(i["L3_ffn_gu_w"]).reshape(64, 2, 128, 4, 128).transpose(0, 4, 1, 3, 2).reshape(64 * 128, 1024)
    d = np.asarray(i["L3_ffn_dp_w"]).transpose(0, 2, 1).reshape(64 * 128, 512)
    return np.concatenate([g, d], 1)


def pack(k, inputs):
    x = np.asarray(inputs["x"])
    xt = x.reshape(T, 4, 128).transpose(2, 1, 0).reshape(128, 4 * T)
    cx = np.asarray(inputs["ctx_512"]).transpose(2, 0, 1).reshape(128, NB * L)
    cc = np.concatenate([v for v in k.consts.values()] + [f(inputs) for _, f in PARAMS.values()], 1)
    parts = [np.ascontiguousarray(p.pack(inputs)) for p in k.loads]
    for p, a in zip(k.loads, parts):
        assert a.shape == (128, p.n), (a.shape, p.n)
    ws = np.concatenate([a.reshape(-1) for a in parts])
    return {"xt": np.ascontiguousarray(xt), "ctx": np.ascontiguousarray(cx), "constants": np.ascontiguousarray(cc),
            "weights": ws, "experts1": experts1(inputs), "experts3": experts3(inputs)}


def kernel(**inputs):
    import numpy as _np
    import concourse.bacc as _bacc
    from concourse.bass_utils import run_bass_kernel_spmd as _run

    nc = _bacc.Bacc("TRN2", target_bir_lowering=False, num_devices=1)
    k = build(nc)
    r = _run(nc, [pack(k, inputs)], core_ids=[0])
    o = r.results[0]["out"]
    return _np.ascontiguousarray(o.reshape(128, 4, NB, S).transpose(2, 3, 1, 0).reshape(NB, S, 512))
```

```python
import numpy as np
import concourse.bass as bass
from concourse import mybir

ALU = mybir.AluOpType
ACT = mybir.ActivationFunctionType
F32 = mybir.dt.float32
U32 = mybir.dt.uint32
AX = mybir.AxisListType

NB, S, L, T, H2 = 8, 100, 361, 800, 400
SLOT, RING = 2048, 5
ARENA = 27200
NEG = -1.0e30



def fm(w):
    o, i = w.shape
    m = min(128, o)
    return w.reshape(o // m, m, i // 128, 128).transpose(3, 0, 2, 1).reshape(128, -1)


def tm(w):
    o, i = w.shape
    return w.T.reshape(i // 128, 128, o).transpose(1, 0, 2).reshape(128, -1)


def col(v):
    return v.reshape(-1, 128).T


def rows(v):
    return np.broadcast_to(v.reshape(1, -1), (128, v.size))


def hadamard(n):
    h = np.ones((1, 1), np.float32)
    while h.shape[0] < n:
        h = np.block([[h, h], [h, -h]])
    return h.astype(np.float32)


def swap_matrix(width):
    m = np.zeros((128, 128), np.float32)
    for p in range(128):
        m[p - p % width + (p % width + width // 2) % width, p] = 1.0
    return m


def rope32(pos, div):
    half = 16
    if div:
        inv = (np.float32(1.0) / np.float32(10000.0) ** (np.arange(0, 32, 2, dtype=np.float32) / np.float32(32))).astype(np.float32)
    else:
        inv = (np.float32(10000.0) ** (-np.arange(half, dtype=np.float32) / np.float32(half))).astype(np.float32)
    ang = (np.asarray(pos, np.float32)[None, :] * inv[:, None]).astype(np.float32)
    c, s = np.cos(ang), np.sin(ang)
    c = np.tile(np.concatenate([c, c], 0), (4, 1))
    s = np.tile(np.concatenate([-s, s], 0), (4, 1))
    return c.astype(np.float32), s.astype(np.float32)


def rope_mla(n, dim):
    inv = (np.float32(1.0) / np.float32(10000.0) ** (np.arange(0, dim, 2, dtype=np.float32) / np.float32(dim))).astype(np.float32)
    f = (np.arange(n, dtype=np.float32)[:, None] * inv[None, :]).astype(np.float32)
    return np.repeat(np.cos(f), 2, -1).T.astype(np.float32), np.repeat(np.sin(f), 2, -1).T.astype(np.float32)


def shape_constants():
    c = {}
    c["mean"] = np.full((128, 128), 1.0 / 512, np.float32)
    c["eps"] = rows(np.array([1.1920929e-07, 1e-05, 0.0, 1.0], np.float32))
    m = np.ones((128, H2), np.float32)
    m[:, ::S] = 0.0
    c["restart"] = m
    c["ident"] = np.eye(128, dtype=np.float32)
    c["had"] = hadamard(128)
    c["nhad"] = -hadamard(128)
    c["swap32"] = swap_matrix(32)
    c["swap128"] = swap_matrix(128)
    c["cos1"], c["sin1"] = rope32(range(S), False)
    c["cos3"], c["sin3"] = rope32(range(S), True)
    co, si = rope_mla(L, 128)
    sg = np.where(np.arange(128) < 64, -1.0, 1.0).astype(np.float32)[:, None]
    c["cosk"], c["sink"] = co, si * sg
    co, si = rope_mla(S, 384)
    perm = q384()
    partner = (np.arange(384) + 192) % 384
    sign = np.where(partner < 192, -1.0, 1.0).astype(np.float32)[:, None]
    c["cosq"] = co[perm].reshape(3, 128, S).transpose(1, 0, 2).reshape(128, -1)
    c["sinq"] = (si[partner] * sign)[perm].reshape(3, 128, S).transpose(1, 0, 2).reshape(128, -1)
    cm = np.zeros((128, S), np.float32)
    cm[:S] = np.where(np.arange(S)[:, None] >= np.arange(S)[None, :], 0.0, NEG)
    c["causal"] = cm
    e = np.zeros((128, S), np.float32)
    e[S - 1] = 1.0
    c["lastrow"] = e
    c["iota"] = rows(np.arange(64, dtype=np.float32))
    sel = np.zeros((128, 4, 128), np.float32)
    for k in range(4):
        for p in range(128):
            sel[2 * k + p // 64, k, p] = 1.0
    c["sel8"] = sel.reshape(128, -1)
    c["tri"] = np.zeros((128, 64), np.float32)
    c["tri"][:64] = np.triu(np.ones((64, 64), np.float32), 1)
    c["thr"] = rows(128.0 * np.arange(7, dtype=np.float32))
    c["tiles"] = rows(np.arange(113, dtype=np.float32))
    c["slots"] = rows(np.arange(128, dtype=np.float32))
    c["lane"] = np.arange(128, dtype=np.float32)[:, None]
    c["token"] = np.arange(128, dtype=np.float32)[:, None] + 100 * np.arange(8, dtype=np.float32)[None, :]
    return c


def q384():
    b = np.arange(384).reshape(6, 64)
    return np.concatenate([np.concatenate([b[t], b[t + 3]]) for t in range(3)])


PARAMS = {
    "su": (4, lambda i: col(i["L0_ffn_SU_ug"])),
    "sud": (16, lambda i: col(i["L0_ffn_SU_dp"])),
    "wsu": (16, lambda i: col(i["L0_ffn_Wscale_ug"][:2048])),
    "wsg": (16, lambda i: col(i["L0_ffn_Wscale_ug"][2048:])),
    "wsd": (4, lambda i: col(i["L0_ffn_Wscale_dp"])),
    "bq": (4, lambda i: col(i["L1_attn_bq"])),
    "bk": (2, lambda i: col(np.tile(i["L1_attn_bk"].reshape(2, 1, 32), (1, 4, 1)).reshape(-1))),
    "bv": (64, lambda i: rows(i["L1_attn_bv"])),
    "g1w": (64, lambda i: tm(i["L1_ffn_gate_w"].T)),
    "g1b": (16, lambda i: rows(i["L1_ffn_expert_bias"])),
    "wr": (32, lambda i: tm(i["L2_ffn_Wr"])),
    "br": (8, lambda i: rows(i["L2_ffn_br"])),
    "bern": (16, lambda i: rows(i["L3_attn_bern_u"])),
    "g3w": (260, lambda i: tm(np.concatenate([i["L3_ffn_gate_w"], i["L3_ffn_sh_gate1_w"]]))),
}



class Tok:

    def __init__(self, sem, val):
        self.sem, self.val = sem, val


class Eng:

    def __init__(self, name, sem):
        self.name, self.sem, self.n, self.q, self.met = name, sem, 0, [], {}

    def wait(self, *toks):
        for t in toks:
            if t is None:
                continue
            if isinstance(t, (list, tuple)):
                self.wait(*t)
                continue
            if self.met.get(id(t.sem), 0) < t.val:
                self.met[id(t.sem)] = t.val
                self.q.append((t, None, False))

    def do(self, fn, *toks, inc=True):
        self.wait(*toks)
        self.q.append((None, fn, inc))
        if inc:
            self.n += 1
            return Tok(self.sem, self.n)

    def now(self):
        return Tok(self.sem, self.n) if self.n else None

    def flush(self, eng):
        for t, fn, inc in self.q:
            if t is not None:
                eng.wait_ge(t.sem, t.val)
            else:
                i = fn(eng)
                if inc:
                    i.then_inc(self.sem, 1)


class Piece:
    def __init__(self, ap, tok, n, pack):
        self.ap, self.tok, self.n, self.pack, self.rel = ap, tok, n, pack, None


def pipeline(n, *stages, beside=None):
    for t in range(n + len(stages) - 1):
        for s in range(len(stages) - 1, -1, -1):
            if 0 <= t - s < n:
                stages[s](t - s)
        if beside:
            beside(t)


def run(steps, n=1):
    for _ in range(min(n, len(steps))):
        f = steps.pop(0)
        if f:
            f()


def wants(layers, n):
    return (5 if n == 28 else 11) in layers


def bc(ap, shape, axis=1):
    return ap.unsqueeze(axis).to_broadcast(shape)


class Program:
    def __init__(self, nc, stack, layers):
        self.nc, self.layers = nc, layers
        en = stack.enter_context
        self.sem = lambda name: en(nc.semaphore(name))
        self.pe, self.act, self.dve, self.pool = (Eng(n, self.sem("s_" + n)) for n in ("pe", "act", "dve", "pool"))
        self.sp = Eng("sp", self.sem("s_sp"))
        sb = lambda name, n: en(nc.sbuf_tensor(name, [128, n], F32))
        self.ring = sb("W", RING * SLOT)
        self.wsem = [self.sem(f"s_w{i}") for i in range(RING)]
        self.loads = []
        self.consts = shape_constants()
        self.cw = sum(v.shape[1] for v in self.consts.values()) + sum(n for n, _ in PARAMS.values())
        self.C = sb("C", self.cw)
        self.c, at = {}, 0
        for k, v in self.consts.items():
            self.c[k] = self.C[:, at:at + v.shape[1]]
            at += v.shape[1]
        for k, (n, _) in PARAMS.items():
            self.c[k] = self.C[:, at:at + n]
            at += n
        self.X = sb("X", 4 * T)
        self.x = self.X[:, :].rearrange("p (c t) -> p c t", c=4)
        self.CX = sb("CX", T)
        self.KF = sb("KF", NB * L)
        self.KT = sb("KT", NB * 3 * 128)
        self.A = sb("A", ARENA)
        self.small = sb("small", 832)
        self.P = [en(nc.psum_tensor(f"P{i}", [128, 512], F32)) for i in range(8)]
        self.drained = [None] * 8
        self.nb = 0
        self.s_in = [self.sem(f"s_in{i}") for i in range(5)]
        self.s_out = self.sem("s_out")
        self.ic, self.ix, self.ik, self.ik2, self.ic2 = (Tok(s, 16) for s in self.s_in)
        self.xt = [self.ix, self.ix]
        self.sums, self.squares, self.scales = self.ar(18400, 4, T), self.ar(21600, 4, T), self.ar(24800, T)
        self.gsem = [self.sem(f"s_g{i}") for i in range(16)]
        self.ssem = [self.sem(f"s_s{i}") for i in range(4)]
        self.ng = self.ns = 0
        dram = lambda name, shape, dt, kind: nc.dram_tensor(name, shape, dt, kind=kind).ap()
        self.XD = dram("x_by_token", [T, 512], F32, "Internal")
        self.YD = {n: dram(f"slot_outputs{n}", [128 * n, 512], F32, "Internal") for n in (28, 113) if wants(layers, n)}
        self.E1 = dram("experts1", [16 * 128, 3072], F32, "ExternalInput")
        self.E3 = dram("experts3", [64 * 128, 1536], F32, "ExternalInput")

    def ar(self, at, *shape):
        n = int(np.prod(shape))
        assert at + n <= ARENA, (at, n)
        v = self.A[:, at:at + n]
        if len(shape) == 2:
            return v.rearrange("p (a b) -> p a b", a=shape[0])
        if len(shape) == 3:
            return v.rearrange("p (a b c) -> p a b c", a=shape[0], b=shape[1])
        return v

    def load(self, n, pack):
        assert n <= SLOT
        i = len(self.loads)
        s = i % RING
        if i >= RING:
            assert self.loads[i - RING].rel is not None, "the ring's slot is not released"
        p = Piece(self.ring[:, s * SLOT:s * SLOT + n], Tok(self.wsem[s], 16 * (i // RING + 1)), n, pack)
        self.loads.append(p)
        return p

    def bank(self):
        self.nb += 1
        return (self.nb - 1) % 8

    def barrier(self):
        es = (self.pe, self.act, self.dve, self.pool)
        now = [e.now() for e in es]
        for e in es:
            e.wait(*now)

    def mm(self, out, lhsT, rhs, start, stop, *toks, inc=False):
        return self.pe.do(lambda e: e.matmul(out, lhsT, rhs, start=start, stop=stop), *toks, inc=inc)

    def tr(self, out, in_, n, *toks, inc=False):
        idn = self.c["ident"][0:n, 0:n]
        return self.pe.do(lambda e: e.transpose(out, in_, idn), *toks, inc=inc)

    def chain(self, out, pairs, *toks):
        self.pe.wait(*toks)
        n = len(pairs)
        for i, (a, b) in enumerate(pairs):
            t = self.mm(out, a, b, i == 0, i == n - 1, inc=i == n - 1)
        return t

    def copy(self, eng, out, in_, *toks):
        if eng is self.act:
            return eng.do(lambda e: e.activation(out, in_, ACT.Copy), *toks)
        return eng.do(lambda e: e.tensor_copy(out, in_), *toks)

    def af(self, out, in_, func, *toks, **kw):
        return self.act.do(lambda e: e.activation(out, in_, func, **kw), *toks)

    def tt(self, out, a, b, op, *toks, eng=None):
        return (eng or self.dve).do(lambda e: e.tensor_tensor(out, a, b, op), *toks)

    def ts(self, out, a, s1, s2, o0, o1, *toks, eng=None):
        if o1 is None:
            return (eng or self.dve).do(lambda e: e.tensor_scalar(out, a, s1, None, o0), *toks)
        return (eng or self.dve).do(lambda e: e.tensor_scalar(out, a, s1, s2, o0, o1), *toks)

    def stt(self, out, a, s, b, o0, o1, *toks):
        return self.dve.do(lambda e: e.scalar_tensor_tensor(out=out, in0=a, scalar=s, in1=b, op0=o0, op1=o1), *toks)

    def rec(self, out, a, *toks):
        return self.dve.do(lambda e: e.reciprocal(out, a), *toks)

    def red(self, out, a, op, *toks, negate=None):
        return self.dve.do(lambda e: e.tensor_reduce(out, a, AX.X, op, negate=negate), *toks)

    def hs(self, h):
        return slice(H2 * h, H2 * h + H2)

    def tiles_sum(self, sq, src, h, *toks):
        hs = self.hs(h)
        t = self.tt(sq[:, 0:2, hs], src[:, 0:2, hs], src[:, 2:4, hs], ALU.add, *toks)
        return self.tt(sq[:, 0, hs], sq[:, 0, hs], sq[:, 1, hs], ALU.add, t)

    def mean(self, sq, h, t):
        b = self.bank()
        self.pe.wait(self.drained[b])
        return b, self.mm(self.P[b][:, 0:H2], self.c["mean"], sq[:, 0, self.hs(h)], True, True, t, self.ic, inc=True)

    def deviation(self, sq, rs, eps, h, t):
        hs = self.hs(h)
        b, t = self.mean(sq, h, t)
        t = self.af(rs[:, hs], self.P[b][:, 0:H2], ACT.Sqrt, t, bias=self.c["eps"][:, eps:eps + 1])
        self.drained[b] = t
        return self.rec(rs[:, hs], rs[:, hs], t)

    def squares_sum(self, src, sq, h, *toks):
        hs = self.hs(h)
        t = self.af(sq[:, :, hs], src[:, :, hs], ACT.Square, *toks)
        return self.tiles_sum(sq, sq, h, t)

    def rms_steps(self, a4, sq, rs, h, t, finish):
        hs = self.hs(h)
        v = {}

        def square():
            v[0] = self.squares_sum(a4, sq, h, t())

        def scale():
            a = self.deviation(sq, rs, 0, h, v[0])
            finish(h, self.tt(a4[:, :, hs], a4[:, :, hs], bc(rs[:, hs], [128, 4, H2]), ALU.mult, a))
        return square, scale

    def norm_steps(self, z, sq, rs, zt, h):
        hs = self.hs(h)
        x3 = [128, 4, H2]
        t = {}

        def add():
            t[0] = self.tiles_sum(sq, z, h, zt[h], self.pe.now())

        def centre():
            b, a = self.mean(sq, h, t[0])
            a = self.tt(z[:, :, hs], z[:, :, hs], bc(self.P[b][:, 0:H2], x3), ALU.subtract, a)
            self.drained[b] = a
            t[1] = self.squares_sum(z, sq, h, a)

        def scale():
            a = self.deviation(sq, rs, 1, h, t[1])
            self.xt[h] = self.tt(self.x[:, :, hs], z[:, :, hs], bc(rs[:, hs], x3), ALU.mult, a, self.pe.now())
        return add, centre, scale

    def norms(self, z, sq, rs, zt):
        (a0, c0, s0), (a1, c1, s1) = (self.norm_steps(z, sq, rs, zt, h) for h in range(2))
        return [a0, c0, None, s0], [a1, c1, None, s1]

    def project(self, w, rhs, rt, kc, ms, evac, wt=None, beside=((), ()), halves=(0, 1)):
        for h in halves:
            for m in ms:
                b = self.bank()
                self.pe.wait(self.drained[b])
                t = self.chain(self.P[b][:, 0:H2], [(w(m, k), rhs(k, h)) for k in range(kc)], rt[h], wt)
                self.drained[b] = evac(m, h, self.P[b][:, 0:H2], t)
                run(beside[h])
            run(beside[h], len(beside[h]))
        return self.pe.now()

    def full(self, name, sel, src, rt, evac, nm=4, beside=((), ())):
        for g in range(0, nm, 4):
            p = self.load(2048, lambda i, g=g: fm(sel(i[name])[g * 128:(g + 4) * 128]))
            w = p.ap.rearrange("p (m k c) -> p m k c", m=4, k=4)
            p.rel = self.project(lambda m, k: w[:, m - g, k, :], lambda k, h: src[:, k, self.hs(h)], rt, 4,
                                 range(g, g + 4), evac, p.tok, beside)

    def add_residual(self, z, zt):
        def evac(m, h, ps, t):
            zt[h] = self.tt(z[:, m, self.hs(h)], ps, self.x[:, m, self.hs(h)], ALU.add, t)
            return zt[h]
        return evac

    def l0_attn(self, tail):
        run(tail, len(tail))
        self.barrier()
        x = self.x
        SQ, R, XN = self.squares, self.scales, self.ar(0, 4, T)
        self.dve.wait(self.ic)
        Q, Kk, V = self.ar(3200, 4, T), self.ar(6400, 4, T), self.ar(9600, 4, T)
        KV = self.ar(12800, 4, T)
        xn = [None, None]
        for h in range(2):
            hs = self.hs(h)
            t = self.deviation(SQ, R, 0, h, self.squares_sum(x, SQ, h, self.xt[h]))
            xn[h] = self.tt(XN[:, :, hs], x[:, :, hs], bc(R[:, hs], [128, 4, H2]), ALU.mult, t)
        dst = [Q, Kk, V]
        done = {}

        def evac(m, h, ps, t):
            t = self.copy(self.dve if m in (4, 6) else self.act, dst[m // 4][:, m % 4, self.hs(h)], ps, t)
            done.setdefault((m // 4, h), []).append(t)
            return t
        tq, tk, tw = {}, {}, {}

        def q_end(h, t):
            tq[h] = self.af(Q[:, :, self.hs(h)], Q[:, :, self.hs(h)], ACT.Sigmoid, t)

        def k_end(h, t):
            hs = self.hs(h)
            tk[h] = self.af(Kk[:, :, hs], Kk[:, :, hs], ACT.Exp, t)

        def total(h, c):
            kv = KV[:, c, self.hs(h)]
            t = scan(kv, Kk[:, c, self.hs(h)], tk[h])
            t = self.ts(kv, kv, 1e-6, None, ALU.add, None, t)
            tw[h] = self.rec(kv, kv, t)

        def scan(out, src, *toks):
            return self.dve.do(lambda e: e.tensor_tensor_scan(out, self.c["restart"], src, 0.0, ALU.mult, ALU.add), *toks)

        def piece(g, beside=((), ())):
            p = self.load(2048, lambda i: fm(i["L0_attn_w_qkv"][g * 512:(g + 1) * 512]))
            w = p.ap.rearrange("p (m k c) -> p m k c", m=4, k=4)
            p.rel = self.project(lambda m, k: w[:, m - 4 * g, k, :], lambda k, h: XN[:, k, self.hs(h)], xn, 4,
                                 range(4 * g, 4 * g + 4), evac, p.tok, beside)
        yt, vt = [None, None], [None, None]
        v3 = lambda a, h: a[:, :, self.hs(h)]

        def weigh(h):
            t = self.tt(v3(V, h), v3(V, h), v3(Kk, h), ALU.mult, done[2, h], tk[h])
            for c in range(4):
                t = scan(V[:, c, self.hs(h)], V[:, c, self.hs(h)], t)
            vt[h] = self.tt(v3(V, h), v3(V, h), v3(KV, h), ALU.mult, t, tw[h])

        def gated(h):
            yt[h] = self.tt(v3(XN, h), v3(V, h), v3(Q, h), ALU.mult, vt[h], tq[h], self.pe.now())
        (k0, k1), (k2, k3) = (self.rms_steps(Kk, SQ, R, h, lambda h=h: done[1, h], k_end) for h in range(2))
        (q0, q1), (q2, q3) = (self.rms_steps(Q, SQ, R, h, lambda h=h: [done[0, h], self.pe.now()], q_end) for h in range(2))
        piece(1)
        t0, t1 = ([lambda c=c, h=h: total(h, c) for c in range(4)] for h in range(2))
        piece(2, ([k0, None, k1, k2], [t0[0], k3, t0[1], t0[2]]))
        piece(0, ([t0[3], lambda: weigh(0)], [q0, q1, lambda: gated(0), q2]))
        H = self.ar(3200, 16, T)
        G = self.ar(16000, 2, H2)
        ht = [None, None]
        gfree = [None, None]
        n = 0
        keys = t1 + [lambda: weigh(1), q3, lambda: gated(1)] + [lambda b=b: self.prep(b) for b in range(NB)]
        for g0 in (0, 4):
            ps = [self.load(2048, lambda i, g=g: np.concatenate(
                [fm(i["L0_attn_w_swiglu"][256 * g:256 * g + 256]), fm(i["L0_attn_w_swiglu"][2048 + 256 * g:2304 + 256 * g])], 1))
                for g in range(g0, g0 + 4)]
            for h in range(2):
                hs = self.hs(h)
                for g in range(g0, g0 + 4):
                    p = ps[g - g0]
                    w = p.ap.rearrange("p (m k c) -> p m k c", m=4, k=4)
                    for m in range(2):
                        bu, bg = self.bank(), self.bank()
                        self.pe.wait(self.drained[bu], self.drained[bg])
                        tu = self.chain(self.P[bu][:, 0:H2], [(w[:, m, k, :], XN[:, k, hs]) for k in range(4)], yt[h], p.tok)
                        tg = self.chain(self.P[bg][:, 0:H2], [(w[:, 2 + m, k, :], XN[:, k, hs]) for k in range(4)])
                        t = self.af(G[:, n % 2, :], self.P[bg][:, 0:H2], ACT.Silu, tg, gfree[n % 2])
                        self.drained[bg] = t
                        t = self.tt(H[:, 2 * g + m, hs], self.P[bu][:, 0:H2], G[:, n % 2, :], ALU.mult, tu, t)
                        self.drained[bu] = gfree[n % 2] = ht[h] = t
                        n += 1
                        run(keys)
                    if h == 1:
                        p.rel = self.pe.now()
        run(keys, len(keys))
        Z, zt = self.sums, [None, None]
        ps = [self.load(2048, lambda i, m=m: fm(i["L0_attn_w_out"][128 * m:128 * m + 128])) for m in range(4)]

        def evac(m, h, pt, t):
            zt[h] = self.stt(Z[:, m, self.hs(h)], x[:, m, self.hs(h)], 2.0, pt, ALU.mult, ALU.add, t)
            return zt[h]
        first, tail = self.norms(Z, SQ, R, zt)
        rel = self.project(lambda m, k: ps[m].ap[:, 128 * k:128 * k + 128], lambda k, h: H[:, k, self.hs(h)], ht, 16,
                           range(4), evac, [p.tok for p in ps], ([], first))
        for p in ps:
            p.rel = rel
        return tail

    def heads32(self, qt, keys, kd, V, vt, nk, mask, at, out, group, early, late, special=None):
        scale = float(np.float32(1.0) / np.sqrt(np.float32(32)))
        NE = 4
        nt = keys.shape[1]
        E = [self.ar(at + 16 * nk * i, 16, nk) for i in range(NE)]
        PT = [self.ar(at + 16 * nk * NE + 1600 * i, 16, S) for i in range(2)]
        KB = [self.ar(at + 16 * nk * NE + 3200 + 4 * nt * nk * i, nt, 4, nk) for i in range(2)]
        M = [self.small[:, 96 * i:96 * i + 96] for i in range(6)]
        st = {}

        clear = [self.pool.do(lambda e, kb=kb: e.memset(kb.rearrange("p a b c -> p (a b c)"), 0.0), self.xt[1]) for kb in KB]

        def spread(b):
            for j in range(4):
                rs = slice(32 * j, 32 * j + 32)
                t = self.copy(self.pool, KB[b % 2][rs, :, j, :], keys[rs, :, nk * b:nk * b + nk], st.get(("s", b - 2)),
                              clear, kd)
            st["kb", b] = t

        def scores(b):
            e, m = E[b % NE], M[b % 6]
            prev = st.get(("pt", b - NE))
            for g in range(4):
                k = self.bank()
                self.pe.wait(self.drained[k])
                t = self.mm(self.P[k][0:S, 0:4 * nk], qt[:, g, S * b:S * b + S],
                            KB[b % 2][:, g * nt // 4, :, :], True, True, st["kb", b], inc=True)
                st["s", b] = t
                o = e[0:S, 4 * g:4 * g + 4, :]
                ps = self.P[k][0:S, 0:4 * nk].rearrange("p (a b) -> p a b", a=4)
                if mask is None:
                    t = self.copy(self.dve, o, ps, t, prev)
                else:
                    t = self.tt(o, ps, bc(mask[0:S, 0:nk], [S, 4, nk]), ALU.add, t, prev)
                self.drained[k] = t
            t = self.red(m[0:S, 0:16], e[0:S, :, 0:nk], ALU.max, t, negate=True)
            st["m", b] = self.ts(m[0:S, 0:16], m[0:S, 0:16], scale, None, ALU.mult, None, t)

        def exps(b):
            e, m = E[b % NE], M[b % 6]
            for h in range(16):
                t = self.af(e[0:S, h, 0:nk], e[0:S, h, 0:nk], ACT.Exp, st["m", b], scale=scale, bias=m[0:S, h:h + 1],
                            accum_out=m[0:S, 16 + h:17 + h])
            st["e", b] = t

        def shares(b):
            e, m = E[b % NE], M[b % 6]
            t = self.rec(m[0:S, 80:96], m[0:S, 16:32], st["e", b])
            if special is not None:
                t = special[0](e, m, t)
                t = special[1](e, m, t)
            v = e[0:S, :, 0:nk]
            st["e", b] = self.tt(v, v, bc(m[0:S, 80:96], [S, 16, nk], 2), ALU.mult, t)

        def turn(b):
            e, pt = E[b % NE], PT[b % 2]
            for g in range(4):
                k = self.bank()
                self.pe.wait(self.drained[k])
                ps = self.P[k][0:nk, 0:4 * S].rearrange("p (a b) -> p a b", a=4)
                for j in range(4):
                    t = self.tr(ps[:, j, :], e[0:S, 4 * g + j, 0:nk], S, st["e", b], inc=j == 3)
                st["pt", b] = t
                t = self.copy(self.act if g % 2 else self.dve, pt[0:nk, 4 * g:4 * g + 4, :], ps, t, st.get(("pv", b - 2)))
                self.drained[k] = t
                st["c", b, g] = t

        def values(b):
            pt = PT[b % 2]
            k = self.bank()
            self.pe.wait(self.drained[k])
            for g in range(4):
                for j in range(4):
                    h = 4 * g + j
                    t = self.mm(self.P[k][32 * j:32 * j + 32, S * g:S * g + S], V[0:nk, b, h // group, :], pt[0:nk, h, :],
                                True, True, st["c", b, g], vt(b), inc=h == 15)
            st["pv", b] = t
            t = self.copy(self.act, out[:, :, S * b:S * b + S], self.P[k][:, 0:4 * S].rearrange("p (a b) -> p a b", a=4), t)
            self.drained[k] = t
            ot[b // 4] = t
        ot = [None, None]
        tail = late(ot)

        def beside(t):
            run(early, 2)
            if t >= 8:
                run(tail)
        pipeline(NB, spread, scores, exps, shares, turn, values, beside=beside)
        run(tail, len(tail))
        return ot

    def values_tm(self, V, w, p, src, rt, bias=None, nk=S):
        vt = {}
        nc_ = 4 if w(1) is not None else 1

        def step(b):
            k = self.bank()
            self.pe.wait(self.drained[k])
            n = w(0).shape[-1]
            t = self.chain(self.P[k][0:nk, 0:n], [(src(c, b), w(c)) for c in range(nc_)], rt[b // 4], p.tok)
            ps = self.P[k][0:nk, 0:n].rearrange("p (a b) -> p a b", b=32)
            if b == NB - 1:
                p.rel = t
            if bias is None:
                t = self.copy(self.act, V[0:nk, b, :, :], ps, t)
            else:
                t = self.tt(V[0:nk, b, :, :], ps, bias[0:nk, :].rearrange("p (a b) -> p a b", b=32), ALU.add, t)
            self.drained[k] = vt[b] = t
        return [lambda b=b: step(b) for b in range(NB)], lambda b: vt[b]

    def xattn(self, pre, tail):
        Q, Kk, V = self.ar(0, 4, T), self.ar(3200, 4, T), self.ar(6400, NB, 16 * 32)
        V = V.rearrange("p b (h d) -> p b h d", h=16)
        cx = self.CX
        p = self.load(1024, lambda i: np.concatenate([fm(i[pre + "Wkv_expand"][:512]), tm(i[pre + "Wkv_expand"][512:])], 1))
        wk = p.ap[:, 0:512].rearrange("p (m c) -> p m c", m=4)
        wv = p.ap[:, 512:1024]
        kd, qd = [], []

        def ek(m, h, ps, t):
            t = self.copy(self.act, Kk[:, m, self.hs(h)], ps, t)
            kd.append(t)
            return t

        def eq(m, h, ps, t):
            t = self.copy(self.dve, Q[:, m, self.hs(h)], ps, t)
            qd.append(t)
            return t
        self.project(lambda m, k: wk[:, m, :], lambda k, h: cx[:, self.hs(h)], [self.ik, self.ik], 1, range(4), ek, p.tok,
                     (tail, []))
        early, vt = self.values_tm(V, lambda c: wv if c == 0 else None, p, lambda c, b: cx[:, S * b:S * b + S],
                                   [self.ik, self.ik])
        self.full(pre + "Wq", lambda w: w, self.x, self.xt, eq)
        self.pe.wait(qd[-1])
        OT = self.ar(10624, 4, T)
        late, rest = self.out_proj(pre + "Wout", OT)
        return rest(self.heads32(Q, Kk, kd[-1], V, vt, S, self.c["causal"], 13824, OT, 1, early, late))

    def out_proj(self, name, OT):
        Z, zt = self.ar(0, 4, T), [None, None]
        evac = self.add_residual(Z, zt)
        v = {}

        def half(ot, ms, h, beside=((), ())):
            return self.project(lambda m, k: v["w"][:, m, k, :], lambda k, h: OT[:, k, self.hs(h)], ot, 4, ms, evac,
                                v["p"].tok, beside, [h])

        def late(ot):
            p = v["p"] = self.load(2048, lambda i: fm(i[name]))
            v["w"] = p.ap.rearrange("p (m k c) -> p m k c", m=4, k=4)
            return [lambda m=m: half(ot, [m], 0) for m in range(4)]

        def rest(ot):
            first, tail = self.norms(Z, self.squares, self.scales, zt)
            v["p"].rel = half(ot, range(4), 1, ([], first))
            return tail
        return late, rest

    def rope(self, src, n, cos, sin, tmp, st, end):
        def step(m, h):
            hs = self.hs(h)
            b = self.bank()
            self.pe.wait(self.drained[b])
            t = self.mm(self.P[b][:, 0:H2], self.c["swap32"], src[:, m, hs], True, True, st[m, h], inc=True)
            s4 = src[:, m, hs].rearrange("p (b s) -> p b s", b=4)
            p4 = self.P[b][:, 0:H2].rearrange("p (b s) -> p b s", b=4)
            tm4 = tmp[:, self.hs(h)].rearrange("p (b s) -> p b s", b=4)
            t1 = self.tt(tm4, p4, bc(sin, [128, 4, S]), ALU.mult, t)
            self.drained[b] = t1
            t2 = self.tt(s4, s4, bc(cos, [128, 4, S]), ALU.mult, t)
            end[0] = self.tt(s4, s4, tm4, ALU.add, t1, t2)
        return [lambda m=m, h=h: step(m, h) for m in range(n) for h in range(2)]

    def l1_attn(self, tail):
        pre = "L1_attn_"
        Q, Kk, V = self.ar(0, 4, T), self.ar(3200, 2, T), self.ar(6400, NB, 64)
        V = V.rearrange("p b (h d) -> p b h d", h=2)
        p = self.load(1280, lambda i: np.concatenate(
            [fm(np.tile(i[pre + "wk"].reshape(2, 1, 32, 512), (1, 4, 1, 1)).reshape(256, 512)), tm(i[pre + "wv"])], 1))
        wk = p.ap[:, 0:1024].rearrange("p (m k c) -> p m k c", m=2, k=4)
        wv = p.ap[:, 1024:1280].rearrange("p (k c) -> p k c", k=4)
        kd, qd = {}, {}

        def ek(m, h, ps, t):
            kd[m, h] = self.af(Kk[:, m, self.hs(h)], ps, ACT.Identity, t, bias=self.c["bk"][:, m:m + 1])
            return kd[m, h]

        def eq(m, h, ps, t):
            qd[m, h] = self.af(Q[:, m, self.hs(h)], ps, ACT.Identity, t, bias=self.c["bq"][:, m:m + 1])
            return qd[m, h]
        self.project(lambda m, k: wk[:, m, k, :], lambda k, h: self.x[:, k, self.hs(h)], self.xt, 4, range(2), ek, p.tok,
                     (tail, []))
        early, vt = self.values_tm(V, lambda c: wv[:, c, :], p, lambda c, b: self.x[:, c, S * b:S * b + S],
                                   self.xt, bias=self.c["bv"])
        tmp, tk, tq = self.ar(9700, T), [None], [None]
        self.full(pre + "wq", lambda w: w, self.x, self.xt, eq,
                  beside=([], self.rope(Kk, 2, self.c["cos1"], self.c["sin1"], tmp, kd, tk)))
        for f in zip(early, self.rope(Q, 4, self.c["cos1"], self.c["sin1"], tmp, qd, tq)):
            run(list(f), 2)
        self.pe.wait(tq[0])
        OT = self.ar(10624, 4, T)
        late, rest = self.out_proj(pre + "wo", OT)
        return rest(self.heads32(Q, Kk, tk[0], V, vt, S, self.c["causal"], 13824, OT, 8, [], late))

    def l2_attn(self, tail):
        pre = "L2_attn_"
        Q, Kk, V = self.ar(0, 4, T), self.ar(3200, 4, T), self.ar(6400, NB, 16 * 32)
        V = V.rearrange("p b (h d) -> p b h d", h=16)
        dst, done = [Q, Kk], []

        def evac(m, h, ps, t):
            t = self.copy(self.act, dst[m // 4][:, m % 4, self.hs(h)], ps, t)
            done.append(t)
            return t
        self.full(pre + "W_qkv", lambda w: w[:1024], self.x, self.xt, evac, 8, (tail, []))
        p = self.load(2048, lambda i: tm(i[pre + "W_qkv"][1024:]))
        wv = p.ap.rearrange("p (k c) -> p k c", k=4)
        early, vt = self.values_tm(V, lambda c: wv[:, c, :], p, lambda c, b: self.x[:, c, S * b:S * b + S], self.xt)
        self.pe.wait(done[-1])
        OT = self.ar(10624, 4, T)
        late, rest = self.out_proj(pre + "W_proj", OT)
        return rest(self.heads32(Q, Kk, done[-1], V, vt, S, self.c["causal"], 13824, OT, 1, early, late))

    def l3_attn(self, tail):
        pre = "L3_attn_"
        SB, NK = 10, 60
        Q, Kk, V = self.ar(0, 4, T), self.ar(3200, 4, T), self.ar(6400, NB, 16 * 32)
        V = V.rearrange("p b (h d) -> p b h d", h=16)
        dst, done = [Q, Kk], {}

        def evac(m, h, ps, t):
            done[m, h] = self.copy(self.act, dst[m // 4][:, m % 4, self.hs(h)], ps, t)
            return done[m, h]
        self.full(pre + "wk", lambda w: w, self.x, self.xt, lambda m, h, ps, t: evac(m + 4, h, ps, t), 4, (tail, []))
        XK = self.ar(12544, 4, NB * NK).rearrange("p c (b k) -> p c b k", b=NB)
        xs = self.x.rearrange("p c (b s) -> p c b s", b=NB)
        tx = []
        for c in range(4):
            tx.append(self.copy(self.pool, XK[:, c, :, 0:SB], xs[:, c, :, 0:SB], self.xt))
            tx.append(self.copy(self.pool, XK[:, c, :, SB:NK], xs[:, c, :, 50:S], self.xt))
        tmp, tk, tq = self.ar(14464, T), [None], [None]
        sel = lambda o: {(m, h): done[m + o, h] for m in range(4) for h in range(2)}
        steps = self.rope(Kk, 4, self.c["cos3"], self.c["sin3"], tmp, sel(4), tk)
        self.full(pre + "wq", lambda w: w, self.x, self.xt, evac, 4, (steps[:4], steps[4:]))
        KS = self.ar(10624, 4, NB * NK).rearrange("p c (b k) -> p c b k", b=NB)
        ks = Kk.rearrange("p c (b s) -> p c b s", b=NB)
        for c in range(4):
            self.copy(self.pool, KS[:, c, :, 0:SB], ks[:, c, :, 0:SB], tk[0])
            t2 = self.copy(self.pool, KS[:, c, :, SB:NK], ks[:, c, :, 50:S])
        p = self.load(2048, lambda i: tm(i[pre + "wv"]))
        wv = p.ap.rearrange("p (k c) -> p k c", k=4)
        early, vt = self.values_tm(V, lambda c: wv[:, c, :], p, lambda c, b: XK[:, c, b, :], [tx, tx], nk=NK)
        for f in zip(early, self.rope(Q, 4, self.c["cos3"], self.c["sin3"], tmp, sel(0), tq)):
            run(list(f), 2)
        self.pe.wait(tq[0])
        OT = self.ar(3200, 4, T)

        def special(e, m, t):
            a, r, w = (m[0:S, i:i + 16] for i in (48, 32, 80))
            t = self.red(r, e[0:S, :, SB + 1:NK], ALU.add, t)
            t = self.tt(a, r, w, ALU.mult, t)
            t = self.ts(a, a, 1.0 / 49, 1e-6, ALU.mult, ALU.add, t)
            t = self.rec(a, a, t)
            t = self.tt(a, a, w, ALU.mult, t)
            t = self.tt(a, a, e[0:S, :, SB], ALU.mult, t)
            t = self.ts(a, a, 0.0, 1.0, ALU.max, ALU.min, t)
            return self.tt(a, self.c["bern"][0:S, :], a, ALU.is_lt, t)

        def special2(e, m, t):
            a, r, u = (m[0:S, i:i + 16] for i in (48, 32, 64))
            e50 = e[0:S, :, SB]
            k = self.bank()
            self.pe.wait(self.drained[k])
            t = self.mm(self.P[k][0:S, 0:16], self.c["lastrow"][0:S, :], a, True, True, t, inc=True)
            t = self.stt(u, self.P[k][0:S, 0:16], 1.0 / 50, r, ALU.mult, ALU.mult, t)
            self.drained[k] = t
            return self.tt(e50, e50, u, ALU.add, t)
        late, rest = self.out_proj(pre + "wo", OT)
        return rest(self.heads32(Q, KS.rearrange("p c b k -> p c (b k)"), t2, V, vt, NK, None, 15264, OT, 1, [], late,
                                 (special, special2)))

    def prep(self, b):
        CF = self.ar(17000, NB, L)
        kf = self.KF[:, :].rearrange("p (b l) -> p b l", b=NB)
        kt = self.KT[:, :].rearrange("p (b j d) -> p b j d", b=NB, j=3)
        tmp = self.ar(17000 + NB * L, 2, L)
        k = self.bank()
        self.pe.wait(self.drained[k])
        t = self.mm(self.P[k][:, 0:L], self.c["swap128"], CF[:, b, :], True, True, self.ik2, self.ic2, inc=True)
        t1 = self.tt(tmp[:, b % 2, :], self.P[k][:, 0:L], self.c["sink"], ALU.mult, t)
        self.drained[k] = t1
        t2 = self.tt(kf[:, b, :], CF[:, b, :], self.c["cosk"], ALU.mult, t)
        t = self.tt(kf[:, b, :], kf[:, b, :], tmp[:, b % 2, :], ALU.add, t1, t2)
        k = self.bank()
        self.pe.wait(self.drained[k])
        ps = self.P[k][:, 0:384].rearrange("p (j d) -> p j d", j=3)
        for j in range(3):
            n = min(128, L - 128 * j)
            t3 = self.tr(ps[0:n, j, :], kf[:, b, 128 * j:128 * j + n], 128, t, inc=j == 2)
        self.copy(self.act, kt[:, b, 0:2, :], ps[:, 0:2, :], t3)
        self.drained[k] = self.copy(self.act, kt[0:L - 256, b, 2, :], ps[0:L - 256, 2, :])

    def mla(self, pre, roped, tail):
        kf = self.KF[:, :].rearrange("p (b l) -> p b l", b=NB)
        kt = self.KT[:, :].rearrange("p (b j d) -> p b j d", b=NB, j=3)
        x = self.x
        Z = self.sums
        QE = [self.ar(3200 * i, 4, T) for i in range(2)]
        CT = self.ar(6400, 4, T)
        QH = self.ar(9600, 2, T)
        PQ = self.ar(11200, 2, 384)
        MH = self.ar(12736, 2, 128)
        Pm = self.ar(12992, 2, 4 * L)
        PT = self.ar(12992 + 8 * L, 2, 3 * H2)
        QB = self.ar(21600, 2, 2400)
        sm = self.small
        perm = q384() if roped else np.arange(384)
        zt = [None, None]
        st = {}

        def head(h):
            hg, hh = h // 4, h % 4
            v = {}

            def weights():
                if hh == 0:
                    st["wq"] = self.load(2048, lambda i: fm(i[pre + "Wq"][512 * hg:512 * hg + 512]))
                p = self.load(896, lambda i: pad_rows(
                    [i[pre + "W_qr"][h][perm].T, i[pre + "W_kr"][h].T,
                     i[pre + "w_kc_q"][h][:, perm] if roped else
                     i[pre + "w_kc_q"][h].T.reshape(3, 128, 128).transpose(1, 0, 2).reshape(128, 384)]))
                w1, w3, v["w4"] = p.ap[:, 0:384], p.ap[:, 384:512], p.ap[:, 512:896]
                v["p"] = p
                pq = v["pq"] = PQ[:, h % 2, :].rearrange("p (j d) -> p j d", j=3)
                k = self.bank()
                self.pe.wait(self.drained[k])
                ps = self.P[k][:, 0:384].rearrange("p (j d) -> p j d", j=3)
                for j in range(3):
                    t = self.mm(ps[:, j, :], w1[:, 128 * j:128 * j + 128], w3, True, True, p.tok, inc=j == 2)
                self.drained[k] = v["tp"] = self.copy(self.act, pq, ps, t)

            def queries(hf):
                wq = st["wq"]
                wqt = wq.ap.rearrange("p (m k c) -> p m k c", m=4, k=4)
                hs = self.hs(hf)
                if hf:
                    run(tail, len(tail))
                k = self.bank()
                self.pe.wait(self.drained[k])
                t = self.chain(self.P[k][:, 0:H2], [(wqt[:, hh, c, :], x[:, c, hs]) for c in range(4)], self.xt[hf], wq.tok)
                self.drained[k] = v["q", hf] = self.copy(self.act, QH[:, h % 2, hs], self.P[k][:, 0:H2], t)
                run(tail)
                if hf and hh == 3:
                    wq.rel = t

            def plain():
                w4j = v["w4"].rearrange("p (j c) -> p j c", j=3)
                k = self.bank()
                self.pe.wait(self.drained[k])
                t = self.chain(self.P[k][:, 0:128], [(w4j[:, j, :], v["pq"][:, j, :]) for j in range(3)], v["tp"])
                self.drained[k] = tm_ = self.copy(self.dve, MH[:, h % 2, :], self.P[k][:, 0:128], t)
                for hf in range(2):
                    hs = self.hs(hf)
                    k = self.bank()
                    self.pe.wait(self.drained[k])
                    t = self.mm(self.P[k][:, 0:H2], MH[:, h % 2, :], QH[:, h % 2, hs], True, True, tm_, v["q", hf], inc=True)
                    self.drained[k] = st["qe", h, hf] = self.copy(self.dve, QE[hg % 2][:, hh, hs], self.P[k][:, 0:H2], t)
                v["p"].rel = t

            def big(hf):
                w4j = v["w4"].rearrange("p (j c) -> p j c", j=3)
                qb = QB[:, hf, :].rearrange("p (s j t) -> p s j t", s=2, j=3)
                for j in range(3):
                    k = self.bank()
                    self.pe.wait(self.drained[k])
                    t = self.mm(self.P[k][:, 0:H2], w4j[:, j, :], QH[:, h % 2, self.hs(hf)], True, True, v["q", hf], inc=True)
                    v3 = lambda ap: ap.rearrange("p (b s) -> p b s", b=4)
                    qc, qs = v3(qb[:, 0, j, :]), v3(qb[:, 1, j, :])
                    ps = v3(self.P[k][:, 0:H2])
                    cos, sin = (bc(self.c[n][:, S * j:S * j + S], [128, 4, S]) for n in ("cosq", "sinq"))
                    lo, hi = slice(0, 64), slice(64, 128)
                    t1 = self.tt(qc, ps, cos, ALU.mult, t, st.get(("qe", h - 1, hf)))
                    t2 = self.tt(qs[hi], ps[lo], sin[lo], ALU.mult, t)
                    t2 = self.tt(qs[lo], ps[hi], sin[hi], ALU.mult, t)
                    self.drained[k] = t2
                    v["b", hf] = self.tt(qc, qc, qs, ALU.add, t1, t2, eng=self.pool)

            def fold(hf):
                qb = QB[:, hf, :].rearrange("p (s j t) -> p s j t", s=2, j=3)
                k = self.bank()
                self.pe.wait(self.drained[k])
                t = self.chain(self.P[k][:, 0:H2], [(v["pq"][:, j, :], qb[:, 0, j, :]) for j in range(3)], v["b", hf], v["tp"])
                self.drained[k] = st["qe", h, hf] = self.copy(self.act, QE[hg % 2][:, hh, self.hs(hf)], self.P[k][:, 0:H2], t)
                v["p"].rel = t
            made = [weights, lambda: queries(0), lambda: queries(1)]
            if roped:
                return made, [lambda: big(0), lambda: big(1), lambda: fold(0), lambda: fold(1)]
            return made, [plain]

        def group(hg):
            heads = [head(h) for h in range(4 * hg, 4 * hg + 4)]
            steps = list(heads[0][0])
            for i, (_, made) in enumerate(heads):
                ahead = list(heads[i + 1][0]) if i < 3 else []
                if not roped:
                    steps += ahead + made
                    continue
                for f in made:
                    steps.append(f)
                    steps += ahead[:1]
                    ahead = ahead[1:]
            return steps

        def back(hg):
            v = {}
            base = x if hg == 0 else Z

            def latent(hf):
                if hf == 0:
                    wl = v["wl"] = self.load(512, lambda i: i[pre + "w_kc_kv"][4 * hg:4 * hg + 4].transpose(2, 0, 1).reshape(128, 512))
                    wo = v["wo"] = self.load(2048, lambda i: fm(i[pre + "Wo"][:, 512 * hg:512 * hg + 512]))
                    v["w"] = wo.ap.rearrange("p (m k c) -> p m k c", m=4, k=4)
                wl = v["wl"]
                for hh in range(4):
                    k = self.bank()
                    self.pe.wait(self.drained[k])
                    ct = CT[:, hh, self.hs(hf)]
                    t = self.mm(self.P[k][:, 0:H2], wl.ap[:, 128 * hh:128 * hh + 128], ct, True, True,
                                wl.tok, st["ctt", hg, hf], inc=True)
                    v["cl", hf] = self.copy(self.act if hh % 2 else self.dve, ct, self.P[k][:, 0:H2], t)
                    v.setdefault(("all", hf), []).append(v["cl", hf])
                    self.drained[k] = v["cl", hf]
                if hf:
                    wl.rel = t

            def out(m, hf):
                hs = self.hs(hf)
                k = self.bank()
                self.pe.wait(self.drained[k])
                t = self.chain(self.P[k][:, 0:H2], [(v["w"][:, m, c, :], CT[:, c, hs]) for c in range(4)], v["all", hf], v["wo"].tok)
                zt[hf] = self.tt(Z[:, m, hs], self.P[k][:, 0:H2], base[:, m, hs], ALU.add, t, zt[hf])
                self.drained[k] = zt[hf]
                st["wo", hg, hf] = t
                if m == 3 and hf:
                    v["wo"].rel = t
            return [[lambda hf=hf: latent(hf)] + [lambda m=m, hf=hf: out(m, hf) for m in range(4)] for hf in range(2)]

        first, last = self.norms(Z, self.squares, self.scales, zt)
        ahead = group(0)
        run(ahead, len(ahead))
        behind = []
        for hg in range(4):
            qe = QE[hg % 2]
            rest = behind + (group(hg + 1) if hg < 3 else [])
            share = -(-len(rest) // (NB if roped else 5))
            now, behind = back(hg)

            def beside(t):
                if t >= (6 if roped else 5):
                    run(now)

            def scores(b):
                pm = Pm[:, b % 2, :].rearrange("p (a l) -> p a l", a=4)
                m = sm[:, 64 * (b % 2):64 * (b % 2) + 64]
                for hh in range(4):
                    k = self.bank()
                    self.pe.wait(self.drained[k])
                    t = self.mm(self.P[k][0:S, 0:L], qe[:, hh, S * b:S * b + S], kf[:, b, :], True, True,
                                st["qe", 4 * hg + hh, b // 4], inc=True)
                    t = self.red(m[0:S, hh:hh + 1], self.P[k][0:S, 0:L], ALU.max, t, st.get(("pt", b - 2)), negate=True)
                    t = self.af(pm[0:S, hh, :], self.P[k][0:S, 0:L], ACT.Exp, t, st.get(("pt", b - 2)),
                                bias=m[0:S, hh:hh + 1], accum_out=m[0:S, 4 + hh:5 + hh])
                    self.drained[k] = t
                t = self.rec(m[0:S, 8:12], m[0:S, 4:8], t)
                t = self.tt(pm[0:S, :, :], pm[0:S, :, :], bc(m[0:S, 8:12], [S, 4, L], 2), ALU.mult, t)
                st["p", b] = t

            def turn(b):
                run(rest, share)
                pm = Pm[:, b % 2, :].rearrange("p (a l) -> p a l", a=4)
                pt = PT[:, b % 2, :].rearrange("p (j c) -> p j c", j=3)
                for j in range(3):
                    n = min(128, L - 128 * j)
                    k = self.bank()
                    self.pe.wait(self.drained[k])
                    for hh in range(4):
                        t = self.tr(self.P[k][0:n, S * hh:S * hh + S], pm[0:S, hh, 128 * j:128 * j + n], S, st["p", b], inc=hh == 3)
                    st["pt", b] = t
                    t = self.copy(self.act if j == 1 else self.dve, pt[0:n, j, :], self.P[k][0:n, 0:H2], t, st.get(("pv", b - 2)))
                    self.drained[k] = t
                    st["c", b, j] = t

            def values(b):
                pt = PT[:, b % 2, :].rearrange("p (j c) -> p j c", j=3)
                k = self.bank()
                self.pe.wait(self.drained[k])
                for j in range(3):
                    n = min(128, L - 128 * j)
                    t = self.mm(self.P[k][:, 0:H2], kt[0:n, b, j, :], pt[0:n, j, :], j == 0, j == 2, st["c", b, j], inc=j == 2)
                st["pv", b] = t
                t = self.copy(self.act, CT[:, :, S * b:S * b + S], self.P[k][:, 0:H2].rearrange("p (a s) -> p a s", a=4), t,
                              st.get(("wo", hg - 1, b // 4)))
                self.drained[k] = t
                st["ctt", hg, b // 4] = t
            pipeline(NB, scores, turn, values, beside=beside)
            run(rest, len(rest))
            run(now, len(now))
            for b in range(NB):
                for key in ("p", "pt", "pv"):
                    st[key, b - NB] = st.pop((key, b))
        while behind:
            run(behind)
            run(first)
        run(first, len(first))
        return last

    def l0_ffn(self, tail):
        x = self.x
        B1, B2 = self.ar(0, 16, 512), self.ar(8192, 16, 512)
        H = self.ar(8192, 16, T)
        XH = self.ar(20992, 4, T)
        had, nhad = self.c["had"], self.c["nhad"]
        bt = []
        for g in (2, 3, 0, 1):
            if g == 0:
                run(tail, len(tail))
            p = self.load(2048, lambda i, g=g: tm(i["L0_ffn_W_down"][:, 512 * g:512 * g + 512]))
            w = p.ap.rearrange("p (k c) -> p k c", k=4)
            for k in range(4):
                b = self.bank()
                self.pe.wait(self.drained[b])
                t = self.mm(self.P[b][:, :], had, w[:, k, :], True, True, p.tok, inc=True)
                t = self.copy(self.act if k % 2 else self.dve, B1[:, 4 * g + k, :], self.P[b][:, :], t, self.xt if g < 2 else None)
                self.drained[b] = t
                bt.append(t)
                if k % 2:
                    run(tail)
            p.rel = self.pe.now()
        XS = self.ar(16384, 4, T)
        xs = [None, None]
        for c in range(4):
            for h in range(2):
                xs[h] = self.ts(XS[:, c, self.hs(h)], x[:, c, self.hs(h)], self.c["su"][:, c:c + 1], None, ALU.mult, None, self.xt[h])
        h4 = hadamard(4)
        xh = [None, None]
        r512 = float(np.float32(1.0) / np.sqrt(np.float32(512)))

        def evac(m, h, ps, t):
            xh[h] = self.af(XH[:, m, self.hs(h)], ps, ACT.Copy, t, scale=r512)
            return xh[h]
        self.project(lambda m, k: had if h4[m, k] > 0 else nhad, lambda k, h: XS[:, k, self.hs(h)], xs, 4, range(4), evac)
        src, dst = B1, B2
        t = bt[-2:]
        for lev in range(4):
            s = 1 << lev
            for base in range(0, 16, 2 * s):
                a, b_ = src[:, base:base + s, :], src[:, base + s:base + 2 * s, :]
                self.tt(dst[:, base:base + s, :], a, b_, ALU.add, t)
                t1 = self.tt(dst[:, base + s:base + 2 * s, :], a, b_, ALU.subtract)
            t = t1
            src, dst = dst, src
        wdt = t
        sm = self.small
        ws = self.ts(sm[:, 0:16], self.c["wsu"], 1.0, None, ALU.mult, None)
        ws = self.tt(sm[:, 0:16], sm[:, 0:16], self.c["sud"], ALU.mult, ws)
        wd = self.ts(sm[:, 16:20], self.c["wsd"], float(np.float32(1.0) / np.sqrt(np.float32(2048))), None, ALU.mult, None)
        G = sm[:, 32:832].rearrange("p (a t) -> p a t", a=2)
        ht, gfree, n = [None, None], [None, None], 0
        for g in range(8):
            p = self.load(2048, lambda i, g=g: np.concatenate(
                [fm(i["L0_ffn_W_up"][256 * g:256 * g + 256]), fm(i["L0_ffn_W_gate"][256 * g:256 * g + 256])], 1))
            w = p.ap.rearrange("p (m k c) -> p m k c", m=4, k=4)
            for m in range(2):
                f = 2 * g + m
                for h in range(2):
                    hs = self.hs(h)
                    bu, bg = self.bank(), self.bank()
                    self.pe.wait(self.drained[bu], self.drained[bg])
                    tu = self.chain(self.P[bu][:, 0:H2], [(w[:, m, k, :], XH[:, k, hs]) for k in range(4)], xh[h], p.tok)
                    tg = self.chain(self.P[bg][:, 0:H2], [(w[:, 2 + m, k, :], XH[:, k, hs]) for k in range(4)])
                    t = self.af(G[:, n % 2, :], self.P[bg][:, 0:H2], ACT.Silu, tg, gfree[n % 2], scale=self.c["wsg"][:, f:f + 1])
                    self.drained[bg] = t
                    t = self.stt(H[:, f, hs], self.P[bu][:, 0:H2], sm[:, f:f + 1], G[:, n % 2, :], ALU.mult, ALU.mult, tu, t, ws)
                    self.drained[bu] = gfree[n % 2] = ht[h] = t
                    n += 1
            p.rel = self.pe.now()
        self.dve.wait(self.pe.now())
        Z, zt = XH, [None, None]

        def evacz(m, h, ps, t):
            zt[h] = self.stt(Z[:, m, self.hs(h)], ps, sm[:, 16 + m:17 + m], x[:, m, self.hs(h)], ALU.mult, ALU.add, t, wd)
            return zt[h]
        first, tail = self.norms(Z, H[:, 0:4, :], H[:, 4, :], zt)
        self.project(lambda m, k: B1[:, k, 128 * m:128 * m + 128], lambda k, h: H[:, k, self.hs(h)],
                     [[ht[0], wdt], [ht[1], wdt]], 16, range(4), evacz, None, ([], first))
        return tail

    def router(self, w, n, bias, sm, tail):
        t = None
        for b in range(NB):
            if b == 4:
                run(tail, len(tail))
            k = self.bank()
            self.pe.wait(self.drained[k])
            t = self.chain(self.P[k][0:S, 0:n], [(self.x[:, c, S * b:S * b + S], w[:, c, :]) for c in range(4)], self.xt[b // 4])
            if bias is None:
                t = self.copy(self.dve, sm[0:S, b, 0:n], self.P[k][0:S, 0:n], t)
            else:
                t = self.tt(sm[0:S, b, 0:n], self.P[k][0:S, 0:n], bias[0:S, :], ALU.add, t)
            self.drained[k] = t
        return t

    def top(self, vals, b, n, mx, ix, ixf, *toks):
        v, m, i, f = vals[0:S, b, 0:n], mx[0:S, b, :], ix[0:S, b, :], ixf[0:S, b, :]
        t = self.dve.do(lambda e: e.max(m, v), *toks)
        t = self.dve.do(lambda e: e.max_index(i, m, v), t)
        return self.dve.do(lambda e: e.tensor_copy(f, i), t)

    def shared(self, nf, load, gate, ACC, G, HI):
        x = self.x
        p, q = load()
        w = p.ap[:, 0:1024 * nf].rearrange("p (m k c) -> p m k c", m=2 * nf, k=4)
        wd = (q.ap if q else p.ap[:, 1024:1536]).rearrange("p (f n) -> p f n", f=nf)
        for f in range(nf):
            for h in range(2):
                hs = self.hs(h)
                bg, bu = self.bank(), self.bank()
                self.pe.wait(self.drained[bg], self.drained[bu])
                tg = self.chain(self.P[bg][:, 0:H2], [(w[:, f, k, :], x[:, k, hs]) for k in range(4)], p.tok, self.xt[h])
                tu = self.chain(self.P[bu][:, 0:H2], [(w[:, nf + f, k, :], x[:, k, hs]) for k in range(4)])
                t = self.af(G[:, f, hs], self.P[bg][:, 0:H2], ACT.Silu, tg)
                self.drained[bg] = t
                t = self.tt(HI[:, f, hs], self.P[bu][:, 0:H2], G[:, f, hs], ALU.mult, tu, t)
                self.drained[bu] = t
        acc = {}
        for b in range(NB):
            k = self.bank()
            self.pe.wait(self.drained[k])
            t1 = self.chain(self.P[k][0:S, :], [(HI[:, f, S * b:S * b + S], wd[:, f, :]) for f in range(nf)], t,
                            q.tok if q else None)
            self.drained[k] = acc[b] = gate(ACC[0:S, b, :], self.P[k][0:S, :], b, t1)
        p.rel = self.pe.now()
        if q:
            q.rel = p.rel
        return acc

    def gather(self, out, table, idx, *toks):
        sem = self.gsem[self.ng % len(self.gsem)]
        self.ng += 1
        val = 16 * ((self.ng - 1) // len(self.gsem) + 1)
        self.pool.wait(*toks)
        if val > 16:
            self.pool.wait(Tok(sem, val - 16))
        self.pool.q.append((None, lambda e: e.indirect_dma_start(
            out, None, table, bass.IndirectOffsetOnAxis(ap=idx, axis=0)).then_inc(sem, 16), False))
        return Tok(sem, val)

    def store(self, out, in_, *toks):
        sem = self.ssem[self.ns % len(self.ssem)]
        self.ns += 1
        val = 16 * ((self.ns - 1) // len(self.ssem) + 1)
        self.act.wait(*toks)
        if val > 16:
            self.act.wait(Tok(sem, val - 16))
        self.act.q.append((None, lambda e: e.dma_start(out, in_).then_inc(sem, 16), False))
        return Tok(sem, val)

    def sparse(self, E, kk, nf, MK, CB, mt, ct, wd, shared):
        NT = (T * kk + 127 * E) // 128
        x = self.x
        ACC = self.ar(8000, NB, 512)
        XT = self.ar(12096, NB, 512)
        nw = 1536 * nf
        WT = [self.ar(a, nw) for a in ((12096, 15168, 0) if nf == 2 else (12096, 13632, 15168, 16704, 0, 1536, 3072))]
        R = len(WT)
        XG = self.ar(18240, 4, 512)
        XF = self.ar(20288, 2, 512)
        G, HI = self.ar(21312, 2, 256), self.ar(21824, 2, 256)
        Y = self.ar(22336, 3, 512)
        XD, YD = self.XD, self.YD[NT]
        U = lambda a: a.bitcast(U32)
        sx = []
        for b in range(NB):
            k = self.bank()
            self.pe.wait(self.drained[k])
            for c in range(4):
                t = self.tr(self.P[k][0:S, 128 * c:128 * c + 128], x[:, c, S * b:S * b + S], 128, self.xt[b // 4], inc=c == 3)
            t = self.copy(self.act, XT[0:S, b, :], self.P[k][0:S, :], t)
            self.drained[k] = t
            sx.append(self.store(XD[S * b:S * b + S, :], XT[0:S, b, :], t))
        acc = shared(ACC, self.ar(18240, nf, T), self.ar(18240 + nf * T, nf, T))
        dense = [self.pe.now(), self.dve.now(), self.act.now()]
        MT, RK = self.ar(4000, T), self.ar(4800, T)
        sm = self.small
        for g in range(2):
            k = self.bank()
            self.pe.wait(self.drained[k])
            for b in range(4):
                t = self.tr(self.P[k][0:E, S * b:S * b + S], MK[0:S, 4 * g + b, :], S, mt, inc=b == 3)
            t = self.copy(self.dve, MT[0:E, self.hs(g)], self.P[k][0:E, 0:H2], t)
            self.drained[k] = t
        t = self.dve.do(lambda e: e.tensor_tensor_scan(RK[0:E, :], MT[0:E, :], MT[0:E, :], 0.0, ALU.add, ALU.max), t)
        cmp7, tl, base, end = sm[0:E, 0:7], sm[0:E, 8:9], sm[0:E, 9:10], sm[0:E, 10:11]
        t = self.ts(cmp7, self.c["thr"][0:E, :], RK[0:E, T - 1:T], None, ALU.is_lt, None, t)
        t = self.red(tl, cmp7, ALU.add, t)
        k = self.bank()
        self.pe.wait(self.drained[k])
        t = self.mm(self.P[k][0:E, 0:1], self.c["tri"][0:E, 0:E], tl, True, True, t, inc=True)
        t1 = self.ts(base, self.P[k][0:E, 0:1], 128.0, None, ALU.mult, None, t)
        t2 = self.tt(end, self.P[k][0:E, 0:1], tl, ALU.add, t)
        self.drained[k] = t2
        t = self.stt(RK[0:E, :], RK[0:E, :], base, MT[0:E, :], ALU.add, ALU.mult, t1, t2)
        CM = self.ar(5600, 113)
        tc = self.ts(CM[0:E, 0:NT], self.c["tiles"][0:E, 0:NT], end, None, ALU.is_ge, None, t)
        SLT = self.ar(6400, NB, E)
        g_ = 512 // E
        ts_ = t
        for g in range(0, NB, min(g_, NB)):
            n = min(g_, NB)
            k = self.bank()
            self.pe.wait(self.drained[k])
            for b in range(n):
                t = self.tr(self.P[k][0:S, E * b:E * b + E], RK[0:E, S * (g + b):S * (g + b) + S], E, ts_, inc=b == n - 1)
            t = self.copy(self.dve, SLT[0:S, g:g + n, :], self.P[k][0:S, 0:E * n].rearrange("p (b e) -> p b e", b=n), t)
            self.drained[k] = t
        SV, SI = self.ar(5720, NB, 8), U(self.ar(5784, NB, 8))
        for b in range(NB):
            t = self.dve.do(lambda e, b=b: e.max(SV[0:S, b, :], SLT[0:S, b, :]), t)
        SF = self.ar(5860, NB, 8)
        t = self.ts(SF[0:S, :, 0:kk], SV[0:S, :, 0:kk], -1.0, None, ALU.add, None, t)
        t = self.dve.do(lambda e: e.tensor_copy(SI[0:S, :, 0:kk], SF[0:S, :, 0:kk]), t)
        IT, IP, FT, FP = U(self.ar(5930, NB, 8)), U(self.ar(6000, NB, 8)), self.ar(6070, NB, 8), self.ar(6140, NB, 8)
        pick = lambda a: a[0:S, :, 0:kk]
        t = self.ts(pick(IT), pick(SI), 7, None, ALU.logical_shift_right, None, t)
        t = self.ts(pick(IP), pick(SI), 127, None, ALU.bitwise_and, None, t)
        t = self.dve.do(lambda e: e.tensor_copy(pick(FT), pick(IT)), t)
        tp = self.dve.do(lambda e: e.tensor_copy(pick(FP), pick(IP)), t)
        OA, OB = self.ar(22336, 4, 120), self.ar(22816, 4, 128)
        lk = self.bank()
        self.pe.wait(self.drained[lk])
        used, n = {}, 0
        for b in range(NB):
            for j in range(kk):
                oa, ob = OA[0:S, n % 4, 0:NT], OB[0:S, n % 4, :]
                t1 = self.ts(oa, self.c["tiles"][0:S, 0:NT], FT[0:S, b, j:j + 1], self.c["token"][0:S, b:b + 1],
                             ALU.is_equal, ALU.mult, tp, used.get(n - 4))
                t2 = self.ts(ob, self.c["slots"][0:S, :], FP[0:S, b, j:j + 1], None, ALU.is_equal, None, tp, used.get(n - 4))
                used[n] = t = self.mm(self.P[lk][0:NT, 0:128], oa, ob, n == 0, n == NB * kk - 1, t1, t2, inc=True)
                n += 1
        TF, TI = self.ar(7500, 128), U(self.ar(7630, NT))
        t = self.copy(self.dve, TF[0:NT, :], self.P[lk][0:NT, 0:128], t)
        self.drained[lk] = t
        k = self.bank()
        self.pe.wait(self.drained[k])
        t = self.tr(self.P[k][:, 0:NT], TF[0:NT, :], NT, t, inc=True)
        ti = self.copy(self.dve, TI[:, :], self.P[k][:, 0:NT], t)
        self.drained[k] = ti
        k = self.bank()
        self.pe.wait(self.drained[k])
        t = self.mm(self.P[k][:, 0:NT], self.c["mean"][0:E, :], CM[0:E, 0:NT], True, True, tc, inc=True)
        WF, WI = self.ar(7060, NT), U(self.ar(7180, NT))
        t = self.ts(WF, self.P[k][:, 0:NT], 512.0, float(E - 1), ALU.mult, ALU.min, t)
        self.drained[k] = t
        t = self.ts(WF, WF, 128.0, self.c["lane"], ALU.mult, ALU.add, t)
        wi = self.dve.do(lambda e: e.tensor_copy(WI[:, :], WF[:, :]), t)
        GP, EQ = self.ar(7300, NB, 8), self.ar(3400, NB, E)
        t = ct
        for j in range(kk):
            t = self.tt(EQ[0:S], SLT[0:S], SV[0:S, :, j:j + 1].to_broadcast([S, NB, E]), ALU.is_equal, t)
            t = self.tt(EQ[0:S], EQ[0:S], CB[0:S, :, 0:E], ALU.mult, t)
            t = self.red(GP[0:S, :, j], EQ[0:S], ALU.add, t)
        gp = t
        over = [self.pe.now(), self.dve.now(), self.act.now()]
        st = {}

        def fetch(i):
            tables = over if i % R >= (2 if nf == 2 else 4) else None
            st["w", i] = self.gather(WT[i % R], wd, WI[:, i:i + 1], wi, sx, tables, st.get(("d", i - R)))
            st["x", i] = self.gather(XG[:, i % 4, :], XD[:, :], TI[:, i:i + 1], ti, sx, dense, st.get(("t", i - 4)))

        def turn(i):
            k = self.bank()
            self.pe.wait(self.drained[k])
            for c in range(4):
                t = self.tr(self.P[k][:, 128 * c:128 * c + 128], XG[:, i % 4, 128 * c:128 * c + 128], 128, st["x", i], inc=c == 3)
            st["t", i] = t
            t = self.copy(self.act, XF[:, i % 2, :], self.P[k][:, :], t, st.get(("u", i - 2)))
            self.drained[k] = t
            st["f", i] = t

        def up(i):
            w = WT[i % R][:, 0:1024 * nf].rearrange("p (m k c) -> p m k c", m=2 * nf, k=4)
            xf = XF[:, i % 2, :].rearrange("p (c t) -> p c t", c=4)
            k = self.bank()
            self.pe.wait(self.drained[k])
            for m in range(2 * nf):
                t = self.chain(self.P[k][:, 128 * m:128 * m + 128], [(w[:, m, c, :], xf[:, c, :]) for c in range(4)],
                               st["f", i], st["w", i])
            st["u", i] = t
            n = 128 * nf
            t = self.af(G[:, i % 2, 0:n], self.P[k][:, 0:n], ACT.Silu, t, st.get(("h", i - 2)))
            t = self.tt(HI[:, i % 2, 0:n], self.P[k][:, n:2 * n], G[:, i % 2, 0:n], ALU.mult, t, st.get(("d", i - 2)))
            self.drained[k] = t
            st["h", i] = t

        def down(i):
            w = WT[i % R][:, 1024 * nf:1536 * nf].rearrange("p (f n) -> p f n", f=nf)
            k = self.bank()
            self.pe.wait(self.drained[k])
            t = self.chain(self.P[k][:, :], [(HI[:, i % 2, 128 * f:128 * f + 128], w[:, f, :]) for f in range(nf)], st["h", i])
            st["d", i] = t
            t = self.copy(self.act, Y[:, i % 3, :], self.P[k][:, :], t, st.get(("s", i - 3)))
            self.drained[k] = t
            st["s", i] = self.store(YD[128 * i:128 * i + 128, :], Y[:, i % 3, :], t)
        idle = [lambda i: None] * (2 if nf == 1 else 0)
        pipeline(NT, fetch, *idle, turn, up, down)
        done = [st["s", i] for i in range(NT - min(NT, len(self.ssem)), NT)]
        YG = self.ar(12096, 8, 512)
        pe = self.pe.now()
        Z, zt = self.sums, [None, None]
        n = 0
        steps = [self.norm_steps(Z, self.squares, self.scales, zt, h) for h in range(2)]
        for b in range(NB):
            for j in range(kk):
                t = self.gather(YG[0:S, n % 8, :], YD[:, :], SI[0:S, b, j:j + 1], done, pe, st.get(("y", n - 8)))
                a = ACC[0:S, b, :]
                acc[b] = self.stt(a, YG[0:S, n % 8, :], GP[0:S, b, j:j + 1], a, ALU.mult, ALU.add, t, gp, acc[b])
                st["y", n] = acc[b]
                n += 1
            k = self.bank()
            self.pe.wait(self.drained[k])
            ps = self.P[k][:, 0:4 * S].rearrange("p (c s) -> p c s", c=4)
            for c in range(4):
                t = self.tr(ps[:, c, :], ACC[0:S, b, 128 * c:128 * c + 128], S, acc[b], inc=c == 3)
            sl = slice(S * b, S * b + S)
            zt[b // 4] = self.tt(Z[:, :, sl], ps, x[:, :, sl], ALU.add, t, done)
            self.drained[k] = zt[b // 4]
            if b in (3, 4, 5):
                steps[0][b - 3]()
        return list(steps[1])

    def l1_ffn(self, tail):
        self.dve.wait(self.pe.now())
        self.act.wait(self.pe.now())
        pre = "L1_ffn_"
        E = 16
        SC, CB, OH = self.ar(0, NB, E), self.ar(128, NB, E + 1), self.ar(300, NB, E)
        BI = self.ar(500, NB, E)
        MX, IX, IF = self.ar(700, NB, 8), self.ar(800, NB, 8).bitcast(U32), self.ar(900, NB, 8)
        SS = self.ar(1000, NB)
        w = self.c["g1w"].rearrange("p (k e) -> p k e", k=4)
        t = self.router(w, E, None, SC, tail)
        t = self.af(SC[0:S], SC[0:S], ACT.Sigmoid, t)
        t = self.tt(BI[0:S], SC[0:S], bc(self.c["g1b"][0:S, :], [S, NB, E]), ALU.add, t)
        for b in range(NB):
            t = self.top(BI, b, E, MX, IX, IF, t)
        iota = bc(self.c["iota"][0:S, 0:E], [S, NB, E])
        t = self.tt(CB[0:S, :, 0:E], iota, IF[0:S, :, 0:1].to_broadcast([S, NB, E]), ALU.is_equal, t)
        t = self.tt(OH[0:S], iota, IF[0:S, :, 1:2].to_broadcast([S, NB, E]), ALU.is_equal, t)
        t = tm_ = self.tt(OH[0:S], CB[0:S, :, 0:E], OH[0:S], ALU.add, t)
        t = self.tt(CB[0:S, :, 0:E], OH[0:S], SC[0:S], ALU.mult, t)
        t = self.red(SS[0:S], CB[0:S, :, 0:E], ALU.add, t)
        t = self.ts(SS[0:S], SS[0:S], 1e-20, None, ALU.add, None, t)
        t = self.rec(SS[0:S], SS[0:S], t)
        t = self.tt(CB[0:S, :, 0:E], CB[0:S, :, 0:E], bc(SS[0:S], [S, NB, E], 2), ALU.mult, t)
        return self.sparse(E, 2, 2, OH, CB, tm_, t, self.E1, lambda ACC, G, HI: self.shared(2, lambda: (
            self.load(2048, lambda i: np.concatenate([fm(i[pre + "shared_gate_w"].T), fm(i[pre + "shared_up_w"].T)], 1)),
            self.load(1024, lambda i: tm(i[pre + "shared_down_w"].T))), lambda a, ps, b, t: self.copy(self.act, a, ps, t),
            ACC, G, HI))

    def l3_ffn(self, tail):
        self.dve.wait(self.pe.now())
        self.act.wait(self.pe.now())
        pre = "L3_ffn_"
        E = 64
        LG, CB, WK = self.ar(0, NB, E + 1), self.ar(600, NB, E + 1), self.ar(1200, NB, E)
        MX, NM, SS = self.ar(1800, NB, 8), self.ar(1900, NB), self.ar(1950, NB)
        w = self.c["g3w"].rearrange("p (k e) -> p k e", k=4)
        t = self.router(w, E + 1, None, LG, tail)
        tl = t
        for b in range(NB):
            lg = LG[0:S, b, 0:E]
            t = self.dve.do(lambda e, b=b, lg=lg: e.max(MX[0:S, b, :], lg), t)
            t = self.dve.do(lambda e, b=b, lg=lg: e.match_replace(WK[0:S, b, :], MX[0:S, b, :], lg, -3.0e38), t)
        cb = CB[0:S, :, 0:E]
        MK = self.ar(2000, NB, E)
        t = mt = self.tt(MK[0:S], WK[0:S], LG[0:S, :, 0:E], ALU.not_equal, t)
        t = self.tt(WK[0:S], LG[0:S, :, 0:E], bc(MX[0:S, :, 0], [S, NB, E], 2), ALU.subtract, t)
        t = self.af(WK[0:S], WK[0:S], ACT.Exp, t)
        t = self.tt(cb, MK[0:S], WK[0:S], ALU.mult, t)
        t = self.red(SS[0:S], cb, ALU.add, t)
        t = self.rec(SS[0:S], SS[0:S], t)
        t = self.tt(cb, cb, bc(SS[0:S], [S, NB, E], 2), ALU.mult, t)
        t2 = self.af(CB[0:S, :, E:E + 1], LG[0:S, :, E:E + 1], ACT.Sigmoid, tl)

        return self.sparse(E, 8, 1, MK, CB, mt, t, self.E3, lambda ACC, G, HI: self.shared(1, lambda: (self.load(1536, lambda i: np.concatenate(
            [fm(i[pre + "sh_gate_w"]), fm(i[pre + "sh_up_w"]), i[pre + "sh_down_w"].T], 1)), None),
            lambda a, ps, b, t: self.ts(a, ps, CB[0:S, b, E:E + 1], None, ALU.mult, None, t, t2), ACC, G, HI))

    def l2_ffn(self, tail):
        self.dve.wait(self.pe.now())
        self.act.wait(self.pe.now())
        E = 8
        LG, PR, OH = self.ar(0, NB, E), self.ar(64, NB, E), self.ar(128, NB, E)
        MX, IX, IF = self.ar(192, NB, 8), self.ar(256, NB, 8).bitcast(U32), self.ar(320, NB, 8)
        NM, SS = self.ar(384, NB), self.ar(392, NB)
        GT = self.ar(400, T)
        GB = self.ar(1200, 4, T)
        Hh = self.ar(4400, 4, T)
        w = self.c["wr"].rearrange("p (k e) -> p k e", k=4)
        t = self.router(w, E, self.c["br"], LG, tail)
        t = self.red(NM[0:S], LG[0:S], ALU.max, t)
        t = self.tt(LG[0:S], LG[0:S], bc(NM[0:S], [S, NB, E], 2), ALU.subtract, t)
        t = self.af(PR[0:S], LG[0:S], ACT.Exp, t)
        t = self.red(SS[0:S], PR[0:S], ALU.add, t)
        t = self.rec(SS[0:S], SS[0:S], t)
        t = self.tt(PR[0:S], PR[0:S], bc(SS[0:S], [S, NB, E], 2), ALU.mult, t)
        for b in range(NB):
            t = self.top(PR, b, E, MX, IX, IF, t)
        t = self.tt(OH[0:S], bc(self.c["iota"][0:S, 0:E], [S, NB, E]), IF[0:S, :, 0:1].to_broadcast([S, NB, E]), ALU.is_equal, t)
        t = self.tt(OH[0:S], OH[0:S], MX[0:S, :, 0:1].to_broadcast([S, NB, E]), ALU.mult, t)
        t = self.ts(OH[0:S], OH[0:S], 1.0 / 64, None, ALU.mult, None, t)
        gt = [None, None]
        for b in range(NB):
            k = self.bank()
            self.pe.wait(self.drained[k])
            t1 = self.tr(self.P[k][0:E, 0:S], OH[0:S, b, :], S, t, inc=True)
            gt[b // 4] = self.copy(self.act, GT[0:E, S * b:S * b + S], self.P[k][0:E, 0:S], t1)
            self.drained[k] = gt[b // 4]
        gb = {}
        sel = self.c["sel8"].rearrange("p (k c) -> p k c", k=4)
        for m in range(4):
            for h in range(2):
                k = self.bank()
                self.pe.wait(self.drained[k])
                t1 = self.mm(self.P[k][:, 0:H2], sel[0:E, m, :], GT[0:E, self.hs(h)], True, True, gt[h], inc=True)
                gb[m, h] = self.copy(self.act, GB[:, m, self.hs(h)], self.P[k][:, 0:H2], t1)
                self.drained[k] = gb[m, h]
        ht = [None, None]

        def evac(m, h, ps, t):
            ht[h] = self.tt(Hh[:, m, self.hs(h)], ps, GB[:, m, self.hs(h)], ALU.mult, t, gb[m, h])
            return ht[h]
        self.full("L2_ffn_A", lambda a: a.reshape(512, 512), self.x, self.xt, evac)
        Z, zt = self.sums, [None, None]
        first, tail = self.norms(Z, self.squares, self.scales, zt)
        self.full("L2_ffn_B", lambda a: a.transpose(1, 0, 2).reshape(512, 512), Hh, ht, self.add_residual(Z, zt),
                  beside=([], first))
        return tail

    def layer(self, n, tail):
        return [self.l0_attn, lambda t: self.xattn("L0_xattn_", t), self.l0_ffn,
                self.l1_attn, lambda t: self.mla("L1_xattn_", False, t), self.l1_ffn,
                self.l2_attn, lambda t: self.mla("L2_xattn_", True, t), self.l2_ffn,
                self.l3_attn, lambda t: self.xattn("L3_xattn_", t), self.l3_ffn][n](tail)


def pad_rows(parts):
    out = []
    for a in parts:
        b = np.zeros((128, a.shape[1]), np.float32)
        b[:a.shape[0]] = a
        out.append(b)
    return np.concatenate(out, 1)


def build(nc, layers=range(12)):
    from contextlib import ExitStack
    with ExitStack() as stack:
        k = Program(nc, stack, layers)
        k.act.wait(k.ic)
        if layers[0] != 0:
            for b in range(NB):
                k.prep(b)
            k.barrier()
        tail = []
        for n in layers:
            if n:
                for e in (k.pe, k.act, k.dve, k.pool):
                    e.wait(k.ic2)
            tail = k.layer(n, tail)
        run(tail, len(tail))
        total = sum(128 * p.n for p in k.loads)
        wd = nc.dram_tensor("weights", [total], F32, kind="ExternalInput").ap()
        cd = nc.dram_tensor("constants", [128, k.cw], F32, kind="ExternalInput").ap()
        xd = nc.dram_tensor("xt", [128, 4 * T], F32, kind="ExternalInput").ap()
        kd = nc.dram_tensor("ctx", [128, NB * L], F32, kind="ExternalInput").ap()
        od = nc.dram_tensor("out", [128, 4 * T], F32, kind="ExternalOutput").ap()
        block = stack.enter_context(nc.Block())

        @block.sync
        def _(e):
            e.dma_start(k.C[:, 0:532], cd[:, 0:532]).then_inc(k.s_in[0], 16)
            e.dma_start(k.X[:, :], xd).then_inc(k.s_in[1], 16)
            at = 0
            sp = Eng("sp", None)
            for i, p in enumerate(k.loads):
                if i >= RING:
                    sp.wait(k.loads[i - RING].rel)
                src = wd[at:at + 128 * p.n].rearrange("(p n) -> p n", n=p.n)
                at += 128 * p.n
                sem = p.tok.sem
                if i == (3 if k.layers[0] == 0 else 0):
                    sp.q.append((None, lambda e: e.dma_start(k.C[:, 532:], cd[:, 532:]).then_inc(k.s_in[4], 16), False))
                    sp.q.append((None, lambda e: e.dma_start(k.A[:, 17000:17000 + NB * L], kd).then_inc(k.s_in[3], 16), False))
                    sp.q.append((None, lambda e: e.dma_start(
                        k.CX[:, :].rearrange("p (b s) -> p b s", b=NB),
                        kd.rearrange("p (b l) -> p b l", b=NB)[:, :, 0:S]).then_inc(k.s_in[2], 16), False))
                sp.q.append((None, lambda e, p=p, src=src, sem=sem: e.dma_start(p.ap, src).then_inc(sem, 16), False))
            sp.flush(e)
            for t in k.xt:
                e.wait_ge(t.sem, t.val)
            e.dma_start(od, k.X[:, :]).then_inc(k.s_out, 16)
            e.wait_ge(k.s_out, 16)

        @block.tensor
        def _(e):
            k.pe.flush(e)

        @block.scalar
        def _(e):
            k.act.flush(e)

        @block.vector
        def _(e):
            k.dve.flush(e)

        @block.gpsimd
        def _(e):
            k.pool.flush(e)
    return k


def experts1(i):
    g = np.asarray(i["L1_ffn_experts_gate_up"]).reshape(16, 4, 128, 4, 128).transpose(0, 2, 3, 1, 4).reshape(16 * 128, 2048)
    d = np.asarray(i["L1_ffn_experts_down"]).reshape(16, 2, 128, 512).transpose(0, 2, 1, 3).reshape(16 * 128, 1024)
    return np.concatenate([g, d], 1)


def experts3(i):
    g = np.asarray(i["L3_ffn_gu_w"]).reshape(64, 2, 128, 4, 128).transpose(0, 4, 1, 3, 2).reshape(64 * 128, 1024)
    d = np.asarray(i["L3_ffn_dp_w"]).transpose(0, 2, 1).reshape(64 * 128, 512)
    return np.concatenate([g, d], 1)


def pack(k, inputs):
    x = np.asarray(inputs["x"])
    xt = x.reshape(T, 4, 128).transpose(2, 1, 0).reshape(128, 4 * T)
    cx = np.asarray(inputs["ctx_512"]).transpose(2, 0, 1).reshape(128, NB * L)
    cc = np.concatenate([v for v in k.consts.values()] + [f(inputs) for _, f in PARAMS.values()], 1)
    parts = [np.ascontiguousarray(p.pack(inputs)) for p in k.loads]
    for p, a in zip(k.loads, parts):
        assert a.shape == (128, p.n), (a.shape, p.n)
    ws = np.concatenate([a.reshape(-1) for a in parts])
    return {"xt": np.ascontiguousarray(xt), "ctx": np.ascontiguousarray(cx), "constants": np.ascontiguousarray(cc),
            "weights": ws, "experts1": experts1(inputs), "experts3": experts3(inputs)}


def kernel(**inputs):
    import numpy as _np
    import concourse.bacc as _bacc
    from concourse.bass_utils import run_bass_kernel_spmd as _run

    nc = _bacc.Bacc("TRN2", target_bir_lowering=False, num_devices=1)
    k = build(nc)
    r = _run(nc, [pack(k, inputs)], core_ids=[0])
    o = r.results[0]["out"]
    return _np.ascontiguousarray(o.reshape(128, 4, NB, S).transpose(2, 3, 1, 0).reshape(NB, S, 512))
```
